# Optimizing a Trainium2 kernel written in Bass

```python
import numpy as np
import jax
import jax.numpy as jnp

def _softmax(x, axis=-1):
    return jax.nn.softmax(x, axis=axis)

def _gelu(x):
    return jax.nn.gelu(x, approximate=True)

def _silu(x):
    return jax.nn.silu(x)

def _sigmoid(x):
    return jax.nn.sigmoid(x)

def _layernorm(x, axis=-1, eps=1e-05):
    m = jnp.mean(x, axis=axis, keepdims=True)
    v = jnp.var(x, axis=axis, keepdims=True)
    return (x - m) / jnp.sqrt(v + eps)

def _scatter_add(tgt, idx, src, axis=0):
    return tgt.at[idx].add(src)

def _segment_sum(src, seg, n):
    return jax.ops.segment_sum(src, seg, n)
kernel_name = 'mk_vit_tower_cls_d4_tok_img512_r4_323f3f'

def setup_inputs(seed: int=0):
    np.random.seed(seed)
    _w = jnp.asarray

    def _rec_inputs():
        import jax
        import jax.numpy as jnp
        _rk = jax.random.key(seed)
        x = -0.000392918 + 0.999932 * jax.random.normal(jax.random.fold_in(_rk, 1), (8, 1, 128, 128), jnp.float32)
        cls_tok = 0.02 * jax.random.normal(jax.random.fold_in(_rk, 5), (1, 1, 128), jnp.float32)
        return (x, cls_tok)
    x, cls_tok = _rec_inputs()

    def _L0_tok_setup():
        import math
        import jax, jax.numpy as jnp
        import numpy as np
        PW = PH = 16
        EMB = 128
        HID = 128
        B, H, W = (64, 128, 128)
        L = H // PW * (W // PH)
        SIGMA_ZERO = 0.1

        def _f_noise(x):
            return jnp.sign(x) * jnp.sqrt(jnp.abs(x))

        def _noisy_linear(x, w, b, sw, sb, eps_in, eps_out):
            ei = _f_noise(eps_in)
            eo = _f_noise(eps_out)
            w_n = w + sw * (eo[:, None] * ei[None, :])
            b_n = b + sb * eo
            return x @ w_n.T + b_n

        def _unfold_patches(x):
            b = x.shape[0]
            p = x.reshape(b, H // PW, PW, W // PH, PH)
            p = p.transpose(0, 1, 3, 2, 4)
            return p.reshape(b, L, PW * PH)

        def _pos_encoding(x):
            pos = jnp.arange(L, dtype=jnp.float32)[:, None]
            div = jnp.exp(jnp.arange(0, EMB, 2, dtype=jnp.float32) * (-math.log(10000.0) / EMB))
            ang = pos * div
            pe = jnp.stack([jnp.sin(ang), jnp.cos(ang)], axis=-1).reshape(L, EMB)
            return x + pe[None, :, :]
        key = jax.random.key(seed)
        ks = jax.random.split(key, 12)
        in_f = PW * PH
        sig = SIGMA_ZERO / math.sqrt(in_f)
        bnd1 = 1.0 / math.sqrt(in_f)
        bnd3 = 1.0 / math.sqrt(HID)
        u = lambda k, shape, bnd: jax.random.uniform(k, shape, jnp.float32, -bnd, bnd)
        return {'inputs': jax.random.normal(ks[0], (B, 1, H, W), jnp.float32), 'W1_w': u(ks[1], (HID, in_f), bnd1), 'W1_b': u(ks[2], (HID,), bnd1), 'W1_sw': jnp.full((HID, in_f), sig, jnp.float32), 'W1_sb': jnp.full((HID,), sig, jnp.float32), 'W2_w': u(ks[3], (HID, in_f), bnd1), 'W2_b': u(ks[4], (HID,), bnd1), 'W2_sw': jnp.full((HID, in_f), sig, jnp.float32), 'W2_sb': jnp.full((HID,), sig, jnp.float32), 'W3_w': u(ks[5], (EMB, HID), bnd3), 'W3_b': u(ks[6], (EMB,), bnd3), 'eps_in1': jax.random.normal(ks[7], (in_f,), jnp.float32), 'eps_out1': jax.random.normal(ks[8], (HID,), jnp.float32), 'eps_in2': jax.random.normal(ks[9], (in_f,), jnp.float32), 'eps_out2': jax.random.normal(ks[10], (HID,), jnp.float32)}
    _L0_tok_all = _L0_tok_setup()
    _L0_tok_in = {k: v for k, v in _L0_tok_all.items() if k in ('W1_w', 'W1_b', 'W1_sw', 'W1_sb', 'W2_w', 'W2_b', 'W2_sw', 'W2_sb', 'W3_w', 'W3_b', 'eps_in1', 'eps_out1', 'eps_in2', 'eps_out2')}
    del _L0_tok_all

    def _L0_attn_setup():
        import jax, jax.numpy as jnp
        import numpy as np
        EPS = 1.1920929e-07

        def _rmsnorm(x, g):
            inv = jax.lax.rsqrt(jnp.mean(x * x, axis=-1, keepdims=True) + EPS)
            return x * inv * g
        key = jax.random.key(seed)
        k1, k2, k3 = jax.random.split(key, 3)
        B, T, C, H = (4, 512, 128, 8)
        D = C // H
        x = jax.random.normal(k1, (B, T, C), dtype=jnp.float32)
        delta_w = jax.random.normal(k2, (C, C), dtype=jnp.float32) * 0.02
        qkv_w = jax.random.normal(k3, (C, C), dtype=jnp.float32) * 0.02
        g1 = jnp.ones((D,), dtype=jnp.float32)
        g2 = jnp.ones((D,), dtype=jnp.float32)
        g3 = jnp.ones((D,), dtype=jnp.float32)
        return {'x': x, 'delta_w': delta_w, 'qkv_w': qkv_w, 'g1': g1, 'g2': g2, 'g3': g3}
    _L0_attn_all = _L0_attn_setup()
    _L0_attn_in = {k: v for k, v in _L0_attn_all.items() if k in ('delta_w', 'qkv_w', 'g1', 'g2', 'g3')}
    del _L0_attn_all

    def _L0_ffn_setup():
        import jax, jax.numpy as jnp
        import numpy as np
        D_MODEL, N_GROUPS, N_EXPERTS = (128, 8, 8)
        TOP_K_L1, TOP_K_L2 = (2, 2)
        BATCH, SEQ = (2, 128)
        key = jax.random.key(seed)
        ks = jax.random.split(key, 6)
        d, G, E = (D_MODEL, N_GROUPS, N_EXPERTS)
        scale = 0.02
        x = jax.random.normal(ks[0], (BATCH, SEQ, d), dtype=jnp.float32)
        g1 = jax.random.normal(ks[1], (d, G), dtype=jnp.float32) * scale
        g2 = jax.random.normal(ks[2], (G, d, E), dtype=jnp.float32) * scale
        W1 = jax.random.normal(ks[3], (G, E, d, 2 * d), dtype=jnp.float32) * scale
        b1 = jnp.zeros((G, E, 2 * d), dtype=jnp.float32)
        W2 = jax.random.normal(ks[4], (G, E, 2 * d, d), dtype=jnp.float32) * scale
        b2 = jnp.zeros((G, E, d), dtype=jnp.float32)
        return {'x': x, 'g1': g1, 'g2': g2, 'W1': W1, 'b1': b1, 'W2': W2, 'b2': b2}
    _L0_ffn_all = _L0_ffn_setup()
    _L0_ffn_in = {k: v for k, v in _L0_ffn_all.items() if k in ('g1', 'g2', 'W1', 'b1', 'W2', 'b2')}
    del _L0_ffn_all

    def _L1_attn_setup():
        import jax, jax.numpy as jnp
        import numpy as np
        BN_EPS = 1e-05
        B, N, C, H, HID = (16, 256, 128, 8, 512)

        def _bn(x, g, b, m, v):
            return (x - m) * (g * jax.lax.rsqrt(v + BN_EPS)) + b

        def _stage(x, w, bias, g, be, m, v):
            return jax.nn.relu(_bn(x @ w.T + bias, g, be, m, v))
        key = jax.random.key(seed)
        ks = iter(jax.random.split(key, 64))
        d = {'x': jax.random.normal(next(ks), (B, N, C), dtype=jnp.float32)}

        def lin_bn(pref, out_f, in_f):
            d[pref + '_w'] = jax.random.normal(next(ks), (out_f, in_f), dtype=jnp.float32) * 0.02
            d[pref + '_b'] = jax.random.normal(next(ks), (out_f,), dtype=jnp.float32) * 0.02
            d[pref + '_g'] = 1.0 + 0.1 * jax.random.normal(next(ks), (out_f,), dtype=jnp.float32)
            d[pref + '_be'] = 0.1 * jax.random.normal(next(ks), (out_f,), dtype=jnp.float32)
            d[pref + '_m'] = 0.1 * jax.random.normal(next(ks), (out_f,), dtype=jnp.float32)
            d[pref + '_v'] = jax.random.uniform(next(ks), (out_f,), dtype=jnp.float32, minval=0.5, maxval=1.5)
        for p in ('q', 'k', 'v', 'p'):
            lin_bn(p, C, C)
        lin_bn('f1', HID, C)
        lin_bn('f2', C, HID)
        return d
    _L1_attn_all = _L1_attn_setup()
    _L1_attn_in = {k: v for k, v in _L1_attn_all.items() if k in ('q_w', 'q_b', 'q_g', 'q_be', 'q_m', 'q_v', 'k_w', 'k_b', 'k_g', 'k_be', 'k_m', 'k_v', 'v_w', 'v_b', 'v_g', 'v_be', 'v_m', 'v_v', 'p_w', 'p_b', 'p_g', 'p_be', 'p_m', 'p_v', 'f1_w', 'f1_b', 'f1_g', 'f1_be', 'f1_m', 'f1_v', 'f2_w', 'f2_b', 'f2_g', 'f2_be', 'f2_m', 'f2_v')}
    del _L1_attn_all

    def _L1_ffn_setup():
        import jax, jax.numpy as jnp
        import numpy as np
        B, N, D, E = (8, 2048, 128, 8)
        H = 2 * D
        key = jax.random.key(seed)
        ks = jax.random.split(key, 7)
        s = 0.02
        return {'x': jax.random.normal(ks[0], (B, N, D), dtype=jnp.float32), 'W1': jax.random.normal(ks[1], (E, D, H), dtype=jnp.float32) * s, 'b1': jnp.zeros((E, H), dtype=jnp.float32), 'W2': jax.random.normal(ks[2], (E, H, D), dtype=jnp.float32) * s, 'b2': jnp.zeros((E, D), dtype=jnp.float32), 'Wg': jax.random.normal(ks[3], (D, E), dtype=jnp.float32) * s, 'bg': jnp.zeros((E,), dtype=jnp.float32)}
    _L1_ffn_all = _L1_ffn_setup()
    _L1_ffn_in = {k: v for k, v in _L1_ffn_all.items() if k in ('W1', 'b1', 'W2', 'b2', 'Wg', 'bg')}
    del _L1_ffn_all

    def _L2_attn_setup():
        import jax, jax.numpy as jnp
        import numpy as np
        key = jax.random.key(seed)
        k1, k2, k3 = jax.random.split(key, 3)
        B, S, E = (4, 1024, 128)
        x = jax.random.normal(k1, (B, S, E), dtype=jnp.float32)
        lim_qkv = float(np.sqrt(6.0 / (E + 3 * E)))
        W_qkv = jax.random.uniform(k2, (3 * E, E), minval=-lim_qkv, maxval=lim_qkv, dtype=jnp.float32)
        b_qkv = jnp.zeros((3 * E,), dtype=jnp.float32)
        lim_out = float(np.sqrt(6.0 / (E + E)))
        W_out = jax.random.uniform(k3, (E, E), minval=-lim_out, maxval=lim_out, dtype=jnp.float32)
        b_out = jnp.zeros((E,), dtype=jnp.float32)
        return {'x': x, 'W_qkv': W_qkv, 'b_qkv': b_qkv, 'W_out': W_out, 'b_out': b_out}
    _L2_attn_all = _L2_attn_setup()
    _L2_attn_in = {k: v for k, v in _L2_attn_all.items() if k in ('W_qkv', 'b_qkv', 'W_out', 'b_out')}
    del _L2_attn_all

    def _L2_ffn_setup():
        import jax, jax.numpy as jnp
        import numpy as np
        D = 128
        E = 8
        K = 2
        EXP = 4
        LN_EPS = 1e-05
        key = jax.random.key(seed)
        ks = jax.random.split(key, 8)
        B, T = (8, 512)
        Dh = D * EXP
        x = jax.random.normal(ks[0], (B, T, D), dtype=jnp.float32)
        ln_g = jnp.ones((D,), dtype=jnp.float32)
        ln_b = jnp.zeros((D,), dtype=jnp.float32)
        lim_r = np.sqrt(6.0 / (D + E)).astype(np.float32)
        w_r = jax.random.uniform(ks[1], (E, D), dtype=jnp.float32, minval=-lim_r, maxval=lim_r)
        b_r = jnp.zeros((E,), dtype=jnp.float32)
        lim1 = np.sqrt(6.0 / (D + Dh)).astype(np.float32)
        W1 = jax.random.uniform(ks[2], (E, D, Dh), dtype=jnp.float32, minval=-lim1, maxval=lim1)
        b1 = jnp.zeros((E, Dh), dtype=jnp.float32)
        W2 = jax.random.uniform(ks[3], (E, Dh, D), dtype=jnp.float32, minval=-lim1, maxval=lim1)
        b2 = jnp.zeros((E, D), dtype=jnp.float32)
        return {'x': x, 'ln_g': ln_g, 'ln_b': ln_b, 'w_r': w_r, 'b_r': b_r, 'W1': W1, 'b1': b1, 'W2': W2, 'b2': b2}
    _L2_ffn_all = _L2_ffn_setup()
    _L2_ffn_in = {k: v for k, v in _L2_ffn_all.items() if k in ('ln_g', 'ln_b', 'w_r', 'b_r', 'W1', 'b1', 'W2', 'b2')}
    del _L2_ffn_all

    def _L3_attn_setup():
        import jax, jax.numpy as jnp
        import numpy as np
        import math
        D_MODEL = 128
        NUM_HEADS = 8
        LN_EPS = 1e-05
        key = jax.random.key(seed)
        ks = jax.random.split(key, 8)
        B, L, D = (2, 512, D_MODEL)
        x = jax.random.normal(ks[0], (B, L, D), dtype=jnp.float32)
        s = 0.02
        return {'x': x, 'W_qkv': jax.random.normal(ks[1], (D, 3 * D), dtype=jnp.float32) * s, 'b_qkv': jnp.zeros((3 * D,), dtype=jnp.float32), 'W_out': jax.random.normal(ks[2], (D, D), dtype=jnp.float32) * s, 'b_out': jnp.zeros((D,), dtype=jnp.float32), 'decay_logits': jnp.zeros((NUM_HEADS,), dtype=jnp.float32), 'ln_g': jnp.ones((D,), dtype=jnp.float32), 'ln_b': jnp.zeros((D,), dtype=jnp.float32)}
    _L3_attn_all = _L3_attn_setup()
    _L3_attn_in = {k: v for k, v in _L3_attn_all.items() if k in ('W_qkv', 'b_qkv', 'W_out', 'b_out', 'decay_logits', 'ln_g', 'ln_b')}
    del _L3_attn_all

    def _L3_ffn_setup():
        import jax, jax.numpy as jnp
        import numpy as np
        D_MODEL = 128
        D_FF = 128
        N_EXPERTS = 16
        TOP_K = 3
        BATCH, SEQ = (1, 512)

        def _swiglu(combined):
            gate, up = jnp.split(combined, 2, axis=-1)
            return jax.nn.silu(gate) * up
        key = jax.random.key(seed)
        ks = jax.random.split(key, 6)
        x = jax.random.normal(ks[0], (BATCH, SEQ, D_MODEL), dtype=jnp.float32)
        gate_w = 0.01 * jax.random.normal(ks[1], (N_EXPERTS, D_MODEL), dtype=jnp.float32)
        expert_bias = jnp.zeros((N_EXPERTS,), dtype=jnp.float32)
        shared_gate_up = 0.02 * jax.random.normal(ks[2], (2 * D_FF, D_MODEL), dtype=jnp.float32)
        shared_down = 0.02 * jax.random.normal(ks[3], (D_MODEL, D_FF), dtype=jnp.float32)
        expert_gate_up = 0.02 * jax.random.normal(ks[4], (N_EXPERTS, 2 * D_FF, D_MODEL), dtype=jnp.float32)
        expert_down = 0.02 * jax.random.normal(ks[5], (N_EXPERTS, D_MODEL, D_FF), dtype=jnp.float32)
        return {'x': x, 'gate_w': gate_w, 'expert_bias': expert_bias, 'shared_gate_up': shared_gate_up, 'shared_down': shared_down, 'expert_gate_up': expert_gate_up, 'expert_down': expert_down}
    _L3_ffn_all = _L3_ffn_setup()
    _L3_ffn_in = {k: v for k, v in _L3_ffn_all.items() if k in ('gate_w', 'expert_bias', 'shared_gate_up', 'shared_down', 'expert_gate_up', 'expert_down')}
    del _L3_ffn_all
    return {'x': x, 'cls_tok': cls_tok, 'L0_tok_W1_w': _L0_tok_in['W1_w'], 'L0_tok_W1_b': _L0_tok_in['W1_b'], 'L0_tok_W1_sw': _L0_tok_in['W1_sw'], 'L0_tok_W1_sb': _L0_tok_in['W1_sb'], 'L0_tok_W2_w': _L0_tok_in['W2_w'], 'L0_tok_W2_b': _L0_tok_in['W2_b'], 'L0_tok_W2_sw': _L0_tok_in['W2_sw'], 'L0_tok_W2_sb': _L0_tok_in['W2_sb'], 'L0_tok_W3_w': _L0_tok_in['W3_w'], 'L0_tok_W3_b': _L0_tok_in['W3_b'], 'L0_tok_eps_in1': _L0_tok_in['eps_in1'], 'L0_tok_eps_out1': _L0_tok_in['eps_out1'], 'L0_tok_eps_in2': _L0_tok_in['eps_in2'], 'L0_tok_eps_out2': _L0_tok_in['eps_out2'], 'L0_attn_delta_w': _L0_attn_in['delta_w'], 'L0_attn_qkv_w': _L0_attn_in['qkv_w'], 'L0_attn_g1': _L0_attn_in['g1'], 'L0_attn_g2': _L0_attn_in['g2'], 'L0_attn_g3': _L0_attn_in['g3'], 'L0_ffn_g1': _L0_ffn_in['g1'], 'L0_ffn_g2': _L0_ffn_in['g2'], 'L0_ffn_W1': _L0_ffn_in['W1'], 'L0_ffn_b1': _L0_ffn_in['b1'], 'L0_ffn_W2': _L0_ffn_in['W2'], 'L0_ffn_b2': _L0_ffn_in['b2'], 'L1_attn_q_w': _L1_attn_in['q_w'], 'L1_attn_q_b': _L1_attn_in['q_b'], 'L1_attn_q_g': _L1_attn_in['q_g'], 'L1_attn_q_be': _L1_attn_in['q_be'], 'L1_attn_q_m': _L1_attn_in['q_m'], 'L1_attn_q_v': _L1_attn_in['q_v'], 'L1_attn_k_w': _L1_attn_in['k_w'], 'L1_attn_k_b': _L1_attn_in['k_b'], 'L1_attn_k_g': _L1_attn_in['k_g'], 'L1_attn_k_be': _L1_attn_in['k_be'], 'L1_attn_k_m': _L1_attn_in['k_m'], 'L1_attn_k_v': _L1_attn_in['k_v'], 'L1_attn_v_w': _L1_attn_in['v_w'], 'L1_attn_v_b': _L1_attn_in['v_b'], 'L1_attn_v_g': _L1_attn_in['v_g'], 'L1_attn_v_be': _L1_attn_in['v_be'], 'L1_attn_v_m': _L1_attn_in['v_m'], 'L1_attn_v_v': _L1_attn_in['v_v'], 'L1_attn_p_w': _L1_attn_in['p_w'], 'L1_attn_p_b': _L1_attn_in['p_b'], 'L1_attn_p_g': _L1_attn_in['p_g'], 'L1_attn_p_be': _L1_attn_in['p_be'], 'L1_attn_p_m': _L1_attn_in['p_m'], 'L1_attn_p_v': _L1_attn_in['p_v'], 'L1_attn_f1_w': _L1_attn_in['f1_w'], 'L1_attn_f1_b': _L1_attn_in['f1_b'], 'L1_attn_f1_g': _L1_attn_in['f1_g'], 'L1_attn_f1_be': _L1_attn_in['f1_be'], 'L1_attn_f1_m': _L1_attn_in['f1_m'], 'L1_attn_f1_v': _L1_attn_in['f1_v'], 'L1_attn_f2_w': _L1_attn_in['f2_w'], 'L1_attn_f2_b': _L1_attn_in['f2_b'], 'L1_attn_f2_g': _L1_attn_in['f2_g'], 'L1_attn_f2_be': _L1_attn_in['f2_be'], 'L1_attn_f2_m': _L1_attn_in['f2_m'], 'L1_attn_f2_v': _L1_attn_in['f2_v'], 'L1_ffn_W1': _L1_ffn_in['W1'], 'L1_ffn_b1': _L1_ffn_in['b1'], 'L1_ffn_W2': _L1_ffn_in['W2'], 'L1_ffn_b2': _L1_ffn_in['b2'], 'L1_ffn_Wg': _L1_ffn_in['Wg'], 'L1_ffn_bg': _L1_ffn_in['bg'], 'L2_attn_W_qkv': _L2_attn_in['W_qkv'], 'L2_attn_b_qkv': _L2_attn_in['b_qkv'], 'L2_attn_W_out': _L2_attn_in['W_out'], 'L2_attn_b_out': _L2_attn_in['b_out'], 'L2_ffn_ln_g': _L2_ffn_in['ln_g'], 'L2_ffn_ln_b': _L2_ffn_in['ln_b'], 'L2_ffn_w_r': _L2_ffn_in['w_r'], 'L2_ffn_b_r': _L2_ffn_in['b_r'], 'L2_ffn_W1': _L2_ffn_in['W1'], 'L2_ffn_b1': _L2_ffn_in['b1'], 'L2_ffn_W2': _L2_ffn_in['W2'], 'L2_ffn_b2': _L2_ffn_in['b2'], 'L3_attn_W_qkv': _L3_attn_in['W_qkv'], 'L3_attn_b_qkv': _L3_attn_in['b_qkv'], 'L3_attn_W_out': _L3_attn_in['W_out'], 'L3_attn_b_out': _L3_attn_in['b_out'], 'L3_attn_decay_logits': _L3_attn_in['decay_logits'], 'L3_attn_ln_g': _L3_attn_in['ln_g'], 'L3_attn_ln_b': _L3_attn_in['ln_b'], 'L3_ffn_gate_w': _L3_ffn_in['gate_w'], 'L3_ffn_expert_bias': _L3_ffn_in['expert_bias'], 'L3_ffn_shared_gate_up': _L3_ffn_in['shared_gate_up'], 'L3_ffn_shared_down': _L3_ffn_in['shared_down'], 'L3_ffn_expert_gate_up': _L3_ffn_in['expert_gate_up'], 'L3_ffn_expert_down': _L3_ffn_in['expert_down']}

def reference(x, cls_tok, L0_tok_W1_w, L0_tok_W1_b, L0_tok_W1_sw, L0_tok_W1_sb, L0_tok_W2_w, L0_tok_W2_b, L0_tok_W2_sw, L0_tok_W2_sb, L0_tok_W3_w, L0_tok_W3_b, L0_tok_eps_in1, L0_tok_eps_out1, L0_tok_eps_in2, L0_tok_eps_out2, L0_attn_delta_w, L0_attn_qkv_w, L0_attn_g1, L0_attn_g2, L0_attn_g3, L0_ffn_g1, L0_ffn_g2, L0_ffn_W1, L0_ffn_b1, L0_ffn_W2, L0_ffn_b2, L1_attn_q_w, L1_attn_q_b, L1_attn_q_g, L1_attn_q_be, L1_attn_q_m, L1_attn_q_v, L1_attn_k_w, L1_attn_k_b, L1_attn_k_g, L1_attn_k_be, L1_attn_k_m, L1_attn_k_v, L1_attn_v_w, L1_attn_v_b, L1_attn_v_g, L1_attn_v_be, L1_attn_v_m, L1_attn_v_v, L1_attn_p_w, L1_attn_p_b, L1_attn_p_g, L1_attn_p_be, L1_attn_p_m, L1_attn_p_v, L1_attn_f1_w, L1_attn_f1_b, L1_attn_f1_g, L1_attn_f1_be, L1_attn_f1_m, L1_attn_f1_v, L1_attn_f2_w, L1_attn_f2_b, L1_attn_f2_g, L1_attn_f2_be, L1_attn_f2_m, L1_attn_f2_v, L1_ffn_W1, L1_ffn_b1, L1_ffn_W2, L1_ffn_b2, L1_ffn_Wg, L1_ffn_bg, L2_attn_W_qkv, L2_attn_b_qkv, L2_attn_W_out, L2_attn_b_out, L2_ffn_ln_g, L2_ffn_ln_b, L2_ffn_w_r, L2_ffn_b_r, L2_ffn_W1, L2_ffn_b1, L2_ffn_W2, L2_ffn_b2, L3_attn_W_qkv, L3_attn_b_qkv, L3_attn_W_out, L3_attn_b_out, L3_attn_decay_logits, L3_attn_ln_g, L3_attn_ln_b, L3_ffn_gate_w, L3_ffn_expert_bias, L3_ffn_shared_gate_up, L3_ffn_shared_down, L3_ffn_expert_gate_up, L3_ffn_expert_down):
    import jax
    import jax.numpy as jnp

    def _L0_tok_ref(inputs, W1_w, W1_b, W1_sw, W1_sb, W2_w, W2_b, W2_sw, W2_sb, W3_w, W3_b, eps_in1, eps_out1, eps_in2, eps_out2):
        import math
        import jax, jax.numpy as jnp
        import numpy as np
        PW = PH = 16
        EMB = 128
        HID = 128
        B, H, W = (64, 128, 128)
        L = H // PW * (W // PH)
        SIGMA_ZERO = 0.1

        def _f_noise(x):
            return jnp.sign(x) * jnp.sqrt(jnp.abs(x))

        def _noisy_linear(x, w, b, sw, sb, eps_in, eps_out):
            ei = _f_noise(eps_in)
            eo = _f_noise(eps_out)
            w_n = w + sw * (eo[:, None] * ei[None, :])
            b_n = b + sb * eo
            return x @ w_n.T + b_n

        def _unfold_patches(x):
            b = x.shape[0]
            p = x.reshape(b, H // PW, PW, W // PH, PH)
            p = p.transpose(0, 1, 3, 2, 4)
            return p.reshape(b, L, PW * PH)

        def _pos_encoding(x):
            pos = jnp.arange(L, dtype=jnp.float32)[:, None]
            div = jnp.exp(jnp.arange(0, EMB, 2, dtype=jnp.float32) * (-math.log(10000.0) / EMB))
            ang = pos * div
            pe = jnp.stack([jnp.sin(ang), jnp.cos(ang)], axis=-1).reshape(L, EMB)
            return x + pe[None, :, :]
        x = _unfold_patches(inputs)
        g = _noisy_linear(x, W1_w, W1_b, W1_sw, W1_sb, eps_in1, eps_out1)
        x_gate = g * jnp.tanh(jax.nn.softplus(g))
        x_inner = _noisy_linear(x, W2_w, W2_b, W2_sw, W2_sb, eps_in2, eps_out2)
        x = x_gate * x_inner
        x = x @ W3_w.T + W3_b
        return _pos_encoding(x)

    def _L0_attn_ref(x, delta_w, qkv_w, g1, g2, g3):
        import jax, jax.numpy as jnp
        import numpy as np
        EPS = 1.1920929e-07

        def _rmsnorm(x, g):
            inv = jax.lax.rsqrt(jnp.mean(x * x, axis=-1, keepdims=True) + EPS)
            return x * inv * g
        B, T, C = x.shape
        H = 8
        D = C // H
        sqrt_d = jnp.float32(D) ** 0.5
        W = qkv_w + delta_w
        w = (x @ W.T).reshape(B, T, H, D).transpose(0, 2, 1, 3)
        att = jnp.einsum('bhif,bhjf->bhij', _rmsnorm(w, g1), _rmsnorm(w, g2)) / sqrt_d
        score = jax.nn.softmax(att, axis=-1) + jax.nn.softmax(att, axis=-2)
        y = jnp.einsum('bhij,bhjf->bihf', score, _rmsnorm(w, g3))
        return y.reshape(B, T, C) @ W

    def _L0_ffn_ref(x, g1, g2, W1, b1, W2, b2):
        import jax, jax.numpy as jnp
        import numpy as np
        D_MODEL, N_GROUPS, N_EXPERTS = (128, 8, 8)
        TOP_K_L1, TOP_K_L2 = (2, 2)
        BATCH, SEQ = (2, 128)
        B, S, d = x.shape
        G, E = (g1.shape[1], g2.shape[2])
        xt = x.reshape(-1, d)
        logits1 = xt @ g1
        v1, i1 = jax.lax.top_k(logits1, TOP_K_L1)
        w1 = jax.nn.softmax(v1.astype(jnp.float32), axis=-1).astype(x.dtype)
        c1 = jnp.sum(jax.nn.one_hot(i1, G, dtype=x.dtype) * w1[..., None], axis=1)
        logits2 = jnp.einsum('td,gde->tge', xt, g2)
        v2, i2 = jax.lax.top_k(logits2, TOP_K_L2)
        w2 = jax.nn.softmax(v2.astype(jnp.float32), axis=-1).astype(x.dtype)
        c2 = jnp.sum(jax.nn.one_hot(i2, E, dtype=x.dtype) * w2[..., None], axis=2)
        h = jax.nn.relu(jnp.einsum('td,gedh->tgeh', xt, W1) + b1)
        y = jnp.einsum('tgeh,gehd->tged', h, W2) + b2
        group_out = jnp.einsum('tged,tge->tgd', y, c2)
        out = jnp.einsum('tgd,tg->td', group_out, c1)
        return out.reshape(B, S, d)

    def _L1_attn_ref(x, q_w, q_b, q_g, q_be, q_m, q_v, k_w, k_b, k_g, k_be, k_m, k_v, v_w, v_b, v_g, v_be, v_m, v_v, p_w, p_b, p_g, p_be, p_m, p_v, f1_w, f1_b, f1_g, f1_be, f1_m, f1_v, f2_w, f2_b, f2_g, f2_be, f2_m, f2_v):
        import jax, jax.numpy as jnp
        import numpy as np
        BN_EPS = 1e-05
        B, N, C, H, HID = (16, 256, 128, 8, 512)

        def _bn(x, g, b, m, v):
            return (x - m) * (g * jax.lax.rsqrt(v + BN_EPS)) + b

        def _stage(x, w, bias, g, be, m, v):
            return jax.nn.relu(_bn(x @ w.T + bias, g, be, m, v))
        b, n, c = x.shape
        hd = c // H

        def heads(t):
            return t.reshape(b, n, H, hd).transpose(0, 2, 1, 3)
        q = heads(_stage(x, q_w, q_b, q_g, q_be, q_m, q_v))
        k = heads(_stage(x, k_w, k_b, k_g, k_be, k_m, k_v))
        v = heads(_stage(x, v_w, v_b, v_g, v_be, v_m, v_v))
        attn = jnp.einsum('bhqd,bhkd->bhqk', q, k) * 0.125
        o = jnp.einsum('bhqk,bhkd->bhqd', attn, v)
        o = o.transpose(0, 2, 1, 3).reshape(b, n, c)
        o = jax.nn.relu(o)
        x1 = x + _stage(o, p_w, p_b, p_g, p_be, p_m, p_v)
        h = _stage(x1, f1_w, f1_b, f1_g, f1_be, f1_m, f1_v)
        y = _stage(h, f2_w, f2_b, f2_g, f2_be, f2_m, f2_v)
        return x1 + y

    def _L1_ffn_ref(x, W1, b1, W2, b2, Wg, bg):
        import jax, jax.numpy as jnp
        import numpy as np
        B, N, D, E = (8, 2048, 128, 8)
        H = 2 * D
        Bs, Ns, Ds = x.shape
        xf = x.reshape(Bs * Ns, Ds)
        logits = xf @ Wg + bg
        idx = jnp.argmax(logits, axis=-1)
        out = jnp.zeros_like(xf)
        num_experts = W1.shape[0]
        for e in range(num_experts):
            h = jax.nn.relu(xf @ W1[e] + b1[e])
            y = h @ W2[e] + b2[e]
            out = jnp.where((idx == e)[:, None], y, out)
        return out.reshape(Bs, Ns, Ds)

    def _L2_attn_ref(x, W_qkv, b_qkv, W_out, b_out):
        import jax, jax.numpy as jnp
        import numpy as np
        B, S, E = x.shape
        H = 8
        D = E // H
        qkv = x @ W_qkv.T + b_qkv
        qkv = qkv.reshape(B, S, H, 3 * D)
        q, k, v = jnp.split(qkv, 3, axis=-1)
        q = jax.nn.sigmoid(q)
        k = jax.nn.sigmoid(k)
        i = jnp.sum(q * jnp.sum(k, axis=1, keepdims=True), axis=3, keepdims=True)
        o = jnp.sum(k * jnp.sum(q, axis=1, keepdims=True), axis=3, keepdims=True)
        i_hat = jnp.sum(q * jnp.sum(k / o, axis=1, keepdims=True), axis=3, keepdims=True)
        o_hat = jnp.sum(k * jnp.sum(q / i, axis=1, keepdims=True), axis=3, keepdims=True)
        vw = v * jax.nn.softmax(o_hat, axis=1)
        kv = jnp.einsum('bshd,bshe->bsde', k, vw)
        r = jnp.einsum('bshd,bsde->bshe', q / i, kv) * jax.nn.sigmoid(i_hat)
        values = r.reshape(B, S, E)
        return values @ W_out.T + b_out

    def _L2_ffn_ref(x, ln_g, ln_b, w_r, b_r, W1, b1, W2, b2):
        import jax, jax.numpy as jnp
        import numpy as np
        D = 128
        E = 8
        K = 2
        EXP = 4
        LN_EPS = 1e-05
        B, T, d = x.shape
        mu = jnp.mean(x, axis=-1, keepdims=True)
        var = jnp.mean(jnp.square(x - mu), axis=-1, keepdims=True)
        h = (x - mu) * jax.lax.rsqrt(var + LN_EPS) * ln_g + ln_b
        logits = jnp.einsum('btd,ed->bte', h, w_r) + b_r
        topk_vals, topk_idx = jax.lax.top_k(logits, K)
        gates = jax.nn.softmax(topk_vals, axis=-1)
        hf = h.reshape(B * T, d)
        hid = jax.nn.gelu(jnp.einsum('nd,edf->nef', hf, W1) + b1, approximate=False)
        expert_stack = jnp.einsum('nef,efd->ned', hid, W2) + b2
        idx_flat = topk_idx.reshape(B * T, K)
        gates_flat = gates.reshape(B * T, K)
        gathered = jnp.take_along_axis(expert_stack, idx_flat[:, :, None], axis=1)
        mixed = jnp.sum(gathered * gates_flat[:, :, None], axis=1).reshape(B, T, d)
        return x + mixed

    def _L3_attn_ref(x, W_qkv, b_qkv, W_out, b_out, decay_logits, ln_g, ln_b):
        import jax, jax.numpy as jnp
        import numpy as np
        import math
        D_MODEL = 128
        NUM_HEADS = 8
        LN_EPS = 1e-05
        B, L, D = x.shape
        H = NUM_HEADS
        E = D // H
        qkv = x @ W_qkv + b_qkv
        q, k, v = jnp.split(qkv, 3, axis=-1)
        q = q.reshape(B, L, H, E)
        k = k.reshape(B, L, H, E)
        v = v.reshape(B, L, H, E)
        q = (jax.nn.elu(q) + 1.0) / math.sqrt(E)
        k = jax.nn.elu(k) + 1.0
        lam = 0.99 + 0.01 * jax.nn.sigmoid(decay_logits)
        lam = lam.reshape(1, 1, H, 1)
        idx = jnp.arange(L, dtype=jnp.float32).reshape(1, L, 1, 1)
        decay_k = lam ** (-idx)
        decay_q = lam ** idx
        k_d = k * decay_k
        kv = jnp.einsum('blhe,blhf->blhef', k_d, v)
        mem = jnp.cumsum(kv, axis=1)
        k_sum = jnp.cumsum(k_d, axis=1)
        q_d = q * decay_q
        num = jnp.einsum('blhe,blhef->blhf', q_d, mem)
        den = jnp.einsum('blhe,blhe->blh', q_d, k_sum)[..., None] + 1e-06
        out = (num / den).reshape(B, L, D)
        out = out @ W_out + b_out
        mu = jnp.mean(out, axis=-1, keepdims=True)
        var = jnp.var(out, axis=-1, keepdims=True)
        return (out - mu) / jnp.sqrt(var + LN_EPS) * ln_g + ln_b

    def _L3_ffn_ref(x, gate_w, expert_bias, shared_gate_up, shared_down, expert_gate_up, expert_down):
        import jax, jax.numpy as jnp
        import numpy as np
        D_MODEL = 128
        D_FF = 128
        N_EXPERTS = 16
        TOP_K = 3
        BATCH, SEQ = (1, 512)

        def _swiglu(combined):
            gate, up = jnp.split(combined, 2, axis=-1)
            return jax.nn.silu(gate) * up
        B, S, D = x.shape
        xf = x.reshape(-1, D)
        shared_out = _swiglu(xf @ shared_gate_up.T) @ shared_down.T
        logits = xf @ gate_w.T
        affinity = jax.nn.sigmoid(logits)
        routing_scores = affinity + expert_bias
        _, sel = jax.lax.top_k(routing_scores, TOP_K)
        sel_aff = jnp.take_along_axis(affinity, sel, axis=1)
        gating = sel_aff / (sel_aff.sum(axis=-1, keepdims=True) + 1e-09)
        combined = jnp.einsum('td,efd->tef', xf, expert_gate_up)
        hidden = _swiglu(combined)
        expert_out = jnp.einsum('tef,edf->ted', hidden, expert_down)
        sel_out = jnp.take_along_axis(expert_out, sel[:, :, None], axis=1)
        routed_out = jnp.einsum('tk,tkd->td', gating, sel_out)
        out = shared_out + routed_out
        return out.reshape(B, S, D)
    h = _L0_tok_ref(x, L0_tok_W1_w, L0_tok_W1_b, L0_tok_W1_sw, L0_tok_W1_sb, L0_tok_W2_w, L0_tok_W2_b, L0_tok_W2_sw, L0_tok_W2_sb, L0_tok_W3_w, L0_tok_W3_b, L0_tok_eps_in1, L0_tok_eps_out1, L0_tok_eps_in2, L0_tok_eps_out2)
    h = jnp.concatenate([jnp.broadcast_to(cls_tok, (h.shape[0], 1, h.shape[2])), h], axis=1)
    h = h + _L0_attn_ref(_layernorm(h, axis=-1), L0_attn_delta_w, L0_attn_qkv_w, L0_attn_g1, L0_attn_g2, L0_attn_g3)
    h = h + _L0_ffn_ref(_layernorm(h, axis=-1), L0_ffn_g1, L0_ffn_g2, L0_ffn_W1, L0_ffn_b1, L0_ffn_W2, L0_ffn_b2)
    h = h + _L1_attn_ref(_layernorm(h, axis=-1), L1_attn_q_w, L1_attn_q_b, L1_attn_q_g, L1_attn_q_be, L1_attn_q_m, L1_attn_q_v, L1_attn_k_w, L1_attn_k_b, L1_attn_k_g, L1_attn_k_be, L1_attn_k_m, L1_attn_k_v, L1_attn_v_w, L1_attn_v_b, L1_attn_v_g, L1_attn_v_be, L1_attn_v_m, L1_attn_v_v, L1_attn_p_w, L1_attn_p_b, L1_attn_p_g, L1_attn_p_be, L1_attn_p_m, L1_attn_p_v, L1_attn_f1_w, L1_attn_f1_b, L1_attn_f1_g, L1_attn_f1_be, L1_attn_f1_m, L1_attn_f1_v, L1_attn_f2_w, L1_attn_f2_b, L1_attn_f2_g, L1_attn_f2_be, L1_attn_f2_m, L1_attn_f2_v)
    h = h + _L1_ffn_ref(_layernorm(h, axis=-1), L1_ffn_W1, L1_ffn_b1, L1_ffn_W2, L1_ffn_b2, L1_ffn_Wg, L1_ffn_bg)
    h = h + _L2_attn_ref(_layernorm(h, axis=-1), L2_attn_W_qkv, L2_attn_b_qkv, L2_attn_W_out, L2_attn_b_out)
    h = h + _L2_ffn_ref(_layernorm(h, axis=-1), L2_ffn_ln_g, L2_ffn_ln_b, L2_ffn_w_r, L2_ffn_b_r, L2_ffn_W1, L2_ffn_b1, L2_ffn_W2, L2_ffn_b2)
    h = h + _L3_attn_ref(_layernorm(h, axis=-1), L3_attn_W_qkv, L3_attn_b_qkv, L3_attn_W_out, L3_attn_b_out, L3_attn_decay_logits, L3_attn_ln_g, L3_attn_ln_b)
    h = h + _L3_ffn_ref(_layernorm(h, axis=-1), L3_ffn_gate_w, L3_ffn_expert_bias, L3_ffn_shared_gate_up, L3_ffn_shared_down, L3_ffn_expert_gate_up, L3_ffn_expert_down)
    return h

_drawn_inputs = setup_inputs


def setup_inputs(seed=0):
    import zlib

    import numpy as np

    out = dict(_drawn_inputs(seed))
    spreads = {'L0_tok_W1_sw': (0.0062500000931322575, 0.6),
     'L0_tok_W1_sb': (0.0062500000931322575, 0.6),
     'L0_tok_W2_sw': (0.0062500000931322575, 0.6),
     'L0_tok_W2_sb': (0.0062500000931322575, 0.6),
     'L0_attn_g1': (1.0, 0.6),
     'L0_attn_g2': (1.0, 0.6),
     'L0_attn_g3': (1.0, 0.2),
     'L0_ffn_b1': (0.0, 0.729),
     'L0_ffn_b2': (0.0, 0.303),
     'L1_ffn_b1': (0.0, 2.0),
     'L1_ffn_b2': (0.0, 0.8),
     'L1_ffn_bg': (0.0, 0.1),
     'L2_attn_b_qkv': (0.0, 2.0),
     'L2_attn_b_out': (0.0, 0.8),
     'L2_ffn_ln_g': (1.0, 0.6),
     'L2_ffn_ln_b': (0.0, 2.0),
     'L2_ffn_b_r': (0.0, 2.0),
     'L2_ffn_b1': (0.0, 2.0),
     'L2_ffn_b2': (0.0, 2.0),
     'L3_attn_b_qkv': (0.0, 2.0),
     'L3_attn_b_out': (0.0, 2.0),
     'L3_attn_decay_logits': (0.0, 2.0),
     'L3_attn_ln_g': (1.0, 0.6),
     'L3_attn_ln_b': (0.0, 0.8),
     'L3_ffn_expert_bias': (0.0, 2.0)}
    factors = {'L0_tok_W1_b': 5.62,
     'L0_tok_W2_b': 5.961,
     'L0_tok_eps_in1': 2.903,
     'L0_tok_eps_in2': 2.695,
     'L0_ffn_W1': 3.071,
     'L1_attn_q_w': 4.681,
     'L1_attn_q_b': 8.0,
     'L1_attn_q_g': 8.0,
     'L1_attn_q_be': 8.0,
     'L1_attn_q_m': 6.545,
     'L1_attn_q_v': 8.0,
     'L1_attn_k_w': 4.138,
     'L1_attn_k_b': 8.0,
     'L1_attn_k_g': 8.0,
     'L1_attn_k_be': 5.371,
     'L1_attn_k_m': 4.441,
     'L1_attn_k_v': 8.0,
     'L1_attn_v_b': 8.0,
     'L1_attn_v_g': 8.0,
     'L1_attn_v_be': 5.019,
     'L1_attn_v_m': 4.839,
     'L1_attn_v_v': 8.0,
     'L1_attn_p_b': 64.0,
     'L1_attn_p_g': 8.0,
     'L1_attn_p_v': 6.493,
     'L1_attn_f1_b': 64.0,
     'L1_attn_f1_g': 8.0,
     'L1_attn_f1_be': 35.984,
     'L1_attn_f1_m': 38.096,
     'L1_attn_f1_v': 8.0,
     'L1_attn_f2_b': 57.384,
     'L1_attn_f2_g': 8.0,
     'L1_attn_f2_v': 7.28,
     'L1_ffn_W1': 25.768,
     'L2_attn_W_qkv': 64.0,
     'L2_attn_W_out': 64.0,
     'L3_ffn_gate_w': 64.0,
     'L3_ffn_shared_gate_up': 32.269,
     'L3_ffn_shared_down': 38.36,
     'L3_ffn_expert_gate_up': 47.769,
     'L3_ffn_expert_down': 59.99,
     'L1_attn_p_be': 8.0,
     'L1_attn_p_m': 8.0,
     'L1_attn_f2_be': 8.0,
     'L1_attn_f2_m': 8.0,
     'L1_ffn_W2': 8.0,
     'L1_ffn_Wg': 8.0,
     'L2_ffn_w_r': 8.0,
     'L2_ffn_W1': 8.0,
     'L2_ffn_W2': 8.0,
     'L3_attn_W_qkv': 8.0,
     'L3_attn_W_out': 8.0}
    for name, (base, spread) in spreads.items():
        noise = np.random.default_rng([zlib.crc32(name.encode()), seed]).standard_normal(out[name].shape)
        drawn = base * np.exp(spread * noise) if base else spread * noise
        out[name] = jnp.asarray(drawn.astype(out[name].dtype))
    for name, factor in factors.items():
        out[name] = (out[name] * factor).astype(out[name].dtype)
    return out
```

```python
from contextlib import ExitStack

import concourse.bass as bass
import numpy as np
from concourse import mybir

F32 = mybir.dt.float32
BF16 = mybir.dt.bfloat16
ALU = mybir.AluOpType
ACT = mybir.ActivationFunctionType
AX = mybir.AxisListType.X

D = 128
B = 8
PATCH = 16
SIDE = 128 // PATCH
NPATCH = SIDE * SIDE
T = NPATCH + 1
N = B * T
HALF = N // 2
HB = B // 2
H = 8
HD = D // H
VW = HD + 1
TT = 104
NT = N // TT
BANK = 512
PARTS = 32
NFF1 = 512 // D

CONST_BLOCKS = [
    ("ident", D), ("mean", D), ("blk_mean", D), ("blk_one", D), ("blk_kv", D), ("headmask", H),
    ("rev", 16), ("index", T), ("causal", T), ("pos", NPATCH), ("perm", 7 * D), ("eps", 2),
]
CONST_AT = {}
_at = 0
for _name, _w in CONST_BLOCKS:
    CONST_AT[_name] = (_at, _w)
    _at += _w
CONST_W = _at

BN_STAGES = ["q", "k", "v", "p", "f2"]
COLS = (["ei1a", "ei1b", "ei2a", "ei2b", "eo1", "eo2", "b1", "b2", "sb1", "sb2", "b3", "cls", "g1", "g2", "g3"]
        + [f"bn_{p}_{s}" for p in "bgemv" for s in BN_STAGES + ["f1_0", "f1_1", "f1_2", "f1_3"]]
        + ["l2bq", "l2bk", "l2bv", "l2bo", "l2g", "l2b", "l3bq", "l3bk", "l3bv", "l3bo", "l3dl", "l3g", "l3b"])
COL = {name: i for i, name in enumerate(COLS)}
NBN = len(BN_STAGES) + 4

MATS = (["w1a", "w1b", "w2a", "w2b", "s1a", "s1b", "s2a", "s2b", "w3", "a0qT", "a0dT", "a0q", "a0d",
         "a1q", "a1k", "a1v", "a1p"] + [f"a1f1_{c}" for c in range(NFF1)] + [f"a1f2_{c}" for c in range(NFF1)]
        + ["a2q", "a2k", "a2v", "a2o", "a3q", "a3k", "a3v", "a3o"])
MAT = {name: i for i, name in enumerate(MATS)}
MATS_FIRST = MAT["a1q"]
ROUTE_W = [72, 8, 8, 16]
ROUTE_AT = [0, 72, 80, 88]
ROUTES = sum(ROUTE_W)


class Moe:

    def __init__(self, layer, experts, hidden, cols, unroll, gated):
        self.layer, self.E, self.cols, self.U, self.gated = layer, experts, cols, unroll, gated
        self.I = experts // unroll
        self.S = 2 if gated else hidden // D
        self.groups = max(1, experts // PARTS)

    def expert(self, i, u):
        if self.groups == 1:
            return i * self.U + u, 0, i * self.U + u
        g, r = u % self.groups, i * (self.U // self.groups) + u // self.groups
        return r + g * PARTS, g, r


MOES = [Moe(0, 64, 256, 512, 4, False), Moe(1, 8, 256, 512, 2, False),
        Moe(2, 8, 512, 1024, 2, False), Moe(3, 16, 128, 384, 2, True)]


def tower(nc, patches, consts, sel_d, cols_d, mats_d, route_d, rows_eo, bias_rows,
          w_moe, b1_moe, b2_moe, out):
    ctx = ExitStack()
    with ctx:
        def sb(name, shape, dt=F32):
            return ctx.enter_context(nc.sbuf_tensor(name, shape, dt))

        def sem(name):
            return ctx.enter_context(nc.semaphore(name))

        cst = sb("cst", [D, CONST_W])

        def const(name, k=None, w=None):
            at, width = CONST_AT[name]
            if k is not None:
                at, width = at + k * w, w
            return cst[:, at:at + width]

        sel = sb("sel", [D, PARTS * D], BF16)
        col = sb("col", [D, len(COLS)])
        mats = sb("mats", [D, len(MATS), D])
        route_w = sb("route_w", [D, ROUTES])
        xp = sb("xp", [D, 2, BANK])
        eo_rows = sb("eo_rows", [D, 2, D])
        bias_bc = sb("bias_bc", [D, 32])

        h = sb("h", [D, N])
        xn = sb("xn", [D, N])
        hx = sb("hx", [D, N])
        xc = sb("xc", [D, N])
        sq = sb("sq", [D, N])
        std = sb("std", [D, N])
        rstd = sb("rstd", [D, N])
        t = [sb(f"t{i}", [D, N]) for i in range(10)]
        qm = sb("qm", [D, H, N])
        vtok = sb("vtok", [T, B, H, VW])
        vtok2 = sb("vtok2", [T, 2, H, HD])
        ea = sb("ea", [T, 2, H, T])
        eb = sb("eb", [T, 2, H, T])
        eat = sb("eat", [T, 2, H, T])
        sm = sb("sm", [T, 2, 6, H])
        ytok = sb("ytok", [T, B, D])
        ktok = sb("ktok", [T, B, D])
        vtok1 = sb("vtok1", [T, B, D])
        kv = sb("kv", [D, B, D])
        h1 = sb("h1", [D, NFF1, N])
        sums = sb("sums", [D, 8, B])
        decay = sb("decay", [D, 2, T])
        bnst = sb("bnst", [D, 3, NBN])
        bns = sb("bns", [D, NBN])
        bnb = sb("bnb", [D, NBN])
        small = sb("small", [D, 16])
        nz = sb("nz", [D, 3, 6 + 2 * D])
        g1m = sb("g1m", [D, H])

        NLMAX = NT * 72
        lg = sb("lg", [TT, NLMAX])
        r_oh = [sb(f"r_oh{i}", [TT, NLMAX]) for i in range(4)]
        r_s = sb("r_s", [TT, 8, NT * 9])
        gates = sb("gates", [TT, NT, 64])
        res = sb("res", [TT, NT, 64])
        parts = sb("parts", [TT, NT, 2, 4, PARTS], BF16)
        gT = sb("gT", [64, N])
        stack = sb("stack", [D, 2, N], BF16)
        cb = sb("cb", [D, 2, N])
        ab = sb("ab", [D, 2, N])
        tb = sb("tb", [D, 2, HALF])
        gb = sb("gb", [D, 2, N])
        identb = sb("identb", [D, D], BF16)
        aff = sb("aff", [TT, NT * 16])
        w_sb = [sb(f"w{m.layer}_sb", [D, m.U, m.cols]) for m in MOES]
        ws_sb = sb("ws_sb", [D, 384])
        b1_sb = [sb(f"b1_{m.layer}", [D, m.E * m.S]) for m in MOES[:3]]
        b2_sb = [sb(f"b2_{m.layer}", [m.E, D]) for m in MOES[:3]]

        ps = ctx.enter_context(nc.psum_tensor("ps", [D, 8, BANK], F32))

        def psb(bank):
            return ps[:, bank, :].bitcast(BF16)

        def pair(k, rows=D):
            return ps[0:rows, 2 * k:2 * k + 2, 0:HALF]

        def two(ap):
            return ap.rearrange("p (a n) -> p a n", a=2)

        def img(ap):
            return ap.rearrange("p (b t) -> p b t", b=B)

        names = """ld_const ld_sel ld_col ld_mat0 ld_mat1 ld_route ld_patch ld_eo ld_bias ld_shared
        dve_chain
        noise_abs noise_root wn_ready emb_g emb_clamped emb_e emb_x emb_proj h_ready
        ln_mean ln_centred ln_squared ln_var ln_std ln_out ln_post pool_ready identb_ready
        a0_w a0_wsum a0_sq a0_ms a0_std a0_q a0_vF a0_vT a0_vtok a0_scores a0_ea_in a0_eb_in a0_ea a0_eb a0_eT a0_eat a0_v2
        a0_y a0_ytok a0_yT a0_yF a0_out
        bn_std bn_ready a1_qkv a1_v a1_tr a1_tok a1_kv a1_kvm a1_o a1_orelu a1_p a1_prelu a1_x1
        a1_f1 a1_h1 a1_f2 a1_y
        a2_qkv a2_in a2_prod a2_io a2_prod2 a2_hats a2_sig a2_einp a2_e a2_ks a2_qk a2_A a2_vw a2_vs a2_vse a2_t a2_acc a2_r a2_out
        a3_qkv a3_v a3_lam a3_lnlam a3_dec a3_min a3_exp a3_qk a3_vT a3_vtok a3_scores a3_att a3_y a3_ytok a3_yT a3_yF a3_out a3_z
        stored""".split()
        S = {n: sem(n) for n in names}
        rt = {n: sem(f"route_{n}") for n in ("logits", "aff", "d", "e", "parts", "gT", "ready", "shared")}
        RT_E = {0: 1, 2: 2, 3: 2}
        RT_T = {0: 2, 1: 4, 2: 6, 3: 7}
        RT_READY = {0: 3, 1: 5, 2: 7, 3: 8}
        moe_done = sem("moe_done")
        mo = [{n: sem(f"m{m}_{n}") for n in ("cb_done", "cb_ready", "h_ready", "a_ready", "g_ready", "g_used")}
              for m in range(4)]
        mo[3]["t_ready"] = sem("m3_t_ready")

        w_loaded = [[sem(f"w{m.layer}_loaded{u}") for u in range(m.U)] for m in MOES]

        def wait(eng, s, value):
            if isinstance(value, int) and value <= 0:
                return
            eng.wait_ge(s, value)

        block = ctx.enter_context(nc.Block())

        def mat(name):
            return mats[:, MAT[name], :]

        def c_(name):
            return col[:, COL[name]:COL[name] + 1]

        @block.sync
        def _(sp):
            sp.dma_start(col[:, :], cols_d).then_inc(S["ld_col"], 16)
            sp.dma_start(eo_rows[:, :, :], rows_eo.rearrange("(o a) n -> o a n", o=1).broadcast_to([D, 2, D])).then_inc(S["ld_eo"], 16)
            sp.dma_start(mats[:, 0:MATS_FIRST, :], mats_d[:, 0:MATS_FIRST, :]).then_inc(S["ld_mat0"], 16)
            sp.dma_start(xp[:, :, :], patches).then_inc(S["ld_patch"], 16)
            sp.dma_start(cst[:, :], consts).then_inc(S["ld_const"], 16)
            sp.dma_start(route_w[:, :], route_d).then_inc(S["ld_route"], 16)
            sp.dma_start(sel[:, :], sel_d).then_inc(S["ld_sel"], 16)
            for m in range(3):
                sp.dma_start(b1_sb[m][:, :], b1_moe[m]).then_inc(S["ld_bias"], 16)
                sp.dma_start(b2_sb[m][:, :], b2_moe[m]).then_inc(S["ld_bias"], 16)
            sp.dma_start(bias_bc[:, :], bias_rows.rearrange("(o n) -> o n", o=1).broadcast_to([D, 32])).then_inc(S["ld_bias"], 16)
            sp.dma_start(mats[:, MATS_FIRST:, :], mats_d[:, MATS_FIRST:, :]).then_inc(S["ld_mat1"], 16)
            for m in MOES:
                L = m.layer

                def load(i, u):
                    e, _, _ = m.expert(i, u)
                    if m.gated:
                        e = e + 1
                    wait(sp, mo[L]["g_used"], ((i - 1) * m.U + u + 1) * m.S)
                    src = w_moe[L][e] if isinstance(e, int) else w_moe[L][bass.ds(e, 1)].rearrange("o p n -> p (o n)")
                    sp.dma_start(w_sb[L][:, u, :], src).then_inc(w_loaded[L][u], 16)

                if m.gated:
                    sp.dma_start(ws_sb[:, :], w_moe[L][0]).then_inc(S["ld_shared"], 16)
                for u in range(m.U):
                    load(0, u)
                with sp.Fori(1, m.I) as i:
                    for u in range(m.U):
                        load(i, u)
            sp.wait_ge(S["h_ready"], 10)
            sp.dma_start(out, h[:, :]).then_inc(S["stored"], 16)
            sp.wait_ge(S["stored"], 16)

        @block.tensor
        def _(pe):
            def mm(o, lhsT, rhs, start=True, stop=True, **kw):
                return nc.tensor.matmul(o, lhsT, rhs, start=start, stop=stop, **kw)

            def full(k, lhsT, src, start=True, stop=True):
                for a in range(2):
                    last = mm(ps[:, 2 * k + a, 0:HALF], lhsT, src[:, a * HALF:(a + 1) * HALF], start, stop)
                return last

            def ln(k, src):
                full(0, const("mean"), src).then_inc(S["ln_mean"], 1)
                pe.wait_ge(S["ln_squared"], k + 1)
                full(1, const("mean"), sq[:, :]).then_inc(S["ln_var"], 1)

            pe.wait_ge(S["ld_patch"], 16)
            for l in range(2):
                pe.wait_ge(S["wn_ready"], l + 1)
                for c in range(2):
                    last = mm(ps[:, l, :], t[6 + l][:, c * D:(c + 1) * D], xp[:, c, :], c == 0, c == 1)
                last.then_inc(S["emb_g"], 1)
            pe.wait_ge(S["emb_x"], 1)
            mm(ps[:, 2, :], mat("w3"), t[4][:, 0:BANK]).then_inc(S["emb_proj"], 1)

            pe.wait_ge(S["ld_const"], 16)
            pe.wait_ge(S["h_ready"], 1)
            ln(0, h)
            pe.wait_ge(S["ln_out"], 1)
            pe.wait_ge(S["a0_wsum"], 1)
            full(0, mat("a0qT"), xn).then_inc(S["a0_w"], 1)
            pe.wait_ge(S["a0_sq"], 1)
            full(1, const("blk_mean"), sq[:, :]).then_inc(S["a0_ms"], 1)

            def to_tokens(src, banks, ready):
                for b in range(B):
                    last = nc.tensor.transpose(ps[0:T, banks + b // HB, (b % HB) * D:(b % HB + 1) * D],
                                               src[:, b * T:(b + 1) * T], const("ident"))
                last.then_inc(ready, 1)

            pe.wait_ge(S["a0_vF"], 1)
            to_tokens(t[2], 0, S["a0_vT"])
            pe.wait_ge(S["a0_q"], 1)

            def scores_ij(b):
                for hh in range(H):
                    last = mm(ps[0:T, hh // 4, (hh % 4) * T:(hh % 4 + 1) * T],
                              qm[:, hh, b * T:(b + 1) * T], t[1][:, b * T:(b + 1) * T])
                last.then_inc(S["a0_scores"], 1)

            def scores_ji(b, k, ready):
                for a in range(2):
                    last = mm(ps[0:T, 2 * k + a, 0:HALF].rearrange("p (h t) -> p h t", h=4), t[1][:, b * T:(b + 1) * T],
                              qm[:, 4 * a:4 * a + 4, b * T:(b + 1) * T])
                last.then_inc(ready, 1)

            pe.wait_ge(S["a0_vtok"], 1)
            scores_ij(0)
            scores_ji(0, 1, S["a0_scores"])
            for b in range(B):
                if b + 1 < B:
                    pe.wait_ge(S["a0_ea_in"], b + 1)
                    scores_ij(b + 1)
                    pe.wait_ge(S["a0_eb_in"], b + 1)
                    scores_ji(b + 1, 1, S["a0_scores"])
                pe.wait_ge(S["a0_ea"], b + 1)
                wait(pe, S["a0_eat"], b)
                for hh in range(H):
                    last = nc.tensor.transpose(ps[0:T, 4 + hh // 4, (hh % 4) * T:(hh % 4 + 1) * T],
                                               ea[:, b % 2, hh, :], const("ident")[0:T, 0:T])
                last.then_inc(S["a0_eT"], 1)
                pe.wait_ge(S["a0_eat"], b + 1)
                pe.wait_ge(S["a0_v2"], b + 1)
                wait(pe, S["a0_ytok"], b - 1)
                for hh in range(H):
                    mm(ps[0:T, 6 + b % 2, hh * VW:(hh + 1) * VW], eat[:, b % 2, hh, :], vtok[:, b, hh, :])
                for hh in range(H):
                    last = mm(ps[0:T, 6 + b % 2, H * VW + hh * HD:H * VW + (hh + 1) * HD],
                              eb[:, b % 2, hh, :], vtok2[:, b % 2, hh, :])
                last.then_inc(S["a0_y"], 1)

            def to_features(done, ready):
                for b in range(B):
                    pe.wait_ge(done, b + 1)
                    last = nc.tensor.transpose(ps[:, b // HB, (b % HB) * T:(b % HB + 1) * T], ytok[:, b, :],
                                               const("ident")[0:T, 0:T])
                last.then_inc(ready, 1)

            to_features(S["a0_ytok"], S["a0_yT"])
            pe.wait_ge(S["a0_yF"], 1)
            full(1, mat("a0q"), t[3]).then_inc(S["a0_out"], 1)

            def route(m, src):
                if m.layer == 0:
                    pe.wait_ge(S["identb_ready"], 1)
                w, at = ROUTE_W[m.layer], ROUTE_AT[m.layer]
                for k in range(NT):
                    last = mm(ps[0:TT, 0, k * w:(k + 1) * w], src[:, k * TT:(k + 1) * TT], route_w[:, at:at + w])
                last.then_inc(rt["logits"], 1)
                pe.wait_ge(rt["parts"], m.layer + 1)
                if not m.gated:
                    for k in range(NT):
                        last = nc.tensor.transpose(ps[0:m.E, 2 + k // 4, (k % 4) * TT:(k % 4 + 1) * TT],
                                                   gates[:, k, 0:m.E], const("ident")[0:TT, 0:TT])
                    last.then_inc(rt["gT"], 1)
                for g in range(m.groups):
                    for k in range(NT):
                        last = nc.tensor.transpose(psb(4 + g)[:, k * TT:(k + 1) * TT],
                                                   parts[:, k, g, :, :].rearrange("p a b -> p (a b)"), identb[0:TT, 0:TT])
                last.then_inc(rt["gT"], 1)

            def experts(m, src, res_src):
                L, X = m.layer, mo[m.layer]
                W = w_sb[L]

                def broadcast(i, u):
                    _, g, r = m.expert(i, u)
                    n = i * m.U + u
                    wait(pe, X["cb_ready"], n)
                    for a in range(2):
                        last = mm(ps[:, 4 + a, 0:HALF], sel[:, bass.ds(r * D, D)], stack[:, g, a * HALF:(a + 1) * HALF])
                    last.then_inc(X["cb_done"], 1)

                def first(i, u, s):
                    k = (i * m.U + u) * m.S + s
                    if s == 0:
                        pe.wait_ge(w_loaded[L][u], (i + 1) * 16)
                        broadcast(i, u)
                    if m.gated:
                        wait(pe, X["t_ready"], k - 1)
                        for j in range(2):
                            last = mm(ps[:, 2 * (s % 2) + j, 0:HALF], W[:, u, j * D:(j + 1) * D], src[:, s * HALF:(s + 1) * HALF])
                    else:
                        wait(pe, X["a_ready"], k - 1)
                        last = full(s % 2, W[:, u, s * D:(s + 1) * D], src)
                    last.then_inc(X["h_ready"], 1)

                def second(i, u, s):
                    k = (i * m.U + u) * m.S + s
                    pe.wait_ge(X["g_ready"], k + 1)
                    if m.gated:
                        last = mm(ps[:, 6 + s, 0:HALF], W[:, u, 2 * D:3 * D], gb[:, s, 0:HALF], False, False)
                    else:
                        last = full(3, W[:, u, (m.S + s) * D:(m.S + s + 1) * D], gb[:, s % 2, :], False, False)
                    last.then_inc(X["g_used"], 1)

                def body(i, final):
                    for u in range(m.U):
                        for s in range(m.S):
                            s2, u2, i2 = (s + 1, u, i) if s + 1 < m.S else (0, u + 1, i) if u + 1 < m.U else (0, 0, i + 1)
                            if not (final and u == m.U - 1 and s == m.S - 1):
                                first(i2, u2, s2)
                            second(i, u, s)

                pe.wait_ge(rt["ready"], RT_READY[L])
                if L == 0:
                    pe.wait_ge(S["ld_sel"], 16)
                if m.gated:
                    pe.wait_ge(S["ld_shared"], 16)
                    for s in range(2):
                        for j in range(2):
                            last = mm(ps[:, 2 * s + j, 0:HALF], ws_sb[:, j * D:(j + 1) * D], src[:, s * HALF:(s + 1) * HALF])
                        last.then_inc(moe_done, 1)
                    for s in range(2):
                        pe.wait_ge(rt["shared"], s + 1)
                        mm(ps[:, 6 + s, 0:HALF], ws_sb[:, 2 * D:3 * D], gb[:, s, 0:HALF], True, False).then_inc(moe_done, 1)
                else:
                    for a in range(2):
                        mm(ps[:, 6 + a, 0:HALF], b2_sb[L][:, :], gT[0:m.E, a * HALF:(a + 1) * HALF], True, False)
                first(0, 0, 0)
                body(0, False)
                with pe.Fori(1, m.I - 1) as i:
                    body(i, False)
                body(m.I - 1, True)
                full(3, const("ident"), res_src, False, True).then_inc(moe_done, 1)

            pe.wait_ge(S["h_ready"], 2)
            ln(1, h)
            pe.wait_ge(S["ln_out"], 2)
            pe.wait_ge(S["ld_route"], 16)
            route(MOES[0], xn)
            pe.wait_ge(S["ld_bias"], 7 * 16)
            experts(MOES[0], xn, h)

            pe.wait_ge(S["h_ready"], 3)
            ln(2, h)
            pe.wait_ge(S["ln_out"], 3)
            pe.wait_ge(S["ld_mat1"], 16)
            for k, name in enumerate(("a1q", "a1k", "a1v")):
                full((0, 1, 2)[k], mat(name), xn).then_inc(S["a1_qkv"], 1)
            pe.wait_ge(S["a1_v"], 1)
            to_tokens(t[1], 0, S["a1_tr"])
            to_tokens(t[2], 2, S["a1_tr"])
            pe.wait_ge(S["a1_tok"], 2)
            for b in range(B):
                last = mm(ps[:, 4 + b // HB, (b % HB) * D:(b % HB + 1) * D], ktok[:, b, :], vtok1[:, b, :])
            last.then_inc(S["a1_kv"], 1)
            pe.wait_ge(S["a1_kvm"], 1)
            for b in range(B):
                last = mm(ps[:, b // HB, (b % HB) * T:(b % HB + 1) * T], kv[:, b, :], t[0][:, b * T:(b + 1) * T])
            last.then_inc(S["a1_o"], 1)
            pe.wait_ge(S["a1_orelu"], 1)
            full(1, mat("a1p"), t[3]).then_inc(S["a1_p"], 1)
            pe.wait_ge(S["a1_x1"], 1)
            for c in range(NFF1):
                if c == 3:
                    pe.wait_ge(S["a1_h1"], 1)
                full(c % 3, mat(f"a1f1_{c}"), t[5]).then_inc(S["a1_f1"], 1)
            for c in range(NFF1):
                pe.wait_ge(S["a1_h1"], c + 1)
                last = full(3, mat(f"a1f2_{c}"), h1[:, c, :], c == 0, c == NFF1 - 1)
            last.then_inc(S["a1_f2"], 1)

            pe.wait_ge(S["h_ready"], 4)
            ln(3, h)
            pe.wait_ge(S["ln_out"], 4)
            route(MOES[1], xn)
            experts(MOES[1], xn, h)

            pe.wait_ge(S["h_ready"], 5)
            ln(4, h)
            pe.wait_ge(S["ln_out"], 5)
            for k, name in enumerate(("a2q", "a2k", "a2v")):
                full(k, mat(name), xn).then_inc(S["a2_qkv"], 1)
            pe.wait_ge(S["a2_prod"], 1)
            full(0, const("blk_one"), t[3]).then_inc(S["a2_io"], 1)
            pe.wait_ge(S["a2_prod"], 2)
            full(1, const("blk_one"), t[4]).then_inc(S["a2_io"], 1)
            pe.wait_ge(S["a2_prod2"], 1)
            pe.wait_ge(S["a2_in"], 3)
            full(2, const("blk_one"), t[3]).then_inc(S["a2_hats"], 1)
            pe.wait_ge(S["a2_prod2"], 2)
            full(3, const("blk_one"), t[4]).then_inc(S["a2_hats"], 1)
            pe.wait_ge(S["a2_vw"], 1)
            for dlt in range(H):
                if dlt:
                    P = const("perm", dlt - 1, D)
                    pe.wait_ge(S["a2_qk"], dlt)
                    full(0, P, t[1]).then_inc(S["a2_ks"], 1)
                    wait(pe, S["a2_vse"], dlt - 1)
                    full(3, P, t[2]).then_inc(S["a2_vs"], 1)
                pe.wait_ge(S["a2_qk"], dlt + 1)
                wait(pe, S["a2_t"], dlt)
                full(1, const("blk_one"), t[3 + dlt % 2]).then_inc(S["a2_A"], 1)
            pe.wait_ge(S["a2_r"], 1)
            full(2, mat("a2o"), t[5]).then_inc(S["a2_out"], 1)

            pe.wait_ge(S["h_ready"], 6)
            ln(5, h)
            pe.wait_ge(S["ln_out"], 6)
            ln(6, xn)
            pe.wait_ge(S["ln_post"], 1)
            route(MOES[2], hx)
            pe.wait_ge(S["h_ready"], 7)
            experts(MOES[2], hx, h)

            pe.wait_ge(S["h_ready"], 8)
            ln(7, h)
            pe.wait_ge(S["ln_out"], 8)
            for k, name in enumerate(("a3q", "a3k", "a3v")):
                full(k, mat(name), xn).then_inc(S["a3_qkv"], 1)
            pe.wait_ge(S["a3_v"], 1)
            pe.wait_ge(S["a3_qk"], 1)
            to_tokens(t[2], 0, S["a3_vT"])
            pe.wait_ge(S["a3_vtok"], 1)
            scores_ji(0, 1, S["a3_scores"])
            for b in range(B):
                if b + 1 < B:
                    wait(pe, S["a3_att"], b)
                    scores_ji(b + 1, 1 + (b + 1) % 2, S["a3_scores"])
                pe.wait_ge(S["a3_att"], b + 1)
                wait(pe, S["a3_ytok"], b - 1)
                for hh in range(H):
                    last = mm(ps[0:T, 6 + b % 2, hh * VW:(hh + 1) * VW], ea[:, b % 2, hh, :], vtok[:, b, hh, :])
                last.then_inc(S["a3_y"], 1)
            to_features(S["a3_ytok"], S["a3_yT"])
            pe.wait_ge(S["a3_yF"], 1)
            full(2, mat("a3o"), t[3]).then_inc(S["a3_out"], 1)
            pe.wait_ge(S["a3_z"], 1)
            ln(8, t[4])

            pe.wait_ge(S["h_ready"], 9)
            ln(9, h)
            pe.wait_ge(S["ln_out"], 10)
            route(MOES[3], xn)
            experts(MOES[3], xn, h)


        @block.scalar
        def _(act):
            def fn(o, i, f, **kw):
                return nc.scalar.activation(o, i, f, **kw)

            eps_ln = const("eps")[:, 0:1]
            eps_rms = const("eps")[:, 1:2]

            def ln(k):
                act.wait_ge(S["ln_centred"], k + 1)
                fn(sq[:, :], xc[:, :], ACT.Square).then_inc(S["ln_squared"], 1)
                act.wait_ge(S["ln_var"], k + 1)
                fn(two(std[:, :]), pair(1), ACT.Sqrt, bias=eps_ln).then_inc(S["ln_std"], 1)

            act.wait_ge(S["ld_col"], 16)
            act.wait_ge(S["ld_eo"], 16)
            e6, erow = col[:, 0:6], eo_rows[:, :, :].rearrange("p a n -> p (a n)")
            fn(nz[:, 0, 0:6], e6, ACT.Abs)
            fn(nz[:, 0, 6:], erow, ACT.Abs).then_inc(S["noise_abs"], 1)
            fn(nz[:, 2, 0:6], e6, ACT.Sign)
            fn(nz[:, 2, 6:], erow, ACT.Sign)
            act.wait_ge(S["noise_abs"], 1)
            fn(nz[:, 1, :], nz[:, 0, :], ACT.Sqrt).then_inc(S["noise_root"], 1)
            act.wait_ge(S["emb_clamped"], 1)
            fn(t[2][:, 0:BANK], t[0][:, 0:BANK], ACT.Exp).then_inc(S["emb_e"], 1)
            act.wait_ge(S["ld_const"], 16)
            fn(small[:, 4:5], c_("l3dl"), ACT.Sigmoid).then_inc(S["a3_lam"], 1)
            act.wait_ge(S["a3_lnlam"], 1)
            fn(small[:, 6:7], small[:, 5:6], ACT.Ln).then_inc(S["a3_lam"], 1)
            act.wait_ge(S["a3_lnlam"], 2)
            fn(decay[:, 0, :], const("index"), ACT.Exp, scale=small[:, 6:7])
            fn(decay[:, 1, :], const("index"), ACT.Exp, scale=small[:, 7:8]).then_inc(S["a3_dec"], 1)
            fn(bnst[:, 0, :], col[:, COL["bn_v_q"]:COL["bn_v_q"] + NBN], ACT.Sqrt, bias=eps_ln).then_inc(S["bn_std"], 1)

            ln(0)
            act.wait_ge(S["a0_w"], 1)
            fn(two(sq[:, :]), pair(0), ACT.Square).then_inc(S["a0_sq"], 1)
            act.wait_ge(S["a0_ms"], 1)
            fn(two(std[:, :]), pair(1), ACT.Sqrt, bias=eps_rms).then_inc(S["a0_std"], 1)
            for b in range(B):
                act.wait_ge(S["a0_ea_in"], b + 1)
                fn(ea[:, b % 2], ea[:, b % 2], ACT.Exp).then_inc(S["a0_ea"], 1)
                act.wait_ge(S["a0_eb_in"], b + 1)
                fn(eb[:, b % 2], eb[:, b % 2], ACT.Exp).then_inc(S["a0_eb"], 1)
                act.wait_ge(S["a0_eT"], b + 1)
                wait(act, S["a0_y"], b - 1)
                fn(eat[:, b % 2].rearrange("p (a h) n -> p a (h n)", a=2), pair(2, T), ACT.Copy).then_inc(S["a0_eat"], 1)
            act.wait_ge(S["a0_yT"], 1)
            fn(two(t[3][:, :]), pair(0), ACT.Copy).then_inc(S["a0_yF"], 1)

            def route(m):
                R = rt
                if m.gated:
                    act.wait_ge(R["logits"], m.layer + 1)
                    fn(aff[:, :], ps[0:TT, 0, 0:NT * m.E], ACT.Sigmoid).then_inc(R["aff"], 1)
                    return
                if m.layer != 1:
                    act.wait_ge(R["d"], RT_E[m.layer])
                    n = NT * 9 if m.layer == 0 else NT
                    fn(r_s[:, 4, 0:n], r_s[:, 3, 0:n], ACT.Exp).then_inc(R["e"], 1)
                act.wait_ge(R["gT"], RT_T[m.layer] - 1)
                fn(gT[0:m.E, 0:4 * TT], ps[0:m.E, 2, 0:4 * TT], ACT.Copy)
                fn(gT[0:m.E, 4 * TT:N], ps[0:m.E, 3, 0:N - 4 * TT], ACT.Copy).then_inc(R["ready"], 1)

            def experts(m, func):
                L, X = m.layer, mo[m.layer]
                if m.gated:
                    for s in range(2):
                        act.wait_ge(moe_done, 4 + s)
                        fn(ab[:, s, 0:HALF], ps[:, 2 * s, 0:HALF], func).then_inc(rt["e"], 1)

                def body(i):
                    for u in range(m.U):
                        e, _, _ = m.expert(i, u)
                        n = i * m.U + u
                        act.wait_ge(X["cb_done"], n + 1)
                        wait(act, X["g_ready"], (n - 1) * m.S)
                        fn(two(cb[:, u % 2, :]), pair(2), ACT.Copy).then_inc(X["cb_ready"], 1)
                        for s in range(m.S):
                            k = n * m.S + s
                            act.wait_ge(X["h_ready"], k + 1)
                            if m.gated:
                                wait(act, X["t_ready"], k - 1)
                                if isinstance(i, int) and i == 0 and u == 0:
                                    act.wait_ge(rt["shared"], 2)
                                fn(ab[:, s, 0:HALF], ps[:, 2 * s, 0:HALF], func).then_inc(X["a_ready"], 1)
                            else:
                                wait(act, X["g_ready"], k - 1)
                                at = e * m.S + s
                                bias = b1_sb[L][:, at:at + 1] if isinstance(at, int) else b1_sb[L][:, bass.ds(at, 1)]
                                fn(two(ab[:, s % 2, :]), pair(s % 2), func, bias=bias).then_inc(X["a_ready"], 1)

                if L == 0:
                    act.wait_ge(S["ld_bias"], 7 * 16)
                body(0)
                with act.Fori(1, m.I - 1) as i:
                    body(i)
                body(m.I - 1)

            ln(1)
            route(MOES[0])
            experts(MOES[0], ACT.Relu)

            def bn(o, i, k):
                return fn(o, i, ACT.Relu, scale=bns[:, k:k + 1], bias=bnb[:, k:k + 1])

            ln(2)
            act.wait_ge(S["bn_ready"], 1)
            for k in range(3):
                act.wait_ge(S["a1_qkv"], k + 1)
                last = bn(two(t[k][:, :]), pair(k), k)
            last.then_inc(S["a1_v"], 1)
            act.wait_ge(S["a1_tr"], 2)
            fn(vtok1[:, :, :].rearrange("p (a b) n -> p a (b n)", a=2), ps[0:T, 2:4, :], ACT.Copy).then_inc(S["a1_tok"], 1)
            act.wait_ge(S["a1_o"], 1)
            fn(two(t[3][:, :]), pair(0), ACT.Relu).then_inc(S["a1_orelu"], 1)
            act.wait_ge(S["a1_p"], 1)
            bn(two(t[4][:, :]), pair(1), 3).then_inc(S["a1_prelu"], 1)
            for c in range(NFF1):
                act.wait_ge(S["a1_f1"], c + 1)
                bn(two(h1[:, c, :]), pair(c % 3), 5 + c).then_inc(S["a1_h1"], 1)
            act.wait_ge(S["a1_f2"], 1)
            bn(two(t[6][:, :]), pair(3), 4).then_inc(S["a1_y"], 1)

            ln(3)
            route(MOES[1])
            experts(MOES[1], ACT.Relu)

            ln(4)
            act.wait_ge(S["a2_qkv"], 1)
            fn(two(t[0][:, :]), pair(0), ACT.Sigmoid, bias=c_("l2bq")).then_inc(S["a2_in"], 1)
            act.wait_ge(S["a2_qkv"], 2)
            fn(two(t[1][:, :]), pair(1), ACT.Sigmoid, bias=c_("l2bk")).then_inc(S["a2_in"], 1)
            act.wait_ge(S["a2_qkv"], 3)
            fn(two(t[2][:, :]), pair(2), ACT.Identity, bias=c_("l2bv")).then_inc(S["a2_in"], 1)
            act.wait_ge(S["a2_hats"], 1)
            fn(two(t[9][:, :]), pair(2), ACT.Sigmoid).then_inc(S["a2_sig"], 1)
            act.wait_ge(S["a2_einp"], 1)
            fn(t[6][:, :], t[6][:, :], ACT.Exp).then_inc(S["a2_e"], 1)
            for d in range(1, H):
                act.wait_ge(S["a2_vs"], d)
                wait(act, S["a2_t"], d - 1)
                fn(two(ab[:, d % 2, :]), pair(3), ACT.Copy).then_inc(S["a2_vse"], 1)

            ln(5)
            ln(6)
            route(MOES[2])
            experts(MOES[2], ACT.Gelu)

            ln(7)
            act.wait_ge(S["a3_qkv"], 3)
            fn(two(t[2][:, :]), pair(2), ACT.Identity, bias=c_("l3bv")).then_inc(S["a3_v"], 1)
            for k in range(2):
                act.wait_ge(S["a3_min"], k + 1)
                fn(t[k][:, :], t[k][:, :], ACT.Exp).then_inc(S["a3_exp"], 1)
            act.wait_ge(S["a3_yT"], 1)
            fn(two(t[3][:, :]), pair(0), ACT.Copy).then_inc(S["a3_yF"], 1)
            act.wait_ge(S["a3_out"], 1)
            fn(two(t[4][:, :]), pair(2), ACT.Identity, bias=c_("l3bo")).then_inc(S["a3_z"], 1)
            ln(8)
            ln(9)
            route(MOES[3])
            experts(MOES[3], ACT.Silu)

        @block.vector
        def _(dve):
            V = nc.vector
            chain = [0]

            def link(ins):
                chain[0] += 1
                ins.then_inc(S["dve_chain"], 1)
                dve.wait_ge(S["dve_chain"], chain[0])

            def bc(ap, *shape):
                return ap.broadcast_to(list(shape))

            def per_img(cols_):
                return bc(cols_.unsqueeze(2), D, B, T)

            def pair4(k, rows=D):
                return ps[0:rows, 2 * k:2 * k + 2, 0:HALF].rearrange("p a (b t) -> p a b t", b=HB)

            def img4(ap):
                return ap.rearrange("p (a b t) -> p a b t", a=2, b=HB)

            def ln(k, src, o=None):
                dve.wait_ge(S["ln_mean"], k + 1)
                V.tensor_tensor(two(xc[:, :]), two(src[:, :]), pair(0), ALU.subtract).then_inc(S["ln_centred"], 1)
                dve.wait_ge(S["ln_std"], k + 1)
                link(V.reciprocal(rstd[:, :], std[:, :]))
                V.tensor_tensor((xn if o is None else o)[:, :], xc[:, :], rstd[:, :], ALU.mult).then_inc(S["ln_out"], 1)

            dve.wait_ge(S["noise_root"], 1)
            link(V.tensor_tensor(nz[:, 0, :], nz[:, 1, :], nz[:, 2, :], ALU.mult))
            dve.wait_ge(S["ld_mat0"], 16)
            for l in range(2):
                row = nz[:, 0, 6 + l * D:6 + (l + 1) * D]
                tmp = t[8][:, 0:2 * D].rearrange("p (c n) -> p c n", c=2)
                link(V.tensor_tensor(tmp, mats[:, 4 + 2 * l:6 + 2 * l, :], bc(row.unsqueeze(1), D, 2, D), ALU.mult))
                for c in range(2):
                    last = V.scalar_tensor_tensor(t[6 + l][:, c * D:(c + 1) * D], t[8][:, c * D:(c + 1) * D],
                                                  nz[:, 0, 2 * l + c:2 * l + c + 1], mats[:, 2 * l + c, :], ALU.mult, ALU.add)
                last.then_inc(S["wn_ready"], 1)
                dve.wait_ge(S["wn_ready"], l + 1)
            for l in range(2):
                link(V.scalar_tensor_tensor(small[:, l:l + 1], c_(f"sb{l + 1}"), nz[:, 0, 4 + l:5 + l], c_(f"b{l + 1}"),
                                            ALU.mult, ALU.add))
            E_ = slice(0, BANK)
            dve.wait_ge(S["emb_g"], 1)
            V.tensor_scalar(t[0][:, E_], ps[:, 0, :], small[:, 0:1], 20.0, ALU.add, ALU.min).then_inc(S["emb_clamped"], 1)
            V.tensor_scalar(t[1][:, E_], ps[:, 0, :], small[:, 0:1], None, ALU.add)
            dve.wait_ge(S["emb_e"], 1)
            link(V.scalar_tensor_tensor(t[3][:, E_], t[2][:, E_], 2.0, t[2][:, E_], ALU.add, ALU.mult))
            link(V.tensor_scalar(t[5][:, E_], t[3][:, E_], 2.0, None, ALU.add))
            link(V.reciprocal(t[5][:, E_], t[5][:, E_]))
            link(V.tensor_tensor(t[3][:, E_], t[3][:, E_], t[5][:, E_], ALU.mult))
            link(V.tensor_tensor(t[3][:, E_], t[3][:, E_], t[1][:, E_], ALU.mult))
            dve.wait_ge(S["emb_g"], 2)
            V.scalar_tensor_tensor(t[4][:, E_], ps[:, 1, :], small[:, 1:2], t[3][:, E_], ALU.add, ALU.mult).then_inc(S["emb_x"], 1)
            V.tensor_copy(img(h[:, :])[:, :, 0:1], bc(c_("cls").unsqueeze(2), D, B, 1))
            dve.wait_ge(S["emb_proj"], 1)
            dve.wait_ge(S["ld_const"], 16)
            V.scalar_tensor_tensor(img(h[:, :])[:, :, 1:T], ps[:, 2, :].rearrange("p (b t) -> p b t", b=B), c_("b3"),
                                   bc(const("pos").unsqueeze(1), D, B, NPATCH), ALU.add, ALU.add).then_inc(S["h_ready"], 1)

            V.tensor_tensor(mat("a0qT"), mat("a0qT"), mat("a0dT"), ALU.add)
            V.tensor_tensor(mat("a0q"), mat("a0q"), mat("a0d"), ALU.add).then_inc(S["a0_wsum"], 1)
            link(V.tensor_scalar(g1m[:, :], const("headmask"), c_("g1"), 1.0 / HD ** 0.5, ALU.mult, ALU.mult))
            V.tensor_copy(identb[:, :], const("ident")).then_inc(S["identb_ready"], 1)
            dve.wait_ge(S["a3_lam"], 1)
            V.tensor_scalar(small[:, 5:6], small[:, 4:5], 0.01, 0.99, ALU.mult, ALU.add).then_inc(S["a3_lnlam"], 1)
            dve.wait_ge(S["a3_lam"], 2)
            V.tensor_scalar(small[:, 7:8], small[:, 6:7], -1.0, None, ALU.mult).then_inc(S["a3_lnlam"], 1)
            dve.wait_ge(S["a3_dec"], 1)
            link(V.tensor_scalar(decay[:, 0, :], decay[:, 0, :], 1.0 / HD ** 0.5, None, ALU.mult))
            dve.wait_ge(S["bn_std"], 1)

            def bncols(p):
                return col[:, COL[f"bn_{p}_q"]:COL[f"bn_{p}_q"] + NBN]

            link(V.reciprocal(bnst[:, 1, :], bnst[:, 0, :]))
            link(V.tensor_tensor(bns[:, :], bncols("g"), bnst[:, 1, :], ALU.mult))
            link(V.tensor_tensor(bnst[:, 2, :], bncols("b"), bncols("m"), ALU.subtract))
            link(V.tensor_tensor(bnst[:, 2, :], bnst[:, 2, :], bns[:, :], ALU.mult))
            V.tensor_tensor(bnb[:, :], bnst[:, 2, :], bncols("e"), ALU.add).then_inc(S["bn_ready"], 1)

            ln(0, h)
            dve.wait_ge(S["a0_std"], 1)
            link(V.reciprocal(rstd[:, :], std[:, :]))
            link(V.tensor_tensor(two(t[0][:, :]), pair(0), two(rstd[:, :]), ALU.mult))
            V.tensor_scalar(t[2][:, :], t[0][:, :], c_("g3"), None, ALU.mult).then_inc(S["a0_vF"], 1)
            V.tensor_scalar(t[1][:, :], t[0][:, :], c_("g2"), None, ALU.mult)
            for hh in range(H):
                last = V.tensor_scalar(qm[:, hh, :], t[0][:, :], g1m[:, hh:hh + 1], None, ALU.mult)
            last.then_inc(S["a0_q"], 1)

            def value_rows(ready, done):
                dve.wait_ge(ready, 1)
                for a in range(2):
                    last = V.tensor_copy(vtok[:, a * HB:(a + 1) * HB, :, 0:HD].rearrange("p b h d -> p (b h) d"),
                                         ps[0:T, a, :].rearrange("p (n d) -> p n d", d=HD))
                last.then_inc(done, 1)

            dve.wait_ge(S["pool_ready"], 1)
            value_rows(S["a0_vT"], S["a0_vtok"])

            def shift(b, pk, j, dst, done):
                stat = sm[:, b % 2, j, :].rearrange("p (a h) -> p a h", a=2)
                link(V.tensor_reduce(stat, pair4(pk, T), AX, ALU.max))
                V.tensor_tensor(dst[:, b % 2].rearrange("p (a h) n -> p a h n", a=2), pair4(pk, T),
                                bc(stat.unsqueeze(3), T, 2, HB, T), ALU.subtract).then_inc(done, 1)

            def shifts(b):
                dve.wait_ge(S["a0_scores"], 2 * b + 1)
                wait(dve, S["a0_y"], b - 1)
                shift(b, 0, 0, ea, S["a0_ea_in"])
                dve.wait_ge(S["a0_scores"], 2 * b + 2)
                shift(b, 1, 1, eb, S["a0_eb_in"])

            def values2(b):
                dve.wait_ge(S["a0_eb"], b + 1)
                link(V.tensor_reduce(sm[:, b % 2, 2, :], eb[:, b % 2], AX, ALU.add))
                link(V.reciprocal(sm[:, b % 2, 3, :], sm[:, b % 2, 2, :]))
                V.tensor_tensor(vtok2[:, b % 2], vtok[:, b, :, 0:HD], bc(sm[:, b % 2, 3, :].unsqueeze(2), T, H, HD),
                                ALU.mult).then_inc(S["a0_v2"], 1)

            def y_rows(b, eps, extra, ready, done):
                dve.wait_ge(ready, b + 1)
                rows = ps[0:T, 6 + b % 2, 0:H * VW].rearrange("p (h d) -> p h d", h=H)
                den = rows[:, :, HD:VW]
                r = sm[:, b % 2, 4, :]
                yb = ytok[:, b, :].rearrange("p (h d) -> p h d", h=H)
                if eps:
                    link(V.tensor_scalar(sm[:, b % 2, 5, :].unsqueeze(2), den, eps, None, ALU.add))
                    den = sm[:, b % 2, 5, :].unsqueeze(2)
                link(V.reciprocal(r.unsqueeze(2), den))
                last = V.tensor_tensor(yb, rows[:, :, 0:HD], bc(r.unsqueeze(2), T, H, HD), ALU.mult)
                if extra:
                    link(last)
                    last = V.tensor_tensor(ytok[:, b, :], ytok[:, b, :], ps[0:T, 6 + b % 2, H * VW:H * VW + D], ALU.add)
                last.then_inc(done, 1)

            shifts(0)
            for b in range(B + 1):
                if b + 1 < B:
                    shifts(b + 1)
                if b < B:
                    values2(b)
                if b >= 1:
                    y_rows(b - 1, 0, True, S["a0_y"], S["a0_ytok"])
            dve.wait_ge(S["a0_out"], 1)
            V.tensor_tensor(two(h[:, :]), two(h[:, :]), pair(1), ALU.add).then_inc(S["h_ready"], 1)

            def route(m):
                R, E = rt, min(m.E, 8) if m.layer == 0 else m.E
                rows = NT * (9 if m.layer == 0 else 1)
                n = rows * E
                flat = lg[:, 0:n]
                logits = ps[0:TT, 0, 0:n]
                if m.gated:
                    dve.wait_ge(R["aff"], 1)
                    logits = aff[:, :]
                else:
                    dve.wait_ge(R["logits"], m.layer + 1)
                if m.layer == 0:
                    link(V.tensor_copy(flat, logits))
                else:
                    if m.layer == 1:
                        dve.wait_ge(S["ld_bias"], 7 * 16)
                    at = {1: 0, 2: 8, 3: 16}[m.layer]
                    link(V.tensor_tensor(flat.rearrange("p (r e) -> p r e", e=E), logits.rearrange("p (r e) -> p r e", e=E),
                                         bc(bias_bc[0:TT, at:at + E].unsqueeze(1), TT, rows, E), ALU.add))

                def re(ap):
                    return ap[:, 0:n].rearrange("p (r e) -> p r e", e=E)

                def along(stat):
                    return bc(stat.unsqueeze(2), TT, rows, E)

                top = {0: 2, 1: 1, 2: 2, 3: 3}[m.layer]
                rev = bc(const("rev")[0:TT, 0:E].unsqueeze(1), TT, rows, E)
                for j in range(top):
                    mx, rk, oh = r_s[:, j, 0:rows], r_s[:, 6, 0:rows], r_oh[j]
                    link(V.tensor_reduce(mx, re(lg), AX, ALU.max))
                    link(V.tensor_tensor(re(r_oh[3]), re(lg), along(mx), ALU.is_equal))
                    link(V.tensor_tensor(re(r_oh[3]), re(r_oh[3]), rev, ALU.mult))
                    link(V.tensor_reduce(rk, re(r_oh[3]), AX, ALU.max))
                    link(V.tensor_tensor(re(oh), re(r_oh[3]), along(rk), ALU.is_equal))
                    if j + 1 < top:
                        link(V.scalar_tensor_tensor(flat, oh[:, 0:n], -1e30, flat, ALU.mult, ALU.add))
                if m.layer in (0, 2):
                    V.tensor_tensor(r_s[:, 3, 0:rows], r_s[:, 1, 0:rows], r_s[:, 0, 0:rows], ALU.subtract).then_inc(R["d"], 1)
                    dve.wait_ge(R["e"], RT_E[m.layer])
                    link(V.tensor_scalar(r_s[:, 5, 0:rows], r_s[:, 4, 0:rows], 1.0, None, ALU.add))
                    link(V.reciprocal(r_s[:, 5, 0:rows], r_s[:, 5, 0:rows]))
                    link(V.tensor_tensor(r_s[:, 7, 0:rows], r_s[:, 4, 0:rows], r_s[:, 5, 0:rows], ALU.mult))
                    link(V.tensor_tensor(re(r_oh[0]), re(r_oh[0]), along(r_s[:, 5, 0:rows]), ALU.mult))
                    link(V.tensor_tensor(re(r_oh[1]), re(r_oh[1]), along(r_s[:, 7, 0:rows]), ALU.mult))
                    if m.layer == 2:
                        link(V.tensor_tensor(gates[:, :, 0:E], re(r_oh[0]), re(r_oh[1]), ALU.add))
                    else:
                        link(V.tensor_tensor(re(r_oh[3]), re(r_oh[0]), re(r_oh[1]), ALU.add))
                        g4 = r_oh[3][:, 0:n].rearrange("p (k r e) -> p k r e", k=NT, e=8)
                        for k in range(NT):
                            last = V.tensor_tensor(gates[:, k, :].rearrange("p (g e) -> p g e", g=8), g4[:, k, 1:9, :],
                                                   bc(g4[:, k, 0, :].unsqueeze(2), TT, 8, 8), ALU.mult)
                        link(last)
                elif m.layer == 1:
                    link(V.tensor_copy(gates[:, :, 0:E], re(r_oh[0])))
                else:
                    link(V.tensor_tensor(re(r_oh[0]), re(r_oh[0]), re(r_oh[1]), ALU.add))
                    link(V.tensor_tensor(re(r_oh[0]), re(r_oh[0]), re(r_oh[2]), ALU.add))
                    link(V.tensor_tensor(re(r_oh[0]), re(r_oh[0]), re(aff), ALU.mult))
                    link(V.tensor_reduce(r_s[:, 3, 0:rows], re(r_oh[0]), AX, ALU.add))
                    link(V.tensor_scalar(r_s[:, 3, 0:rows], r_s[:, 3, 0:rows], 1e-9, None, ALU.add))
                    link(V.reciprocal(r_s[:, 4, 0:rows], r_s[:, 3, 0:rows]))
                    link(V.tensor_tensor(gates[:, :, 0:E], re(r_oh[0]), along(r_s[:, 4, 0:rows]), ALU.mult))
                w = min(m.E, PARTS)
                for g in range(m.groups):
                    src, r = gates[:, :, g * PARTS:g * PARTS + w], res[:, :, g * PARTS:g * PARTS + w]
                    for j in range(3):
                        cpy = V.tensor_copy(parts[:, :, g, j, 0:w], src if j == 0 else r)
                        if j < 2:
                            link(cpy)
                            link(V.tensor_tensor(r, src if j == 0 else r, parts[:, :, g, j, 0:w], ALU.subtract))
                cpy.then_inc(R["parts"], 1)
                dve.wait_ge(R["gT"], RT_T[m.layer])
                for g in range(m.groups):
                    V.tensor_copy(stack[:, g, :], psb(4 + g)[:, 0:N]).then_inc(R["ready"], 1)

            def experts(m):
                L, X = m.layer, mo[m.layer]
                if m.gated:
                    for s in range(2):
                        dve.wait_ge(rt["e"], RT_E[L] + s + 1)
                        V.tensor_tensor(gb[:, s, 0:HALF], ab[:, s, 0:HALF], ps[:, 2 * s + 1, 0:HALF],
                                        ALU.mult).then_inc(rt["shared"], 1)
                    dve.wait_ge(moe_done, 7)

                def body(i):
                    for u in range(m.U):
                        n = i * m.U + u
                        for s in range(m.S):
                            k = n * m.S + s
                            dve.wait_ge(X["a_ready"], k + 1)
                            if m.gated:
                                wait(dve, X["g_ready"], k - 1)
                                V.tensor_tensor(tb[:, s, :], ab[:, s, 0:HALF], ps[:, 2 * s + 1, 0:HALF],
                                                ALU.mult).then_inc(X["t_ready"], 1)
                                dve.wait_ge(X["t_ready"], k + 1)
                            if s == 0:
                                dve.wait_ge(X["cb_ready"], n + 1)
                            wait(dve, X["g_used"], k - 1)
                            if m.gated:
                                V.tensor_tensor(gb[:, s, 0:HALF], tb[:, s, :], cb[:, u % 2, s * HALF:(s + 1) * HALF],
                                                ALU.mult).then_inc(X["g_ready"], 1)
                            else:
                                V.tensor_tensor(gb[:, s % 2, :], ab[:, s % 2, :], cb[:, u % 2, :],
                                                ALU.mult).then_inc(X["g_ready"], 1)

                body(0)
                with dve.Fori(1, m.I - 1) as i:
                    body(i)
                body(m.I - 1)
                dve.wait_ge(moe_done, 8 if m.gated else L + 1)
                V.tensor_copy(two(h[:, :]), pair(3)).then_inc(S["h_ready"], 1)

            ln(1, h)
            route(MOES[0])
            experts(MOES[0])

            ln(2, h)
            dve.wait_ge(S["a1_tr"], 1)
            V.tensor_copy(ktok[:, :, :].rearrange("p (a b) n -> p a (b n)", a=2), ps[0:T, 0:2, :]).then_inc(S["a1_tok"], 1)
            dve.wait_ge(S["a1_kv"], 1)
            V.tensor_tensor(kv[:, :, :], ps[:, 4:6, :].rearrange("p a (b n) -> p (a b) n", n=D),
                            bc(const("blk_kv").unsqueeze(1), D, B, D), ALU.mult).then_inc(S["a1_kvm"], 1)
            dve.wait_ge(S["a1_prelu"], 1)
            V.tensor_tensor(t[5][:, :], xn[:, :], t[4][:, :], ALU.add).then_inc(S["a1_x1"], 1)
            dve.wait_ge(S["a1_x1"], 1)
            link(V.tensor_tensor(h[:, :], h[:, :], t[5][:, :], ALU.add))
            dve.wait_ge(S["a1_y"], 1)
            V.tensor_tensor(h[:, :], h[:, :], t[6][:, :], ALU.add).then_inc(S["h_ready"], 1)

            ln(3, h)
            route(MOES[1])
            experts(MOES[1])

            ln(4, h)
            q, k_, v = t[0], t[1], t[2]
            dve.wait_ge(S["a2_in"], 1)
            link(V.tensor_reduce(sums[:, 0, :], img(q[:, :]), AX, ALU.add))
            dve.wait_ge(S["a2_in"], 2)
            link(V.tensor_reduce(sums[:, 1, :], img(k_[:, :]), AX, ALU.add))
            V.tensor_tensor(img(t[3][:, :]), img(q[:, :]), per_img(sums[:, 1, :]), ALU.mult).then_inc(S["a2_prod"], 1)
            V.tensor_tensor(img(t[4][:, :]), img(k_[:, :]), per_img(sums[:, 0, :]), ALU.mult).then_inc(S["a2_prod"], 1)
            dve.wait_ge(S["a2_io"], 1)
            link(V.reciprocal(two(t[5][:, :]), pair(0)))
            dve.wait_ge(S["a2_io"], 2)
            link(V.reciprocal(two(t[6][:, :]), pair(1)))
            link(V.tensor_tensor(t[7][:, :], k_[:, :], t[6][:, :], ALU.mult))
            link(V.tensor_reduce(sums[:, 2, :], img(t[7][:, :]), AX, ALU.add))
            V.tensor_tensor(img(t[3][:, :]), img(q[:, :]), per_img(sums[:, 2, :]), ALU.mult).then_inc(S["a2_prod2"], 1)
            link(V.tensor_tensor(t[8][:, :], q[:, :], t[5][:, :], ALU.mult))
            link(V.tensor_reduce(sums[:, 3, :], img(t[8][:, :]), AX, ALU.add))
            V.tensor_tensor(img(t[4][:, :]), img(k_[:, :]), per_img(sums[:, 3, :]), ALU.mult).then_inc(S["a2_prod2"], 1)
            dve.wait_ge(S["a2_hats"], 2)
            link(V.tensor_reduce(sums[:, 4, :].rearrange("p (a b) -> p a b", a=2), pair4(3), AX, ALU.max))
            V.tensor_tensor(img4(t[6][:, :]), pair4(3),
                            bc(sums[:, 4, :].rearrange("p (a b) -> p a b", a=2).unsqueeze(3), D, 2, HB, T),
                            ALU.subtract).then_inc(S["a2_einp"], 1)
            dve.wait_ge(S["a2_sig"], 1)
            link(V.tensor_tensor(t[9][:, :], t[9][:, :], t[5][:, :], ALU.mult))
            V.tensor_tensor(t[3][:, :], q[:, :], k_[:, :], ALU.mult).then_inc(S["a2_qk"], 1)
            dve.wait_ge(S["a2_e"], 1)
            link(V.tensor_reduce(sums[:, 5, :], img(t[6][:, :]), AX, ALU.add))
            link(V.reciprocal(sums[:, 6, :], sums[:, 5, :]))
            link(V.tensor_tensor(v[:, :], v[:, :], t[6][:, :], ALU.mult))
            V.tensor_tensor(img(v[:, :]), img(v[:, :]), per_img(sums[:, 6, :]), ALU.mult).then_inc(S["a2_vw"], 1)
            dve.wait_ge(S["a2_vw"], 1)
            for d in range(H):
                if d + 1 < H:
                    dve.wait_ge(S["a2_ks"], d + 1)
                    wait(dve, S["a2_A"], d)
                    V.tensor_tensor(two(t[3 + (d + 1) % 2][:, :]), two(q[:, :]), pair(0), ALU.mult).then_inc(S["a2_qk"], 1)
                dve.wait_ge(S["a2_A"], d + 1)
                if d == 0:
                    V.tensor_tensor(two(t[5][:, :]), two(v[:, :]), pair(1), ALU.mult).then_inc(S["a2_t"], 1)
                else:
                    dve.wait_ge(S["a2_vse"], d)
                    wait(dve, S["a2_acc"], d - 2)
                    V.tensor_tensor(two(t[7 + d % 2][:, :]), two(ab[:, d % 2, :]), pair(1), ALU.mult).then_inc(S["a2_t"], 1)
            dve.wait_ge(S["a2_acc"], H - 1)
            V.tensor_tensor(t[5][:, :], t[5][:, :], t[9][:, :], ALU.mult).then_inc(S["a2_r"], 1)
            dve.wait_ge(S["a2_out"], 1)
            V.scalar_tensor_tensor(two(h[:, :]), pair(2), c_("l2bo"), two(h[:, :]), ALU.add, ALU.add).then_inc(S["h_ready"], 1)

            ln(5, h)
            dve.wait_ge(S["ln_out"], 6)
            V.tensor_tensor(h[:, :], h[:, :], xn[:, :], ALU.add).then_inc(S["h_ready"], 1)
            ln(6, xn, hx)
            dve.wait_ge(S["ln_out"], 7)
            V.tensor_scalar(hx[:, :], hx[:, :], c_("l2g"), c_("l2b"), ALU.mult, ALU.add).then_inc(S["ln_post"], 1)
            route(MOES[2])
            experts(MOES[2])

            ln(7, h)
            for k, name in enumerate(("l3bq", "l3bk")):
                dve.wait_ge(S["a3_qkv"], k + 1)
                V.tensor_scalar(two(t[k][:, :]), pair(k), c_(name), 0.0, ALU.add, ALU.min).then_inc(S["a3_min"], 1)
                link(V.tensor_scalar(two(t[3 + k][:, :]), pair(k), c_(name), 0.0, ALU.add, ALU.max))
            for k in (1, 0):
                dve.wait_ge(S["a3_exp"], k + 1)
                link(V.tensor_tensor(t[k][:, :], t[k][:, :], t[3 + k][:, :], ALU.add))
                link(V.tensor_tensor(img(t[k][:, :]), img(t[k][:, :]), bc(decay[:, k, :].unsqueeze(1), D, B, T), ALU.mult))
            for hh in range(H):
                last = V.tensor_scalar(qm[:, hh, :], t[0][:, :], const("headmask")[:, hh:hh + 1], None, ALU.mult)
            last.then_inc(S["a3_qk"], 1)
            value_rows(S["a3_vT"], S["a3_vtok"])

            def mask(b):
                dve.wait_ge(S["a3_scores"], b + 1)
                wait(dve, S["a3_y"], b - 1)
                V.tensor_tensor(ea[:, b % 2].rearrange("p (a h) n -> p (a h) n", a=2).rearrange("p (a h) n -> p a h n", a=2),
                                pair4(1 + b % 2, T), bc(const("causal")[0:T, :].unsqueeze(1).unsqueeze(1), T, 2, HB, T),
                                ALU.mult).then_inc(S["a3_att"], 1)

            mask(0)
            for b in range(B):
                if b + 1 < B:
                    mask(b + 1)
                y_rows(b, 1e-6, False, S["a3_y"], S["a3_ytok"])
            ln(8, t[4], t[5])
            dve.wait_ge(S["ln_out"], 9)
            link(V.tensor_scalar(t[5][:, :], t[5][:, :], c_("l3g"), c_("l3b"), ALU.mult, ALU.add))
            V.tensor_tensor(h[:, :], h[:, :], t[5][:, :], ALU.add).then_inc(S["h_ready"], 1)
            ln(9, h)
            route(MOES[3])
            experts(MOES[3])

        @block.gpsimd
        def _(pool):
            nc.gpsimd.memset(parts[:, :, :, :, :], 0.0)
            nc.gpsimd.memset(vtok[:, :, :, :], 1.0).then_inc(S["pool_ready"], 1)
            for d in range(1, H):
                pool.wait_ge(S["a2_t"], d + 1)
                wait(pool, S["a2_acc"], d - 1)
                nc.gpsimd.tensor_tensor(t[5][:, :], t[5][:, :], t[7 + d % 2][:, :], ALU.add).then_inc(S["a2_acc"], 1)


def constants():
    blk = np.kron(np.eye(H), np.ones((HD, HD)))
    c = np.zeros((D, CONST_W), np.float32)

    def put(name, a):
        at, w = CONST_AT[name]
        c[:a.shape[0], at:at + a.shape[1]] = a

    put("ident", np.eye(D))
    put("mean", np.full((D, D), 1.0 / D))
    put("blk_mean", blk / HD)
    put("blk_one", blk)
    put("blk_kv", blk * 0.125)
    put("headmask", np.kron(np.eye(H), np.ones((HD, 1))))
    put("rev", np.tile(16.0 - np.arange(16), (D, 1)))
    put("index", np.tile(np.arange(T, dtype=np.float64), (D, 1)))
    put("causal", np.triu(np.ones((T, T))))
    div = np.exp(np.arange(0, D, 2, dtype=np.float32) * np.float32(-np.log(10000.0) / D)).astype(np.float32)
    ang = np.arange(NPATCH, dtype=np.float32)[:, None] * div
    put("pos", np.stack([np.sin(ang), np.cos(ang)], -1).reshape(NPATCH, D).T)
    put("perm", np.concatenate([np.kron(np.roll(np.eye(H), d, axis=0), np.eye(HD)) for d in range(1, H)], axis=1))
    put("eps", np.tile([1e-5, 1.1920929e-07], (D, 1)))
    sel = np.zeros((D, PARTS, D), np.float32)
    for r in range(3 * PARTS):
        sel[r, r % PARTS] = 1.0
    return c, sel.reshape(D, PARTS * D)


def kernel(**inputs):
    import ml_dtypes
    import concourse.bacc as _bacc
    from concourse.bass_utils import run_bass_kernel_spmd as _run

    x = {k: np.asarray(v) for k, v in inputs.items()}
    patches = x["x"].reshape(B, SIDE, PATCH, SIDE, PATCH).transpose(2, 4, 0, 1, 3).reshape(2, D, B * NPATCH).transpose(1, 0, 2)
    consts, sel = constants()

    def heads(a):
        return a.reshape((H, 3, HD) + a.shape[1:]).swapaxes(0, 1).reshape((3, D) + a.shape[1:])

    def tile_heads(a):
        return np.tile(a, H)

    bq2, wq2 = heads(x["L2_attn_b_qkv"]), heads(x["L2_attn_W_qkv"])
    col = {"cls": x["cls_tok"].reshape(D), "b3": x["L0_tok_W3_b"]}
    for l in (1, 2):
        e = x[f"L0_tok_eps_in{l}"]
        col[f"ei{l}a"], col[f"ei{l}b"] = e[:D], e[D:]
        col[f"eo{l}"], col[f"b{l}"], col[f"sb{l}"] = x[f"L0_tok_eps_out{l}"], x[f"L0_tok_W{l}_b"], x[f"L0_tok_W{l}_sb"]
    for g in (1, 2, 3):
        col[f"g{g}"] = tile_heads(x[f"L0_attn_g{g}"])
    for p, key in zip("bgemv", ("b", "g", "be", "m", "v")):
        for s in BN_STAGES:
            col[f"bn_{p}_{s}"] = x[f"L1_attn_{s}_{key}"]
        for c in range(NFF1):
            col[f"bn_{p}_f1_{c}"] = x[f"L1_attn_f1_{key}"][c * D:(c + 1) * D]
    b3 = x["L3_attn_b_qkv"]
    for j, n in enumerate("qkv"):
        col[f"l2b{n}"], col[f"l3b{n}"] = bq2[j], b3[j * D:(j + 1) * D]
    col.update(l2bo=x["L2_attn_b_out"], l2g=x["L2_ffn_ln_g"], l2b=x["L2_ffn_ln_b"], l3bo=x["L3_attn_b_out"],
               l3dl=np.repeat(x["L3_attn_decay_logits"], HD), l3g=x["L3_attn_ln_g"], l3b=x["L3_attn_ln_b"])
    mat = {"w3": x["L0_tok_W3_w"].T, "a0qT": x["L0_attn_qkv_w"].T, "a0dT": x["L0_attn_delta_w"].T,
           "a0q": x["L0_attn_qkv_w"], "a0d": x["L0_attn_delta_w"], "a2o": x["L2_attn_W_out"].T, "a3o": x["L3_attn_W_out"]}
    for l in (1, 2):
        for n, key in (("w", "w"), ("s", "sw")):
            a = x[f"L0_tok_W{l}_{key}"].T
            mat[f"{n}{l}a"], mat[f"{n}{l}b"] = a[:D], a[D:]
    for s in "qkvp":
        mat[f"a1{s}"] = x[f"L1_attn_{s}_w"].T
    for c in range(NFF1):
        mat[f"a1f1_{c}"] = x["L1_attn_f1_w"][c * D:(c + 1) * D].T
        mat[f"a1f2_{c}"] = x["L1_attn_f2_w"][:, c * D:(c + 1) * D].T
    for j, n in enumerate("qkv"):
        mat[f"a2{n}"], mat[f"a3{n}"] = wq2[j].T, x["L3_attn_W_qkv"][:, j * D:(j + 1) * D]
    g2 = x["L0_ffn_g2"].transpose(1, 0, 2).reshape(D, 64)
    route = np.concatenate([x["L0_ffn_g1"], g2, x["L1_ffn_Wg"], x["L2_ffn_w_r"].T, x["L3_ffn_gate_w"].T], axis=1)

    def pack(w1, w2):
        e, f = w1.shape[0], w1.shape[2]
        return np.concatenate([w1, w2.reshape(e, f // D, D, D).transpose(0, 2, 1, 3).reshape(e, D, f)], axis=2)

    gu = np.concatenate([x["L3_ffn_shared_gate_up"][None], x["L3_ffn_expert_gate_up"]], axis=0).transpose(0, 2, 1)
    dn = np.concatenate([x["L3_ffn_shared_down"][None], x["L3_ffn_expert_down"]], axis=0).transpose(0, 2, 1)
    w = [pack(x["L0_ffn_W1"].reshape(64, D, 256), x["L0_ffn_W2"].reshape(64, 256, D)),
         pack(x["L1_ffn_W1"], x["L1_ffn_W2"]), pack(x["L2_ffn_W1"], x["L2_ffn_W2"]), np.concatenate([gu, dn], axis=2)]
    b1 = [x[f"L{l}_ffn_b1"].reshape(-1, D).T for l in range(3)]
    b2 = [x[f"L{l}_ffn_b2"].reshape(-1, D) for l in range(3)]
    data = {
        "patches": patches, "consts": consts, "sel": sel.astype(ml_dtypes.bfloat16),
        "cols": np.stack([col[n] for n in COLS], axis=1), "mats": np.stack([mat[n] for n in MATS], axis=1),
        "route": route, "rows_eo": np.stack([x["L0_tok_eps_out1"], x["L0_tok_eps_out2"]]),
        "bias_rows": np.concatenate([x["L1_ffn_bg"], x["L2_ffn_b_r"], x["L3_ffn_expert_bias"]]),
        **{f"w{l}": w[l] for l in range(4)}, **{f"b1_{l}": b1[l] for l in range(3)}, **{f"b2_{l}": b2[l] for l in range(3)},
    }
    nc = _bacc.Bacc("TRN2", target_bir_lowering=False, num_devices=1)
    arrays, ap = {}, {}
    for name, a in data.items():
        a = np.ascontiguousarray(a)
        arrays[f"in_{name}"] = a
        ap[name] = nc.dram_tensor(f"in_{name}", a.shape, mybir.dt.from_np(a.dtype), kind="ExternalInput").ap()
    out = nc.dram_tensor("out", (D, N), F32, kind="ExternalOutput").ap()
    tower(nc, ap["patches"], ap["consts"], ap["sel"], ap["cols"], ap["mats"], ap["route"], ap["rows_eo"], ap["bias_rows"],
          [ap[f"w{l}"] for l in range(4)], [ap[f"b1_{l}"] for l in range(3)], [ap[f"b2_{l}"] for l in range(3)], out)
    r = _run(nc, [arrays], core_ids=[0])
    return np.ascontiguousarray(r.results[0]["out"].T.reshape(B, T, D))
```

```python
from contextlib import ExitStack

import concourse.bass as bass
import numpy as np
from concourse import mybir

F32 = mybir.dt.float32
F32R = mybir.dt.float32r
BF16 = mybir.dt.bfloat16
ALU = mybir.AluOpType
ACT = mybir.ActivationFunctionType
AX = mybir.AxisListType.X

D = 128
B = 8
PATCH = 16
SIDE = 128 // PATCH
NPATCH = SIDE * SIDE
T = NPATCH + 1
N = B * T
HALF = N // 2
HB = B // 2
H = 8
HD = D // H
VW = HD + 1
TT = 104
NT = N // TT
BANK = 512
PARTS = 32
NFF1 = 512 // D

CONST_BLOCKS = [
    ("ident", D), ("mean", D), ("centre", D), ("blk_mean", D), ("blk_one", D), ("blk_kv", D), ("headmask", H),
    ("rev", 16), ("index", T), ("causal", T), ("pos", NPATCH), ("perm", 7 * D), ("eps", 2),
]
CONST_AT = {}
_at = 0
for _name, _w in CONST_BLOCKS:
    CONST_AT[_name] = (_at, _w)
    _at += _w
CONST_W = _at

BN_STAGES = ["q", "k", "v", "p", "f2"]
COLS = (["ei1a", "ei1b", "ei2a", "ei2b", "eo1", "eo2", "b1", "b2", "sb1", "sb2", "b3", "cls", "g1", "g2", "g3"]
        + [f"bn_{p}_{s}" for p in "bgemv" for s in BN_STAGES + ["f1_0", "f1_1", "f1_2", "f1_3"]]
        + ["l2bq", "l2bk", "l2bv", "l2bo", "l2g", "l2b", "l3bq", "l3bk", "l3bv", "l3bo", "l3dl", "l3g", "l3b"])
COL = {name: i for i, name in enumerate(COLS)}
NBN = len(BN_STAGES) + 4

MATS = (["w1a", "w1b", "w2a", "w2b", "s1a", "s1b", "s2a", "s2b", "w3", "a0qT", "a0dT", "a0q", "a0d",
         "a1q", "a1k", "a1v", "a1p"] + [f"a1f1_{c}" for c in range(NFF1)] + [f"a1f2_{c}" for c in range(NFF1)]
        + ["a2q", "a2k", "a2v", "a2o", "a3q", "a3k", "a3v", "a3o"])
MAT = {name: i for i, name in enumerate(MATS)}
MATS_FIRST = MAT["a1q"]
ROUTE_W = [72, 8, 8, 16]
ROUTE_AT = [0, 72, 80, 88]
ROUTES = sum(ROUTE_W)


class Moe:

    def __init__(self, layer, experts, hidden, unroll, gated):
        self.layer, self.E, self.U, self.gated = layer, experts, unroll, gated
        self.cols = 3 * hidden if gated else 2 * hidden + hidden // D
        self.I = experts // unroll
        self.n0 = self.k0 = self.i0 = 0
        self.C = hidden // D
        self.F = 2 * hidden if gated else hidden
        self.S = 2 * self.C
        self.groups = max(1, experts // PARTS)

    def expert(self, i, u):
        if self.groups == 1:
            return i * self.U + u, 0, i * self.U + u
        g, r = u % self.groups, i * (self.U // self.groups) + u // self.groups
        return r + g * PARTS, g, r


MOES = [Moe(0, 64, 256, 4, False), Moe(1, 8, 256, 4, False), Moe(2, 8, 512, 4, False), Moe(3, 16, 128, 4, True)]


for _m, _next in zip(MOES, MOES[1:]):
    _next.n0, _next.k0, _next.i0 = _m.n0 + _m.E, _m.k0 + _m.E * _m.S, _m.i0 + _m.I


def tower(nc, patches, consts, sel_d, cols_d, mats_d, route_d, rows_eo, bias_rows,
          w_moe, b2_moe, out):
    ctx = ExitStack()
    with ctx:
        def sb(name, shape, dt=F32):
            return ctx.enter_context(nc.sbuf_tensor(name, shape, dt))

        def sem(name):
            return ctx.enter_context(nc.semaphore(name))

        cst = sb("cst", [D, CONST_W])

        def const(name, k=None, w=None):
            at, width = CONST_AT[name]
            if k is not None:
                at, width = at + k * w, w
            return cst[:, at:at + width]

        sel = sb("sel", [D, PARTS * D], BF16)
        col = sb("col", [D, len(COLS)])
        mats = sb("mats", [D, len(MATS), D])
        route_w = sb("route_w", [D, ROUTES])
        xp = sb("xp", [D, 2, BANK])
        eo_rows = sb("eo_rows", [D, 2, D])
        bias_bc = sb("bias_bc", [D, 32])

        h = sb("h", [D, N])
        xn = sb("xn", [D, N])
        hx = sb("hx", [D, N])
        lnv = sb("lnv", [D, N])
        sq = sb("sq", [D, N])
        rstd = sb("rstd", [D, N])
        t = [sb(f"t{i}", [D, N]) for i in range(10)]
        qm = sb("qm", [D, H, N])
        vtok = sb("vtok", [T, B, H, VW])
        vtok2 = sb("vtok2", [T, 2, H, HD])
        ea = sb("ea", [T, 2, H, T])
        eb = sb("eb", [T, 2, H, T])
        eat = sb("eat", [T, 2, H, T])
        sm = sb("sm", [T, 2, 6, H])
        ytok = sb("ytok", [T, B, D])
        ktok = ytok
        vtok1 = sb("vtok1", [T, B, D])
        kv = sb("kv", [D, B, D])
        h1 = qm[:, 0:NFF1, :]
        sums = sb("sums", [D, 8, B])
        decay = sb("decay", [D, 2, T])
        bnst = sb("bnst", [D, 3, NBN])
        bns = sb("bns", [D, NBN])
        bnb = sb("bnb", [D, NBN])
        small = sb("small", [D, 16])
        nz = sb("nz", [D, 3, 6 + 2 * D])
        g1m = sb("g1m", [D, H])

        NLMAX = NT * 72
        lg = sb("lg", [TT, NLMAX])
        r_oh = [sb(f"r_oh{i}", [TT, NLMAX]) for i in range(4)]
        r_s = sb("r_s", [TT, 8, NT * 9])
        gates = sb("gates", [TT, NT, 64])
        res = sb("res", [TT, NT, 64])
        parts = sb("parts", [TT, NT, 2, 4, PARTS], BF16)
        gT = sb("gT", [64, N])
        stack = sb("stack", [D, 2, N], BF16)
        cb = sb("cb", [D, 2, N])
        ab = sb("ab", [D, 4, HALF])
        tb = sb("tb", [D, 2, HALF])
        gb = sb("gb", [D, 4, HALF])
        vs = sb("vs", [D, 2, N])
        identb = sb("identb", [D, D], BF16)

        def eb_of(b):
            return eb[:, b % 2] if b % 4 < 2 else vs[0:T, b % 2, :].rearrange("p (h n) -> p h n", h=H)

        aff = sb("aff", [TT, NT * 16])
        rings = [sb(f"w{m.layer}_sb", [D, m.U, m.cols]) for m in (MOES[0], MOES[2])]
        w_sb = [rings[0], rings[0], rings[1], rings[1]]
        xr = sb("xr", [D, 2, N], F32R)
        wr = sb("wr", [D, 2, 2, max(m.F for m in MOES)], F32R)
        ws_sb = sb("ws_sb", [D, 384])
        b2_sb = [sb(f"b2_{m.layer}", [m.E, D]) for m in MOES[:3]]

        ps = ctx.enter_context(nc.psum_tensor("ps", [D, 8, BANK], F32))

        def psb(bank):
            return ps[:, bank, :].bitcast(BF16)

        def pair(k, rows=D):
            return ps[0:rows, 2 * k:2 * k + 2, 0:HALF]

        def two(ap):
            return ap.rearrange("p (a n) -> p a n", a=2)

        def img(ap):
            return ap.rearrange("p (b t) -> p b t", b=B)

        names = """ld_const ld_sel ld_col ld_mat0 ld_mat1 ld_route ld_patch ld_eo ld_bias ld_shared
        dve_chain
        noise_abs noise_root wn_ready emb_g emb_clamped emb_e emb_x emb_proj h_ready
        ln_centred ln_squared ln_var ln_log ln_rstd ln_out ln_post x_split pool_ready identb_ready
        a0_w a0_n a0_qa a0_max a0_inv a0_wsum a0_sq a0_ms a0_log a0_rinv a0_q a0_vF a0_vT a0_vtok a0_scores a0_ea_in a0_eb_in a0_ea a0_eb a0_eT a0_eat a0_v2
        a0_y a0_ytok a0_yT a0_yF a0_out
        bn_std bn_ready a1_qkv a1_v a1_tr a1_tok a1_kv a1_kvm a1_o a1_orelu a1_p a1_prelu a1_x1
        a1_f1 a1_h1 a1_f2 a1_y
        a2_qkv a2_in a2_prod a2_io a2_prod2 a2_hats a2_sig a2_einp a2_e a2_ks a2_qk a2_A a2_vw a2_vs a2_vse a2_t a2_acc a2_r a2_out
        a3_qkv a3_v a3_lam a3_lnlam a3_dec a3_min a3_exp a3_qk a3_vT a3_vtok a3_scores a3_att a3_y a3_ytok a3_yT a3_yF a3_out a3_z
        stored""".split()
        S = {n: sem(n) for n in names}
        rt = {n: sem(f"route_{n}") for n in ("logits", "aff", "d", "e", "parts", "gT", "ready", "shared_h", "shared_a", "shared_g")}
        RT_E = {0: 1, 2: 2, 3: 2}
        RT_T = {0: 2, 1: 4, 2: 6, 3: 7}
        RT_READY = {0: 3, 1: 5, 2: 7, 3: 8}
        moe_done = sem("moe_done")
        X = {n: sem(f"moe_{n}") for n in ("cb_done", "cb_ready", "h_ready", "a_ready", "t_ready", "g_ready", "g_used",
                                          "w_split", "w_split_hi")}

        w_loaded = [sem(f"w_loaded{u}") for u in range(4)]

        def wait(eng, s, value):
            if isinstance(value, int) and value <= 0:
                return
            eng.wait_ge(s, value)

        block = ctx.enter_context(nc.Block())

        def mat(name):
            return mats[:, MAT[name], :]

        def c_(name):
            return col[:, COL[name]:COL[name] + 1]

        @block.sync
        def _(sp):
            sp.dma_start(col[:, :], cols_d).then_inc(S["ld_col"], 16)
            sp.dma_start(eo_rows[:, :, :], rows_eo.rearrange("(o a) n -> o a n", o=1).broadcast_to([D, 2, D])).then_inc(S["ld_eo"], 16)
            sp.dma_start(mats[:, 0:MATS_FIRST, :], mats_d[:, 0:MATS_FIRST, :]).then_inc(S["ld_mat0"], 16)
            sp.dma_start(xp[:, :, :], patches).then_inc(S["ld_patch"], 16)
            sp.dma_start(cst[:, :], consts).then_inc(S["ld_const"], 16)
            sp.dma_start(route_w[:, :], route_d).then_inc(S["ld_route"], 16)
            sp.dma_start(sel[:, :], sel_d).then_inc(S["ld_sel"], 16)
            for m in range(3):
                sp.dma_start(b2_sb[m][:, :], b2_moe[m]).then_inc(S["ld_bias"], 16)
            sp.dma_start(bias_bc[:, :], bias_rows.rearrange("(o n) -> o n", o=1).broadcast_to([D, 32])).then_inc(S["ld_bias"], 16)
            sp.dma_start(mats[:, MATS_FIRST:, :], mats_d[:, MATS_FIRST:, :]).then_inc(S["ld_mat1"], 16)
            for m in MOES:
                L = m.layer

                def load(i, u):
                    e, _, _ = m.expert(i, u)
                    if m.gated:
                        e = e + 1
                    if L > 0 and isinstance(i, int) and i == 0:
                        prev = MOES[L - 1]
                        sp.wait_ge(X["g_used"], prev.k0 + (prev.E - prev.U + u + 1) * prev.S)
                    if not (isinstance(i, int) and i == 0):
                        sp.wait_ge(X["g_used"], ((i - 1) * m.U + u + 1) * m.S + m.k0)
                    src = w_moe[L][e] if isinstance(e, int) else w_moe[L][bass.ds(e, 1)].rearrange("o p n -> p (o n)")
                    sp.dma_start(w_sb[L][:, u, 0:m.cols], src).then_inc(w_loaded[u], 16)

                if m.gated:
                    sp.dma_start(ws_sb[:, :], w_moe[L][0]).then_inc(S["ld_shared"], 16)
                for u in range(m.U):
                    load(0, u)
                if m.I == 2:
                    for u in range(m.U):
                        load(1, u)
                else:
                    with sp.Fori(1, m.I) as i:
                        for u in range(m.U):
                            load(i, u)
            sp.wait_ge(S["h_ready"], 20)
            sp.dma_start(out, h[:, :]).then_inc(S["stored"], 16)
            sp.wait_ge(S["stored"], 16)

        @block.tensor
        def _(pe):
            def mm(o, lhsT, rhs, start=True, stop=True, **kw):
                return nc.tensor.matmul(o, lhsT, rhs, start=start, stop=stop, **kw)

            def full(k, lhsT, src, start=True, stop=True):
                for a in range(2):
                    last = mm(ps[:, 2 * k + a, 0:HALF], lhsT, src[:, a * HALF:(a + 1) * HALF], start, stop)
                return last

            def halves(k, lhsT, src, ready):
                for a in range(2):
                    mm(ps[:, 2 * k + a, 0:HALF], lhsT, src[:, a * HALF:(a + 1) * HALF]).then_inc(ready, 1)

            def ln(k, src):
                for a in range(2):
                    mm(ps[:, a, 0:HALF], const("centre"), src[:, a * HALF:(a + 1) * HALF]).then_inc(S["ln_centred"], 1)
                for a in range(2):
                    pe.wait_ge(S["ln_squared"], 2 * k + a + 1)
                    mm(ps[:, 2 + a, 0:HALF], const("mean"), sq[:, a * HALF:(a + 1) * HALF]).then_inc(S["ln_var"], 1)

            pe.wait_ge(S["ld_patch"], 16)
            for l in range(2):
                pe.wait_ge(S["wn_ready"], l + 1)
                for c in range(2):
                    last = mm(ps[:, l, :], t[6 + l][:, c * D:(c + 1) * D], xp[:, c, :], c == 0, c == 1)
                last.then_inc(S["emb_g"], 1)
            pe.wait_ge(S["emb_x"], 1)
            mm(ps[:, 2, :], mat("w3"), t[4][:, 0:BANK]).then_inc(S["emb_proj"], 1)

            pe.wait_ge(S["ld_const"], 16)
            pe.wait_ge(S["h_ready"], 2)
            ln(0, h)
            pe.wait_ge(S["ln_out"], 2)
            pe.wait_ge(S["a0_wsum"], 1)
            halves(2, mat("a0qT"), xn, S["a0_w"])
            for a in range(2):
                pe.wait_ge(S["a0_sq"], a + 1)
                mm(ps[:, 2 + a, 0:HALF], const("blk_mean"), sq[:, a * HALF:(a + 1) * HALF]).then_inc(S["a0_ms"], 1)

            def to_tokens(src, banks, ready):
                for b in range(B):
                    last = nc.tensor.transpose(ps[0:T, banks + b // HB, (b % HB) * D:(b % HB + 1) * D],
                                               src[:, b * T:(b + 1) * T], const("ident"))
                last.then_inc(ready, 1)

            pe.wait_ge(S["a0_vF"], 1)
            to_tokens(t[2], 0, S["a0_vT"])

            def scores_ij(b):
                wait(pe, S["a0_ea_in"], b)
                for hh in range(H):
                    last = mm(ps[0:T, hh // 4, (hh % 4) * T:(hh % 4 + 1) * T],
                              qm[:, hh, b * T:(b + 1) * T], t[1][:, b * T:(b + 1) * T])
                last.then_inc(S["a0_scores"], 1)

            def scores_ji(b, k, ready):
                for a in range(2):
                    last = mm(ps[0:T, 2 * k + a, 0:HALF].rearrange("p (h t) -> p h t", h=4), t[1][:, b * T:(b + 1) * T],
                              qm[:, 4 * a:4 * a + 4, b * T:(b + 1) * T])
                last.then_inc(ready, 1)

            def turn(b):
                pe.wait_ge(S["a0_ea"], b + 1)
                wait(pe, S["a0_eat"], b)
                for hh in range(H):
                    last = nc.tensor.transpose(ps[0:T, 4 + hh // 4, (hh % 4) * T:(hh % 4 + 1) * T],
                                               ea[:, b % 2, hh, :], const("ident")[0:T, 0:T])
                last.then_inc(S["a0_eT"], 1)

            def weigh(b):
                pe.wait_ge(S["a0_eat"], b + 1)
                wait(pe, S["a0_ytok"], b - 1)
                for hh in range(H):
                    mm(ps[0:T, 6 + b % 2, hh * VW:(hh + 1) * VW], eat[:, b % 2, hh, :], vtok[:, b, hh, :])
                pe.wait_ge(S["a0_v2"], b + 1)
                for hh in range(H):
                    last = mm(ps[0:T, 6 + b % 2, H * VW + hh * HD:H * VW + (hh + 1) * HD],
                              eb_of(b)[:, hh, :], vtok2[:, b % 2, hh, :])
                last.then_inc(S["a0_y"], 1)

            pe.wait_ge(S["a0_vtok"], 1)
            for b in range(-2, B):
                if b + 2 < B:
                    if b + 2 in (0, HB):
                        pe.wait_ge(S["a0_q"], (b + 2) // HB + 1)
                        pe.wait_ge(S["a0_qa"], (b + 2) // HB + 1)
                    scores_ij(b + 2)
                if 0 <= b + 1 < B:
                    turn(b + 1)
                if b + 2 < B:
                    wait(pe, S["a0_eb_in"], b + 2)
                    scores_ji(b + 2, 1, S["a0_scores"])
                if b >= 0:
                    weigh(b)

            def to_features(done, ready):
                for b in range(B):
                    pe.wait_ge(done, b + 1)
                    last = nc.tensor.transpose(ps[:, b // HB, (b % HB) * T:(b % HB + 1) * T], ytok[:, b, :],
                                               const("ident")[0:T, 0:T])
                last.then_inc(ready, 1)

            to_features(S["a0_ytok"], S["a0_yT"])
            pe.wait_ge(S["a0_yF"], 1)
            halves(1, mat("a0q"), t[3], S["a0_out"])

            def route(m, src, res_src):
                if m.layer == 0:
                    pe.wait_ge(S["identb_ready"], 1)
                w, at = ROUTE_W[m.layer], ROUTE_AT[m.layer]
                for k in range(NT):
                    last = mm(ps[0:TT, 0, k * w:(k + 1) * w], src[:, k * TT:(k + 1) * TT], route_w[:, at:at + w])
                last.then_inc(rt["logits"], 1)
                open_sum(m, src, res_src)
                pe.wait_ge(rt["parts"], m.layer + 1)
                for g in range(m.groups):
                    for k in range(NT):
                        last = nc.tensor.transpose(psb(4 + g)[:, k * TT:(k + 1) * TT],
                                                   parts[:, k, g, :, :].rearrange("p a b -> p (a b)"), identb[0:TT, 0:TT])
                last.then_inc(rt["gT"], 1)
                if not m.gated:
                    for k in range(NT):
                        last = nc.tensor.transpose(ps[0:m.E, 2 + k // 4, (k % 4) * TT:(k % 4 + 1) * TT],
                                                   gates[:, k, 0:m.E], const("ident")[0:TT, 0:TT])
                    last.then_inc(rt["gT"], 1)

            def experts(m, src):
                L = m.layer
                W = w_sb[L]

                def broadcast(i, u):
                    _, g, r = m.expert(i, u)
                    n = i * m.U + u + m.n0
                    wait(pe, X["cb_ready"], n)
                    for a in range(2):
                        last = mm(ps[:, 4 + a, 0:HALF], sel[:, bass.ds(r * D, D)], stack[:, g, a * HALF:(a + 1) * HALF])
                    last.then_inc(X["cb_done"], 1)

                def three_pass(o, w, c, a):
                    for n, (wh, xh) in enumerate(((0, 0), (0, 1), (1, 0))):
                        last = mm(o, wr[:, w, wh, c * D:(c + 1) * D], xr[:, xh, a * HALF:(a + 1) * HALF], n == 0, n == 2)
                    return last

                def first(i, u, s):
                    k = (i * m.U + u) * m.S + s + m.k0
                    c, a = s // 2, s % 2
                    if s == 0:
                        pe.wait_ge(X["w_split"], i * m.U + u + 1 + m.n0)
                        broadcast(i, u)
                    if m.gated:
                        wait(pe, X["a_ready"], k - 1)
                        wait(pe, X["t_ready"], k - m.k0 - 1)
                        for j in range(2):
                            last = three_pass(ps[:, 2 * a + j, 0:HALF], u % 2, j, a)
                    else:
                        wait(pe, X["a_ready"], k - 3)
                        last = three_pass(ps[:, s % 4, 0:HALF], u % 2, c, a)
                    last.then_inc(X["h_ready"], 1)

                def second(i, u, s, final):
                    k = (i * m.U + u) * m.S + s + m.k0
                    c, a = s // 2, s % 2
                    at = 2 * D if m.gated else (m.C + c) * D
                    pe.wait_ge(X["g_ready"], k + 1)
                    mm(ps[:, 6 + a, 0:HALF], W[:, u, at:at + D], gb[:, s % 4, :], False, final and m.gated).then_inc(X["g_used"], 1)

                AHEAD = 1 if m.gated else 2

                def body(i, final):
                    for u in range(m.U):
                        for s in range(m.S):
                            n = u * m.S + s + AHEAD
                            if n < m.U * m.S:
                                first(i, n // m.S, n % m.S)
                            elif not final:
                                first(i + 1, 0, n - m.U * m.S)
                            second(i, u, s, final and u == m.U - 1 and s >= m.S - 2)

                pe.wait_ge(rt["ready"], RT_READY[L])
                pe.wait_ge(S["x_split"], 2 * L + 2)
                if L == 0:
                    pe.wait_ge(S["ld_sel"], 16)
                for s in range(AHEAD):
                    first(0, 0, s)
                body(0, False)
                if m.I > 2:
                    with pe.Fori(1, m.I - 1) as i:
                        body(i, False)
                body(m.I - 1, True)
                if not m.gated:
                    if L == 0:
                        pe.wait_ge(S["ld_bias"], 4 * 16)
                    for a in range(2):
                        mm(ps[:, 6 + a, 0:HALF], b2_sb[L][:, :], gT[0:m.E, a * HALF:(a + 1) * HALF],
                           False, True).then_inc(moe_done, 1)

            def open_sum(m, src, res_src):
                full(3, const("ident"), res_src, True, False)
                if m.gated:
                    pe.wait_ge(S["ld_shared"], 16)
                    for a in range(2):
                        for j in range(2):
                            last = mm(ps[:, 2 + 2 * a + j, 0:HALF], ws_sb[:, j * D:(j + 1) * D], src[:, a * HALF:(a + 1) * HALF])
                        last.then_inc(rt["shared_h"], 1)
                    for a in range(2):
                        pe.wait_ge(rt["shared_g"], a + 1)
                        mm(ps[:, 6 + a, 0:HALF], ws_sb[:, 2 * D:3 * D], gb[:, a, :], False, False).then_inc(rt["shared_h"], 1)

            pe.wait_ge(S["h_ready"], 4)
            ln(1, h)
            pe.wait_ge(S["ln_out"], 4)
            pe.wait_ge(S["ld_route"], 16)
            route(MOES[0], xn, h)
            experts(MOES[0], xn)

            pe.wait_ge(S["h_ready"], 6)
            ln(2, h)
            pe.wait_ge(S["ln_out"], 6)
            pe.wait_ge(S["ld_mat1"], 16)
            for k, name in enumerate(("a1q", "a1k", "a1v")):
                full((0, 1, 2)[k], mat(name), xn).then_inc(S["a1_qkv"], 1)
            pe.wait_ge(S["a1_v"], 1)
            to_tokens(t[1], 0, S["a1_tr"])
            to_tokens(t[2], 2, S["a1_tr"])
            pe.wait_ge(S["a1_tok"], 2)
            for b in range(B):
                last = mm(ps[:, 4 + b // HB, (b % HB) * D:(b % HB + 1) * D], ktok[:, b, :], vtok1[:, b, :])
            last.then_inc(S["a1_kv"], 1)
            pe.wait_ge(S["a1_kvm"], 1)
            for b in range(B):
                last = mm(ps[:, b // HB, (b % HB) * T:(b % HB + 1) * T], kv[:, b, :], t[0][:, b * T:(b + 1) * T])
            last.then_inc(S["a1_o"], 1)
            pe.wait_ge(S["a1_orelu"], 1)
            full(1, mat("a1p"), t[3]).then_inc(S["a1_p"], 1)
            pe.wait_ge(S["a1_x1"], 1)
            for c in range(NFF1):
                if c == 3:
                    pe.wait_ge(S["a1_h1"], 1)
                full(c % 3, mat(f"a1f1_{c}"), t[5]).then_inc(S["a1_f1"], 1)
            for c in range(NFF1):
                pe.wait_ge(S["a1_h1"], c + 1)
                last = full(3, mat(f"a1f2_{c}"), h1[:, c, :], c == 0, c == NFF1 - 1)
            last.then_inc(S["a1_f2"], 1)

            pe.wait_ge(S["h_ready"], 8)
            ln(3, h)
            pe.wait_ge(S["ln_out"], 8)
            route(MOES[1], xn, h)
            experts(MOES[1], xn)

            pe.wait_ge(S["h_ready"], 10)
            ln(4, h)
            pe.wait_ge(S["ln_out"], 10)
            for k, name in enumerate(("a2q", "a2k", "a2v")):
                full(k, mat(name), xn).then_inc(S["a2_qkv"], 1)
            pe.wait_ge(S["a2_prod"], 1)
            full(0, const("blk_one"), t[3]).then_inc(S["a2_io"], 1)
            pe.wait_ge(S["a2_prod"], 2)
            full(1, const("blk_one"), t[4]).then_inc(S["a2_io"], 1)
            pe.wait_ge(S["a2_prod2"], 1)
            pe.wait_ge(S["a2_in"], 3)
            full(2, const("blk_one"), t[3]).then_inc(S["a2_hats"], 1)
            pe.wait_ge(S["a2_prod2"], 2)
            full(3, const("blk_one"), t[4]).then_inc(S["a2_hats"], 1)
            pe.wait_ge(S["a2_vw"], 1)
            for dlt in range(H):
                if dlt:
                    P = const("perm", dlt - 1, D)
                    pe.wait_ge(S["a2_qk"], dlt)
                    full(0, P, t[1]).then_inc(S["a2_ks"], 1)
                    wait(pe, S["a2_vse"], dlt - 1)
                    full(3, P, t[2]).then_inc(S["a2_vs"], 1)
                pe.wait_ge(S["a2_qk"], dlt + 1)
                wait(pe, S["a2_t"], dlt)
                full(1, const("blk_one"), t[3 + dlt % 2]).then_inc(S["a2_A"], 1)
            pe.wait_ge(S["a2_r"], 1)
            halves(2, mat("a2o"), t[5], S["a2_out"])

            pe.wait_ge(S["h_ready"], 12)
            ln(5, h)
            pe.wait_ge(S["ln_out"], 12)
            ln(6, xn)
            pe.wait_ge(S["ln_post"], 1)
            pe.wait_ge(S["h_ready"], 14)
            route(MOES[2], hx, h)
            experts(MOES[2], hx)

            pe.wait_ge(S["h_ready"], 16)
            ln(7, h)
            pe.wait_ge(S["ln_out"], 16)
            for k, name in enumerate(("a3q", "a3k", "a3v")):
                full(k, mat(name), xn).then_inc(S["a3_qkv"], 1)
            pe.wait_ge(S["a3_v"], 1)
            pe.wait_ge(S["a3_qk"], 1)
            to_tokens(t[2], 0, S["a3_vT"])
            pe.wait_ge(S["a3_vtok"], 1)
            scores_ji(0, 1, S["a3_scores"])
            for b in range(B):
                if b + 1 < B:
                    wait(pe, S["a3_att"], b)
                    scores_ji(b + 1, 1 + (b + 1) % 2, S["a3_scores"])
                pe.wait_ge(S["a3_att"], b + 1)
                wait(pe, S["a3_ytok"], b - 1)
                for hh in range(H):
                    last = mm(ps[0:T, 6 + b % 2, hh * VW:(hh + 1) * VW], ea[:, b % 2, hh, :], vtok[:, b, hh, :])
                last.then_inc(S["a3_y"], 1)
            to_features(S["a3_ytok"], S["a3_yT"])
            pe.wait_ge(S["a3_yF"], 1)
            full(2, mat("a3o"), t[3]).then_inc(S["a3_out"], 1)
            pe.wait_ge(S["a3_z"], 1)
            ln(8, t[4])

            pe.wait_ge(S["h_ready"], 18)
            ln(9, h)
            pe.wait_ge(S["ln_out"], 20)
            route(MOES[3], xn, h)
            experts(MOES[3], xn)


        @block.scalar
        def _(act):
            def fn(o, i, f, **kw):
                return nc.scalar.activation(o, i, f, **kw)

            eps_ln = const("eps")[:, 0:1]
            eps_rms = const("eps")[:, 1:2]

            def half(ap, a):
                return ap[:, a * HALF:(a + 1) * HALF]

            def ln(k):
                for a in range(2):
                    act.wait_ge(S["ln_centred"], 2 * k + a + 1)
                    fn(half(sq, a), ps[:, a, 0:HALF], ACT.Square).then_inc(S["ln_squared"], 1)
                for a in range(2):
                    act.wait_ge(S["ln_var"], 2 * k + a + 1)
                    fn(half(lnv, a), ps[:, 2 + a, 0:HALF], ACT.Ln, bias=eps_ln).then_inc(S["ln_log"], 1)
                for a in range(2):
                    act.wait_ge(S["ln_log"], 2 * k + a + 1)
                    fn(half(rstd, a), half(lnv, a), ACT.Exp, scale=-0.5).then_inc(S["ln_rstd"], 1)

            act.wait_ge(S["ld_col"], 16)
            act.wait_ge(S["ld_eo"], 16)
            e6, erow = col[:, 0:6], eo_rows[:, :, :].rearrange("p a n -> p (a n)")
            fn(nz[:, 0, 0:6], e6, ACT.Abs)
            fn(nz[:, 0, 6:], erow, ACT.Abs).then_inc(S["noise_abs"], 1)
            fn(nz[:, 2, 0:6], e6, ACT.Sign)
            fn(nz[:, 2, 6:], erow, ACT.Sign)
            act.wait_ge(S["noise_abs"], 1)
            fn(nz[:, 1, :], nz[:, 0, :], ACT.Sqrt).then_inc(S["noise_root"], 1)
            act.wait_ge(S["ld_const"], 16)
            fn(bnst[:, 0, :], col[:, COL["bn_v_q"]:COL["bn_v_q"] + NBN], ACT.Sqrt, bias=eps_ln).then_inc(S["bn_std"], 1)
            nc.scalar.preload_act_table_set("natural_log_exp_and_others")
            act.wait_ge(S["emb_clamped"], 1)
            fn(t[2][:, 0:BANK], t[0][:, 0:BANK], ACT.Exp).then_inc(S["emb_e"], 1)
            fn(small[:, 4:5], c_("l3dl"), ACT.Exp, scale=-1.0).then_inc(S["a3_lam"], 1)
            act.wait_ge(S["a3_lnlam"], 1)
            fn(small[:, 6:7], small[:, 5:6], ACT.Ln).then_inc(S["a3_lam"], 1)
            act.wait_ge(S["a3_lnlam"], 2)
            fn(decay[:, 0, :], const("index"), ACT.Exp, scale=small[:, 6:7])
            fn(decay[:, 1, :], const("index"), ACT.Exp, scale=small[:, 7:8]).then_inc(S["a3_dec"], 1)

            ln(0)
            for a in range(2):
                act.wait_ge(S["a0_w"], a + 1)
                fn(half(sq, a), ps[:, 4 + a, 0:HALF], ACT.Square).then_inc(S["a0_sq"], 1)
            for a in range(2):
                act.wait_ge(S["a0_ms"], a + 1)
                fn(half(lnv, a), ps[:, 2 + a, 0:HALF], ACT.Ln, bias=eps_rms).then_inc(S["a0_log"], 1)
            for a in range(2):
                act.wait_ge(S["a0_log"], a + 1)
                fn(half(rstd, a), half(lnv, a), ACT.Exp, scale=-0.5).then_inc(S["a0_rinv"], 1)
            act.wait_ge(S["a0_n"], 1)
            fn(t[2][:, :], t[0][:, :], ACT.Identity, scale=c_("g3")).then_inc(S["a0_vF"], 1)
            for a in range(2):
                for hh in range(H // 2, H):
                    last = fn(half(qm[:, hh, :], a), half(t[0], a), ACT.Identity, scale=g1m[:, hh:hh + 1])
                last.then_inc(S["a0_qa"], 1)
            for b in range(-1, B):
                if 0 <= b:
                    act.wait_ge(S["a0_eT"], b + 1)
                    wait(act, S["a0_y"], b - 1)
                    fn(eat[:, b % 2].rearrange("p (a h) n -> p a (h n)", a=2), pair(2, T), ACT.Copy).then_inc(S["a0_eat"], 1)
                if b + 1 < B:
                    act.wait_ge(S["a0_ea_in"], b + 2)
                    fn(ea[:, (b + 1) % 2], ea[:, (b + 1) % 2], ACT.Exp).then_inc(S["a0_ea"], 1)
                    act.wait_ge(S["a0_eb_in"], b + 2)
                    fn(eb_of(b + 1), eb_of(b + 1), ACT.Exp).then_inc(S["a0_eb"], 1)
            act.wait_ge(S["a0_yT"], 1)
            fn(two(t[3][:, :]), pair(0), ACT.Copy).then_inc(S["a0_yF"], 1)

            def route(m):
                R = rt
                if m.gated:
                    act.wait_ge(R["logits"], m.layer + 1)
                    fn(aff[:, :], ps[0:TT, 0, 0:NT * m.E], ACT.Sigmoid).then_inc(R["aff"], 1)
                    nc.scalar.preload_act_table_set("silu_and_others")
                    for a in range(2):
                        act.wait_ge(R["shared_h"], a + 1)
                        fn(ab[:, a, :], ps[:, 2 + 2 * a, 0:HALF], ACT.Silu).then_inc(R["shared_a"], 1)
                    return
                if m.layer != 1:
                    act.wait_ge(R["d"], RT_E[m.layer])
                    n = NT * 9 if m.layer == 0 else NT
                    fn(r_s[:, 4, 0:n], r_s[:, 3, 0:n], ACT.Exp).then_inc(R["e"], 1)
                act.wait_ge(R["gT"], RT_T[m.layer])
                fn(gT[0:m.E, 0:4 * TT], ps[0:m.E, 2, 0:4 * TT], ACT.Copy)
                fn(gT[0:m.E, 4 * TT:N], ps[0:m.E, 3, 0:N - 4 * TT], ACT.Copy).then_inc(R["ready"], 1)

            def experts(m, func):
                L = m.layer

                def body(i):
                    for u in range(m.U):
                        n = i * m.U + u
                        act.wait_ge(X["cb_done"], n + 1 + m.n0)
                        if not (isinstance(n, int) and n < 2):
                            act.wait_ge(X["g_ready"], (n - 1) * m.S + m.k0)
                        fn(two(cb[:, u % 2, :]), pair(2), ACT.Copy).then_inc(X["cb_ready"], 1)
                        for s in range(m.S):
                            k = n * m.S + s + m.k0
                            act.wait_ge(X["h_ready"], k + 1)
                            wait(act, X["g_ready"], k - 3)
                            if m.gated:
                                fn(ab[:, s, :], ps[:, 2 * s, 0:HALF], func).then_inc(X["a_ready"], 1)
                            else:
                                at = 2 * m.C * D + s // 2
                                bias = w_sb[L][:, u, at:at + 1]
                                fn(ab[:, s % 4, :], ps[:, s % 4, 0:HALF], func, bias=bias).then_inc(X["a_ready"], 1)

                body(0)
                if m.I > 2:
                    with act.Fori(1, m.I - 1) as i:
                        body(i)
                body(m.I - 1)

            ln(1)
            route(MOES[0])
            experts(MOES[0], ACT.Relu)

            def bn(o, i, k):
                return fn(o, i, ACT.Relu, scale=bns[:, k:k + 1], bias=bnb[:, k:k + 1])

            ln(2)
            act.wait_ge(S["bn_ready"], 1)
            for k in range(3):
                act.wait_ge(S["a1_qkv"], k + 1)
                last = bn(two(t[k][:, :]), pair(k), k)
            last.then_inc(S["a1_v"], 1)
            act.wait_ge(S["a1_tr"], 2)
            fn(vtok1[:, :, :].rearrange("p (a b) n -> p a (b n)", a=2), ps[0:T, 2:4, :], ACT.Copy).then_inc(S["a1_tok"], 1)
            act.wait_ge(S["a1_o"], 1)
            fn(two(t[3][:, :]), pair(0), ACT.Relu).then_inc(S["a1_orelu"], 1)
            act.wait_ge(S["a1_p"], 1)
            bn(two(t[4][:, :]), pair(1), 3).then_inc(S["a1_prelu"], 1)
            for c in range(NFF1):
                act.wait_ge(S["a1_f1"], c + 1)
                bn(two(h1[:, c, :]), pair(c % 3), 5 + c).then_inc(S["a1_h1"], 1)
            act.wait_ge(S["a1_f2"], 1)
            bn(two(t[6][:, :]), pair(3), 4).then_inc(S["a1_y"], 1)

            ln(3)
            route(MOES[1])
            experts(MOES[1], ACT.Relu)

            ln(4)
            nc.scalar.preload_act_table_set("sigmoid_and_others")
            act.wait_ge(S["a2_qkv"], 1)
            fn(two(t[0][:, :]), pair(0), ACT.Sigmoid, bias=c_("l2bq")).then_inc(S["a2_in"], 1)
            act.wait_ge(S["a2_qkv"], 2)
            fn(two(t[1][:, :]), pair(1), ACT.Sigmoid, bias=c_("l2bk")).then_inc(S["a2_in"], 1)
            act.wait_ge(S["a2_qkv"], 3)
            fn(two(t[2][:, :]), pair(2), ACT.Identity, bias=c_("l2bv")).then_inc(S["a2_in"], 1)
            act.wait_ge(S["a2_hats"], 1)
            fn(two(t[9][:, :]), pair(2), ACT.Sigmoid).then_inc(S["a2_sig"], 1)
            nc.scalar.preload_act_table_set("natural_log_exp_and_others")
            act.wait_ge(S["a2_einp"], 1)
            fn(t[6][:, :], t[6][:, :], ACT.Exp).then_inc(S["a2_e"], 1)
            for d in range(1, H):
                act.wait_ge(S["a2_vs"], d)
                wait(act, S["a2_t"], d - 1)
                fn(two(vs[:, d % 2, :]), pair(3), ACT.Copy).then_inc(S["a2_vse"], 1)

            ln(5)
            ln(6)
            route(MOES[2])
            nc.scalar.preload_act_table_set("gelu_and_others")
            experts(MOES[2], ACT.Gelu)
            nc.scalar.preload_act_table_set("natural_log_exp_and_others")

            ln(7)
            act.wait_ge(S["a3_qkv"], 3)
            fn(two(t[2][:, :]), pair(2), ACT.Identity, bias=c_("l3bv")).then_inc(S["a3_v"], 1)
            for k in range(2):
                act.wait_ge(S["a3_min"], k + 1)
                fn(t[k][:, :], t[k][:, :], ACT.Exp).then_inc(S["a3_exp"], 1)
            act.wait_ge(S["a3_yT"], 1)
            fn(two(t[3][:, :]), pair(0), ACT.Copy).then_inc(S["a3_yF"], 1)
            act.wait_ge(S["a3_out"], 1)
            fn(two(t[4][:, :]), pair(2), ACT.Identity, bias=c_("l3bo")).then_inc(S["a3_z"], 1)
            ln(8)
            ln(9)
            nc.scalar.preload_act_table_set("sigmoid_and_others")
            route(MOES[3])
            experts(MOES[3], ACT.Silu)

        @block.vector
        def _(dve):
            V = nc.vector
            chain = [0]

            def link(ins):
                chain[0] += 1
                ins.then_inc(S["dve_chain"], 1)
                dve.wait_ge(S["dve_chain"], chain[0])

            def bc(ap, *shape):
                return ap.broadcast_to(list(shape))

            def half(ap, a):
                return ap[:, a * HALF:(a + 1) * HALF]

            def per_img(cols_):
                return bc(cols_.unsqueeze(2), D, B, T)

            def pair4(k, rows=D):
                return ps[0:rows, 2 * k:2 * k + 2, 0:HALF].rearrange("p a (b t) -> p a b t", b=HB)

            def img4(ap):
                return ap.rearrange("p (a b t) -> p a b t", a=2, b=HB)

            def ln(k, o=None):
                for a in range(2):
                    dve.wait_ge(S["ln_rstd"], 2 * k + a + 1)
                    V.tensor_tensor((xn if o is None else o)[:, a * HALF:(a + 1) * HALF], ps[:, a, 0:HALF],
                                    rstd[:, a * HALF:(a + 1) * HALF], ALU.mult).then_inc(S["ln_out"], 1)

            dve.wait_ge(S["noise_root"], 1)
            link(V.tensor_tensor(nz[:, 0, :], nz[:, 1, :], nz[:, 2, :], ALU.mult))
            dve.wait_ge(S["ld_mat0"], 16)
            for l in range(2):
                row = nz[:, 0, 6 + l * D:6 + (l + 1) * D]
                tmp = t[8][:, 0:2 * D].rearrange("p (c n) -> p c n", c=2)
                link(V.tensor_tensor(tmp, mats[:, 4 + 2 * l:6 + 2 * l, :], bc(row.unsqueeze(1), D, 2, D), ALU.mult))
                for c in range(2):
                    last = V.scalar_tensor_tensor(t[6 + l][:, c * D:(c + 1) * D], t[8][:, c * D:(c + 1) * D],
                                                  nz[:, 0, 2 * l + c:2 * l + c + 1], mats[:, 2 * l + c, :], ALU.mult, ALU.add)
                last.then_inc(S["wn_ready"], 1)
                dve.wait_ge(S["wn_ready"], l + 1)
            for l in range(2):
                link(V.scalar_tensor_tensor(small[:, l:l + 1], c_(f"sb{l + 1}"), nz[:, 0, 4 + l:5 + l], c_(f"b{l + 1}"),
                                            ALU.mult, ALU.add))
            E_ = slice(0, BANK)
            dve.wait_ge(S["emb_g"], 1)
            V.tensor_scalar(t[0][:, E_], ps[:, 0, :], small[:, 0:1], 20.0, ALU.add, ALU.min).then_inc(S["emb_clamped"], 1)
            V.tensor_scalar(t[1][:, E_], ps[:, 0, :], small[:, 0:1], None, ALU.add)
            dve.wait_ge(S["emb_e"], 1)
            link(V.scalar_tensor_tensor(t[3][:, E_], t[2][:, E_], 2.0, t[2][:, E_], ALU.add, ALU.mult))
            link(V.tensor_scalar(t[5][:, E_], t[3][:, E_], 2.0, None, ALU.add))
            link(V.reciprocal(t[5][:, E_], t[5][:, E_]))
            link(V.tensor_tensor(t[3][:, E_], t[3][:, E_], t[5][:, E_], ALU.mult))
            link(V.tensor_tensor(t[3][:, E_], t[3][:, E_], t[1][:, E_], ALU.mult))
            dve.wait_ge(S["emb_g"], 2)
            V.scalar_tensor_tensor(t[4][:, E_], ps[:, 1, :], small[:, 1:2], t[3][:, E_], ALU.add, ALU.mult).then_inc(S["emb_x"], 1)
            V.tensor_copy(img(h[:, :])[:, :, 0:1], bc(c_("cls").unsqueeze(2), D, B, 1))
            dve.wait_ge(S["emb_proj"], 1)
            dve.wait_ge(S["ld_const"], 16)
            V.scalar_tensor_tensor(img(h[:, :])[:, :, 1:T], ps[:, 2, :].rearrange("p (b t) -> p b t", b=B), c_("b3"),
                                   bc(const("pos").unsqueeze(1), D, B, NPATCH), ALU.add, ALU.add).then_inc(S["h_ready"], 2)

            V.tensor_tensor(mat("a0qT"), mat("a0qT"), mat("a0dT"), ALU.add)
            V.tensor_tensor(mat("a0q"), mat("a0q"), mat("a0d"), ALU.add).then_inc(S["a0_wsum"], 1)
            link(V.tensor_scalar(g1m[:, :], const("headmask"), c_("g1"), 1.0 / HD ** 0.5, ALU.mult, ALU.mult))
            V.tensor_copy(identb[:, :], const("ident")).then_inc(S["identb_ready"], 1)
            dve.wait_ge(S["a3_lam"], 1)
            link(V.tensor_scalar(small[:, 4:5], small[:, 4:5], 1.0, None, ALU.add))
            link(V.reciprocal(small[:, 4:5], small[:, 4:5]))
            V.tensor_scalar(small[:, 5:6], small[:, 4:5], 0.01, 0.99, ALU.mult, ALU.add).then_inc(S["a3_lnlam"], 1)
            dve.wait_ge(S["a3_lam"], 2)
            V.tensor_scalar(small[:, 7:8], small[:, 6:7], -1.0, None, ALU.mult).then_inc(S["a3_lnlam"], 1)
            dve.wait_ge(S["a3_dec"], 1)
            link(V.tensor_scalar(decay[:, 0, :], decay[:, 0, :], 1.0 / HD ** 0.5, None, ALU.mult))
            dve.wait_ge(S["bn_std"], 1)

            def bncols(p):
                return col[:, COL[f"bn_{p}_q"]:COL[f"bn_{p}_q"] + NBN]

            link(V.reciprocal(bnst[:, 1, :], bnst[:, 0, :]))
            link(V.tensor_tensor(bns[:, :], bncols("g"), bnst[:, 1, :], ALU.mult))
            link(V.tensor_tensor(bnst[:, 2, :], bncols("b"), bncols("m"), ALU.subtract))
            link(V.tensor_tensor(bnst[:, 2, :], bnst[:, 2, :], bns[:, :], ALU.mult))
            V.tensor_tensor(bnb[:, :], bnst[:, 2, :], bncols("e"), ALU.add).then_inc(S["bn_ready"], 1)

            ln(0)
            for a in range(2):
                dve.wait_ge(S["a0_rinv"], a + 1)
                last = V.tensor_tensor(half(t[0], a), ps[:, 4 + a, 0:HALF], half(rstd, a), ALU.mult)
            last.then_inc(S["a0_n"], 1)
            dve.wait_ge(S["a0_n"], 1)
            for a in range(2):
                V.tensor_scalar(half(t[1], a), half(t[0], a), c_("g2"), None, ALU.mult)
                for hh in range(H // 2):
                    last = V.tensor_scalar(half(qm[:, hh, :], a), half(t[0], a), g1m[:, hh:hh + 1], None, ALU.mult)
                last.then_inc(S["a0_q"], 1)

            def value_rows(ready, done):
                dve.wait_ge(ready, 1)
                for a in range(2):
                    last = V.tensor_copy(vtok[:, a * HB:(a + 1) * HB, :, 0:HD].rearrange("p b h d -> p (b h) d"),
                                         ps[0:T, a, :].rearrange("p (n d) -> p n d", d=HD))
                last.then_inc(done, 1)

            dve.wait_ge(S["pool_ready"], 1)
            value_rows(S["a0_vT"], S["a0_vtok"])

            def shift(b, pk, j, dst, done, between):
                stat = sm[:, b % 2, j, :].rearrange("p (a h) -> p a h", a=2)
                V.tensor_reduce(stat, pair4(pk, T), AX, ALU.max).then_inc(S["a0_max"], 1)
                between()
                dve.wait_ge(S["a0_max"], 2 * b + j + 1)
                V.tensor_tensor(dst.rearrange("p (a h) n -> p a h n", a=2), pair4(pk, T),
                                bc(stat.unsqueeze(3), T, 2, HB, T), ALU.subtract).then_inc(done, 1)

            def inverse_sums(b):
                if 0 <= b < B:
                    dve.wait_ge(S["a0_eb"], b + 1)
                    link(V.tensor_reduce(sm[:, b % 2, 2, :], eb_of(b), AX, ALU.add))
                    V.reciprocal(sm[:, b % 2, 3, :], sm[:, b % 2, 2, :]).then_inc(S["a0_inv"], 1)

            def y_rows(b, eps, extra, ready, done):
                dve.wait_ge(ready, b + 1)
                rows = ps[0:T, 6 + b % 2, 0:H * VW].rearrange("p (h d) -> p h d", h=H)
                den = rows[:, :, HD:VW]
                r = sm[:, b % 2, 4, :]
                yb = ytok[:, b, :].rearrange("p (h d) -> p h d", h=H)
                if eps:
                    link(V.tensor_scalar(sm[:, b % 2, 5, :].unsqueeze(2), den, eps, None, ALU.add))
                    den = sm[:, b % 2, 5, :].unsqueeze(2)
                link(V.reciprocal(r.unsqueeze(2), den))
                last = V.tensor_tensor(yb, rows[:, :, 0:HD], bc(r.unsqueeze(2), T, H, HD), ALU.mult)
                if extra:
                    link(last)
                    last = V.tensor_tensor(ytok[:, b, :], ytok[:, b, :], ps[0:T, 6 + b % 2, H * VW:H * VW + D], ALU.add)
                last.then_inc(done, 1)

            for b in range(-2, B + 1):
                if b + 2 < B:
                    dve.wait_ge(S["a0_scores"], 2 * (b + 2) + 1)
                    wait(dve, S["a0_eT"], b + 1)
                    shift(b + 2, 0, 0, ea[:, b % 2], S["a0_ea_in"], lambda: None)
                if b >= 1:
                    y_rows(b - 1, 0, True, S["a0_y"], S["a0_ytok"])
                if b + 2 < B:
                    dve.wait_ge(S["a0_scores"], 2 * (b + 2) + 2)
                    wait(dve, S["a0_y"], b - 1)
                    shift(b + 2, 1, 1, eb_of(b + 2), S["a0_eb_in"], lambda: inverse_sums(b + 1))
                else:
                    inverse_sums(b + 1)
            for a in range(2):
                dve.wait_ge(S["a0_out"], a + 1)
                V.tensor_tensor(half(h, a), half(h, a), ps[:, 2 + a, 0:HALF], ALU.add).then_inc(S["h_ready"], 1)

            def split_x(src, L):
                dve.wait_ge(*{0: (S["ln_out"], 4), 1: (S["ln_out"], 8), 2: (S["ln_post"], 1), 3: (S["ln_out"], 20)}[L])
                V.tensor_copy(xr[:, 0, :], src[:, :]).then_inc(S["x_split"], 1)
                dve.wait_ge(S["x_split"], 2 * L + 1)
                V.tensor_tensor(xr[:, 1, :], src[:, :], xr[:, 0, :].bitcast(F32), ALU.subtract).then_inc(S["x_split"], 1)

            def route(m):
                R, E = rt, min(m.E, 8) if m.layer == 0 else m.E
                rows = NT * (9 if m.layer == 0 else 1)
                n = rows * E
                flat = lg[:, 0:n]
                logits = ps[0:TT, 0, 0:n]
                if m.gated:
                    dve.wait_ge(R["aff"], 1)
                    logits = aff[:, :]
                else:
                    dve.wait_ge(R["logits"], m.layer + 1)
                if m.layer == 0:
                    link(V.tensor_copy(flat, logits))
                else:
                    if m.layer == 1:
                        dve.wait_ge(S["ld_bias"], 4 * 16)
                    at = {1: 0, 2: 8, 3: 16}[m.layer]
                    link(V.tensor_tensor(flat.rearrange("p (r e) -> p r e", e=E), logits.rearrange("p (r e) -> p r e", e=E),
                                         bc(bias_bc[0:TT, at:at + E].unsqueeze(1), TT, rows, E), ALU.add))

                def re(ap):
                    return ap[:, 0:n].rearrange("p (r e) -> p r e", e=E)

                def along(stat):
                    return bc(stat.unsqueeze(2), TT, rows, E)

                if m.gated:
                    for a in range(2):
                        dve.wait_ge(R["shared_a"], a + 1)
                        V.tensor_tensor(gb[:, a, :], ab[:, a, :], ps[:, 3 + 2 * a, 0:HALF], ALU.mult).then_inc(R["shared_g"], 1)

                top = {0: 2, 1: 1, 2: 2, 3: 3}[m.layer]
                rev = bc(const("rev")[0:TT, 0:E].unsqueeze(1), TT, rows, E)
                for j in range(top):
                    mx, rk, oh = r_s[:, j, 0:rows], r_s[:, 6, 0:rows], r_oh[j]
                    link(V.tensor_reduce(mx, re(lg), AX, ALU.max))
                    link(V.tensor_tensor(re(r_oh[3]), re(lg), along(mx), ALU.is_equal))
                    link(V.tensor_tensor(re(r_oh[3]), re(r_oh[3]), rev, ALU.mult))
                    link(V.tensor_reduce(rk, re(r_oh[3]), AX, ALU.max))
                    link(V.tensor_tensor(re(oh), re(r_oh[3]), along(rk), ALU.is_equal))
                    if j + 1 < top:
                        link(V.scalar_tensor_tensor(flat, oh[:, 0:n], -1e30, flat, ALU.mult, ALU.add))
                if m.layer in (0, 2):
                    V.tensor_tensor(r_s[:, 3, 0:rows], r_s[:, 1, 0:rows], r_s[:, 0, 0:rows], ALU.subtract).then_inc(R["d"], 1)
                    dve.wait_ge(R["e"], RT_E[m.layer])
                    link(V.tensor_scalar(r_s[:, 5, 0:rows], r_s[:, 4, 0:rows], 1.0, None, ALU.add))
                    link(V.reciprocal(r_s[:, 5, 0:rows], r_s[:, 5, 0:rows]))
                    link(V.tensor_tensor(r_s[:, 7, 0:rows], r_s[:, 4, 0:rows], r_s[:, 5, 0:rows], ALU.mult))
                    link(V.tensor_tensor(re(r_oh[0]), re(r_oh[0]), along(r_s[:, 5, 0:rows]), ALU.mult))
                    link(V.tensor_tensor(re(r_oh[1]), re(r_oh[1]), along(r_s[:, 7, 0:rows]), ALU.mult))
                    if m.layer == 2:
                        link(V.tensor_tensor(gates[:, :, 0:E], re(r_oh[0]), re(r_oh[1]), ALU.add))
                    else:
                        link(V.tensor_tensor(re(r_oh[3]), re(r_oh[0]), re(r_oh[1]), ALU.add))
                        g4 = r_oh[3][:, 0:n].rearrange("p (k r e) -> p k r e", k=NT, e=8)
                        for k in range(NT):
                            last = V.tensor_tensor(gates[:, k, :].rearrange("p (g e) -> p g e", g=8), g4[:, k, 1:9, :],
                                                   bc(g4[:, k, 0, :].unsqueeze(2), TT, 8, 8), ALU.mult)
                        link(last)
                elif m.layer == 1:
                    link(V.tensor_copy(gates[:, :, 0:E], re(r_oh[0])))
                else:
                    link(V.tensor_tensor(re(r_oh[0]), re(r_oh[0]), re(r_oh[1]), ALU.add))
                    link(V.tensor_tensor(re(r_oh[0]), re(r_oh[0]), re(r_oh[2]), ALU.add))
                    link(V.tensor_tensor(re(r_oh[0]), re(r_oh[0]), re(aff), ALU.mult))
                    link(V.tensor_reduce(r_s[:, 3, 0:rows], re(r_oh[0]), AX, ALU.add))
                    link(V.tensor_scalar(r_s[:, 3, 0:rows], r_s[:, 3, 0:rows], 1e-9, None, ALU.add))
                    link(V.reciprocal(r_s[:, 4, 0:rows], r_s[:, 3, 0:rows]))
                    link(V.tensor_tensor(gates[:, :, 0:E], re(r_oh[0]), along(r_s[:, 4, 0:rows]), ALU.mult))
                w = min(m.E, PARTS)
                for g in range(m.groups):
                    src, r = gates[:, :, g * PARTS:g * PARTS + w], res[:, :, g * PARTS:g * PARTS + w]
                    for j in range(3):
                        cpy = V.tensor_copy(parts[:, :, g, j, 0:w], src if j == 0 else r)
                        if j < 2:
                            link(cpy)
                            link(V.tensor_tensor(r, src if j == 0 else r, parts[:, :, g, j, 0:w], ALU.subtract))
                cpy.then_inc(R["parts"], 1)
                dve.wait_ge(R["gT"], RT_T[m.layer])
                for g in range(m.groups):
                    V.tensor_copy(stack[:, g, :], psb(4 + g)[:, 0:N]).then_inc(R["ready"], 1)

            def experts(m):
                L = m.layer

                def split(i, u):
                    n = i * m.U + u
                    w, hi, lo = w_sb[L][:, u, 0:m.F], wr[:, u % 2, 0, 0:m.F], wr[:, u % 2, 1, 0:m.F]
                    dve.wait_ge(w_loaded[u], (i + 1 + m.i0) * 16)
                    if not (isinstance(n, int) and n < 2):
                        dve.wait_ge(X["h_ready"], (n - 1) * m.S + m.k0)
                    V.tensor_copy(hi, w).then_inc(X["w_split_hi"], 1)
                    dve.wait_ge(X["w_split_hi"], n + 1 + m.n0)
                    V.tensor_tensor(lo, w, hi.bitcast(F32), ALU.subtract).then_inc(X["w_split"], 1)

                def body(i, final):
                    for u in range(m.U):
                        n = i * m.U + u
                        for s in range(m.S):
                            k = n * m.S + s + m.k0
                            if s == 1 and u + 1 < m.U:
                                split(i, u + 1)
                            elif s == 1 and not final:
                                split(i + 1, 0)
                            a = s % 2
                            cb_a = cb[:, u % 2, a * HALF:(a + 1) * HALF]
                            if s == 0:
                                dve.wait_ge(X["cb_ready"], n + 1 + m.n0)
                            if m.gated:
                                dve.wait_ge(X["h_ready"], k + 1)
                                wait(dve, X["g_ready"], k - 1)
                                V.tensor_tensor(tb[:, s, :], cb_a, ps[:, 2 * s + 1, 0:HALF], ALU.mult).then_inc(X["t_ready"], 1)
                                dve.wait_ge(X["t_ready"], k - m.k0 + 1)
                            dve.wait_ge(X["a_ready"], k + 1)
                            wait(dve, X["g_used"], k - 3)
                            V.tensor_tensor(gb[:, s % 4, :], ab[:, s % 4, :], tb[:, s, :] if m.gated else cb_a,
                                            ALU.mult).then_inc(X["g_ready"], 1)

                split(0, 0)
                body(0, False)
                if m.I > 2:
                    with dve.Fori(1, m.I - 1) as i:
                        body(i, False)
                body(m.I - 1, True)
                for a in range(2):
                    if m.gated:
                        dve.wait_ge(X["g_used"], m.k0 + m.E * m.S - 1 + a)
                    else:
                        dve.wait_ge(moe_done, 2 * L + a + 1)
                    V.tensor_copy(half(h, a), ps[:, 6 + a, 0:HALF]).then_inc(S["h_ready"], 1)

            ln(1)
            split_x(xn, 0)
            route(MOES[0])
            experts(MOES[0])

            ln(2)
            dve.wait_ge(S["a1_tr"], 1)
            V.tensor_copy(ktok[:, :, :].rearrange("p (a b) n -> p a (b n)", a=2), ps[0:T, 0:2, :]).then_inc(S["a1_tok"], 1)
            dve.wait_ge(S["a1_kv"], 1)
            V.tensor_tensor(kv[:, :, :], ps[:, 4:6, :].rearrange("p a (b n) -> p (a b) n", n=D),
                            bc(const("blk_kv").unsqueeze(1), D, B, D), ALU.mult).then_inc(S["a1_kvm"], 1)
            dve.wait_ge(S["a1_prelu"], 1)
            V.tensor_tensor(t[5][:, :], xn[:, :], t[4][:, :], ALU.add).then_inc(S["a1_x1"], 1)
            dve.wait_ge(S["a1_x1"], 1)
            link(V.tensor_tensor(h[:, :], h[:, :], t[5][:, :], ALU.add))
            dve.wait_ge(S["a1_y"], 1)
            V.tensor_tensor(h[:, :], h[:, :], t[6][:, :], ALU.add).then_inc(S["h_ready"], 2)

            ln(3)
            split_x(xn, 1)
            route(MOES[1])
            experts(MOES[1])

            ln(4)
            q, k_, v = t[0], t[1], t[2]
            dve.wait_ge(S["a2_in"], 1)
            link(V.tensor_reduce(sums[:, 0, :], img(q[:, :]), AX, ALU.add))
            dve.wait_ge(S["a2_in"], 2)
            link(V.tensor_reduce(sums[:, 1, :], img(k_[:, :]), AX, ALU.add))
            V.tensor_tensor(img(t[3][:, :]), img(q[:, :]), per_img(sums[:, 1, :]), ALU.mult).then_inc(S["a2_prod"], 1)
            V.tensor_tensor(img(t[4][:, :]), img(k_[:, :]), per_img(sums[:, 0, :]), ALU.mult).then_inc(S["a2_prod"], 1)
            dve.wait_ge(S["a2_io"], 1)
            link(V.reciprocal(two(t[5][:, :]), pair(0)))
            dve.wait_ge(S["a2_io"], 2)
            link(V.reciprocal(two(t[6][:, :]), pair(1)))
            link(V.tensor_tensor(t[7][:, :], k_[:, :], t[6][:, :], ALU.mult))
            link(V.tensor_reduce(sums[:, 2, :], img(t[7][:, :]), AX, ALU.add))
            V.tensor_tensor(img(t[3][:, :]), img(q[:, :]), per_img(sums[:, 2, :]), ALU.mult).then_inc(S["a2_prod2"], 1)
            link(V.tensor_tensor(t[8][:, :], q[:, :], t[5][:, :], ALU.mult))
            link(V.tensor_reduce(sums[:, 3, :], img(t[8][:, :]), AX, ALU.add))
            V.tensor_tensor(img(t[4][:, :]), img(k_[:, :]), per_img(sums[:, 3, :]), ALU.mult).then_inc(S["a2_prod2"], 1)
            dve.wait_ge(S["a2_hats"], 2)
            link(V.tensor_reduce(sums[:, 4, :].rearrange("p (a b) -> p a b", a=2), pair4(3), AX, ALU.max))
            V.tensor_tensor(img4(t[6][:, :]), pair4(3),
                            bc(sums[:, 4, :].rearrange("p (a b) -> p a b", a=2).unsqueeze(3), D, 2, HB, T),
                            ALU.subtract).then_inc(S["a2_einp"], 1)
            dve.wait_ge(S["a2_sig"], 1)
            link(V.tensor_tensor(t[9][:, :], t[9][:, :], t[5][:, :], ALU.mult))
            V.tensor_tensor(t[3][:, :], q[:, :], k_[:, :], ALU.mult).then_inc(S["a2_qk"], 1)
            dve.wait_ge(S["a2_e"], 1)
            link(V.tensor_reduce(sums[:, 5, :], img(t[6][:, :]), AX, ALU.add))
            link(V.reciprocal(sums[:, 6, :], sums[:, 5, :]))
            link(V.tensor_tensor(v[:, :], v[:, :], t[6][:, :], ALU.mult))
            V.tensor_tensor(img(v[:, :]), img(v[:, :]), per_img(sums[:, 6, :]), ALU.mult).then_inc(S["a2_vw"], 1)
            dve.wait_ge(S["a2_vw"], 1)
            for d in range(H):
                if d + 1 < H:
                    dve.wait_ge(S["a2_ks"], d + 1)
                    wait(dve, S["a2_A"], d)
                    V.tensor_tensor(two(t[3 + (d + 1) % 2][:, :]), two(q[:, :]), pair(0), ALU.mult).then_inc(S["a2_qk"], 1)
                dve.wait_ge(S["a2_A"], d + 1)
                if d == 0:
                    V.tensor_tensor(two(t[5][:, :]), two(v[:, :]), pair(1), ALU.mult).then_inc(S["a2_t"], 1)
                else:
                    dve.wait_ge(S["a2_vse"], d)
                    wait(dve, S["a2_acc"], d - 2)
                    V.tensor_tensor(two(t[7 + d % 2][:, :]), two(vs[:, d % 2, :]), pair(1), ALU.mult).then_inc(S["a2_t"], 1)
            dve.wait_ge(S["a2_acc"], H - 1)
            V.tensor_tensor(t[5][:, :], t[5][:, :], t[9][:, :], ALU.mult).then_inc(S["a2_r"], 1)
            for a in range(2):
                dve.wait_ge(S["a2_out"], a + 1)
                V.scalar_tensor_tensor(half(h, a), ps[:, 4 + a, 0:HALF], c_("l2bo"), half(h, a),
                                       ALU.add, ALU.add).then_inc(S["h_ready"], 1)

            ln(5)
            dve.wait_ge(S["ln_out"], 12)
            V.tensor_tensor(h[:, :], h[:, :], xn[:, :], ALU.add).then_inc(S["h_ready"], 2)
            ln(6, hx)
            dve.wait_ge(S["ln_out"], 14)
            V.tensor_scalar(hx[:, :], hx[:, :], c_("l2g"), c_("l2b"), ALU.mult, ALU.add).then_inc(S["ln_post"], 1)
            split_x(hx, 2)
            route(MOES[2])
            experts(MOES[2])

            ln(7)
            for k, name in enumerate(("l3bq", "l3bk")):
                dve.wait_ge(S["a3_qkv"], k + 1)
                V.tensor_scalar(two(t[k][:, :]), pair(k), c_(name), 0.0, ALU.add, ALU.min).then_inc(S["a3_min"], 1)
                link(V.tensor_scalar(two(t[3 + k][:, :]), pair(k), c_(name), 0.0, ALU.add, ALU.max))
            for k in (1, 0):
                dve.wait_ge(S["a3_exp"], k + 1)
                link(V.tensor_tensor(t[k][:, :], t[k][:, :], t[3 + k][:, :], ALU.add))
                link(V.tensor_tensor(img(t[k][:, :]), img(t[k][:, :]), bc(decay[:, k, :].unsqueeze(1), D, B, T), ALU.mult))
            for hh in range(H):
                last = V.tensor_scalar(qm[:, hh, :], t[0][:, :], const("headmask")[:, hh:hh + 1], None, ALU.mult)
            last.then_inc(S["a3_qk"], 1)
            value_rows(S["a3_vT"], S["a3_vtok"])

            def mask(b):
                dve.wait_ge(S["a3_scores"], b + 1)
                wait(dve, S["a3_y"], b - 1)
                V.tensor_tensor(ea[:, b % 2].rearrange("p (a h) n -> p (a h) n", a=2).rearrange("p (a h) n -> p a h n", a=2),
                                pair4(1 + b % 2, T), bc(const("causal")[0:T, :].unsqueeze(1).unsqueeze(1), T, 2, HB, T),
                                ALU.mult).then_inc(S["a3_att"], 1)

            mask(0)
            for b in range(B):
                if b + 1 < B:
                    mask(b + 1)
                y_rows(b, 1e-6, False, S["a3_y"], S["a3_ytok"])
            ln(8, t[5])
            dve.wait_ge(S["ln_out"], 18)
            link(V.tensor_scalar(t[5][:, :], t[5][:, :], c_("l3g"), c_("l3b"), ALU.mult, ALU.add))
            V.tensor_tensor(h[:, :], h[:, :], t[5][:, :], ALU.add).then_inc(S["h_ready"], 2)
            ln(9)
            split_x(xn, 3)
            route(MOES[3])
            experts(MOES[3])

        @block.gpsimd
        def _(pool):
            nc.gpsimd.memset(parts[:, :, :, :, :], 0.0)
            nc.gpsimd.memset(vtok[:, :, :, :], 1.0).then_inc(S["pool_ready"], 1)
            pool.wait_ge(S["a0_vtok"], 1)
            for b in range(B):
                pool.wait_ge(S["a0_inv"], b + 1)
                wait(pool, S["a0_y"], b - 1)
                nc.gpsimd.tensor_tensor(vtok2[:, b % 2], vtok[:, b, :, 0:HD],
                                        sm[:, b % 2, 3, :].unsqueeze(2).broadcast_to([T, H, HD]), ALU.mult).then_inc(S["a0_v2"], 1)
            for d in range(1, H):
                pool.wait_ge(S["a2_t"], d + 1)
                wait(pool, S["a2_acc"], d - 1)
                nc.gpsimd.tensor_tensor(t[5][:, :], t[5][:, :], t[7 + d % 2][:, :], ALU.add).then_inc(S["a2_acc"], 1)


def constants():
    blk = np.kron(np.eye(H), np.ones((HD, HD)))
    c = np.zeros((D, CONST_W), np.float32)

    def put(name, a):
        at, w = CONST_AT[name]
        c[:a.shape[0], at:at + a.shape[1]] = a

    put("ident", np.eye(D))
    put("mean", np.full((D, D), 1.0 / D))
    put("centre", np.eye(D) - 1.0 / D)
    put("blk_mean", blk / HD)
    put("blk_one", blk)
    put("blk_kv", blk * 0.125)
    put("headmask", np.kron(np.eye(H), np.ones((HD, 1))))
    put("rev", np.tile(16.0 - np.arange(16), (D, 1)))
    put("index", np.tile(np.arange(T, dtype=np.float64), (D, 1)))
    put("causal", np.triu(np.ones((T, T))))
    div = np.exp(np.arange(0, D, 2, dtype=np.float32) * np.float32(-np.log(10000.0) / D)).astype(np.float32)
    ang = np.arange(NPATCH, dtype=np.float32)[:, None] * div
    put("pos", np.stack([np.sin(ang), np.cos(ang)], -1).reshape(NPATCH, D).T)
    put("perm", np.concatenate([np.kron(np.roll(np.eye(H), d, axis=0), np.eye(HD)) for d in range(1, H)], axis=1))
    put("eps", np.tile([1e-5, 1.1920929e-07], (D, 1)))
    sel = np.zeros((D, PARTS, D), np.float32)
    for r in range(3 * PARTS):
        sel[r, r % PARTS] = 1.0
    return c, sel.reshape(D, PARTS * D)


def kernel(**inputs):
    import ml_dtypes
    import concourse.bacc as _bacc
    from concourse.bass_utils import run_bass_kernel_spmd as _run

    x = {k: np.asarray(v) for k, v in inputs.items()}
    patches = x["x"].reshape(B, SIDE, PATCH, SIDE, PATCH).transpose(2, 4, 0, 1, 3).reshape(2, D, B * NPATCH).transpose(1, 0, 2)
    consts, sel = constants()

    def heads(a):
        return a.reshape((H, 3, HD) + a.shape[1:]).swapaxes(0, 1).reshape((3, D) + a.shape[1:])

    def tile_heads(a):
        return np.tile(a, H)

    bq2, wq2 = heads(x["L2_attn_b_qkv"]), heads(x["L2_attn_W_qkv"])
    col = {"cls": x["cls_tok"].reshape(D), "b3": x["L0_tok_W3_b"]}
    for l in (1, 2):
        e = x[f"L0_tok_eps_in{l}"]
        col[f"ei{l}a"], col[f"ei{l}b"] = e[:D], e[D:]
        col[f"eo{l}"], col[f"b{l}"], col[f"sb{l}"] = x[f"L0_tok_eps_out{l}"], x[f"L0_tok_W{l}_b"], x[f"L0_tok_W{l}_sb"]
    for g in (1, 2, 3):
        col[f"g{g}"] = tile_heads(x[f"L0_attn_g{g}"])
    for p, key in zip("bgemv", ("b", "g", "be", "m", "v")):
        for s in BN_STAGES:
            col[f"bn_{p}_{s}"] = x[f"L1_attn_{s}_{key}"]
        for c in range(NFF1):
            col[f"bn_{p}_f1_{c}"] = x[f"L1_attn_f1_{key}"][c * D:(c + 1) * D]
    b3 = x["L3_attn_b_qkv"]
    for j, n in enumerate("qkv"):
        col[f"l2b{n}"], col[f"l3b{n}"] = bq2[j], b3[j * D:(j + 1) * D]
    col.update(l2bo=x["L2_attn_b_out"], l2g=x["L2_ffn_ln_g"], l2b=x["L2_ffn_ln_b"], l3bo=x["L3_attn_b_out"],
               l3dl=np.repeat(x["L3_attn_decay_logits"], HD), l3g=x["L3_attn_ln_g"], l3b=x["L3_attn_ln_b"])
    mat = {"w3": x["L0_tok_W3_w"].T, "a0qT": x["L0_attn_qkv_w"].T, "a0dT": x["L0_attn_delta_w"].T,
           "a0q": x["L0_attn_qkv_w"], "a0d": x["L0_attn_delta_w"], "a2o": x["L2_attn_W_out"].T, "a3o": x["L3_attn_W_out"]}
    for l in (1, 2):
        for n, key in (("w", "w"), ("s", "sw")):
            a = x[f"L0_tok_W{l}_{key}"].T
            mat[f"{n}{l}a"], mat[f"{n}{l}b"] = a[:D], a[D:]
    for s in "qkvp":
        mat[f"a1{s}"] = x[f"L1_attn_{s}_w"].T
    for c in range(NFF1):
        mat[f"a1f1_{c}"] = x["L1_attn_f1_w"][c * D:(c + 1) * D].T
        mat[f"a1f2_{c}"] = x["L1_attn_f2_w"][:, c * D:(c + 1) * D].T
    for j, n in enumerate("qkv"):
        mat[f"a2{n}"], mat[f"a3{n}"] = wq2[j].T, x["L3_attn_W_qkv"][:, j * D:(j + 1) * D]
    g2 = x["L0_ffn_g2"].transpose(1, 0, 2).reshape(D, 64)
    route = np.concatenate([x["L0_ffn_g1"], g2, x["L1_ffn_Wg"], x["L2_ffn_w_r"].T, x["L3_ffn_gate_w"].T], axis=1)

    def pack(l, e, f):
        w1, w2, b1 = (x[f"L{l}_ffn_{n}"] for n in ("W1", "W2", "b1"))
        return np.concatenate([w1.reshape(e, D, f), w2.reshape(e, f // D, D, D).transpose(0, 2, 1, 3).reshape(e, D, f),
                               b1.reshape(e, f // D, D).transpose(0, 2, 1)], axis=2)

    gu = np.concatenate([x["L3_ffn_shared_gate_up"][None], x["L3_ffn_expert_gate_up"]], axis=0).transpose(0, 2, 1)
    dn = np.concatenate([x["L3_ffn_shared_down"][None], x["L3_ffn_expert_down"]], axis=0).transpose(0, 2, 1)
    w = [pack(0, 64, 256), pack(1, 8, 256), pack(2, 8, 512), np.concatenate([gu, dn], axis=2)]
    b2 = [x[f"L{l}_ffn_b2"].reshape(-1, D) for l in range(3)]
    data = {
        "patches": patches, "consts": consts, "sel": sel.astype(ml_dtypes.bfloat16),
        "cols": np.stack([col[n] for n in COLS], axis=1), "mats": np.stack([mat[n] for n in MATS], axis=1),
        "route": route, "rows_eo": np.stack([x["L0_tok_eps_out1"], x["L0_tok_eps_out2"]]),
        "bias_rows": np.concatenate([x["L1_ffn_bg"], x["L2_ffn_b_r"], x["L3_ffn_expert_bias"]]),
        **{f"w{l}": w[l] for l in range(4)}, **{f"b2_{l}": b2[l] for l in range(3)},
    }
    nc = _bacc.Bacc("TRN2", target_bir_lowering=False, num_devices=1)
    arrays, ap = {}, {}
    for name, a in data.items():
        a = np.ascontiguousarray(a)
        arrays[f"in_{name}"] = a
        ap[name] = nc.dram_tensor(f"in_{name}", a.shape, mybir.dt.from_np(a.dtype), kind="ExternalInput").ap()
    out = nc.dram_tensor("out", (D, N), F32, kind="ExternalOutput").ap()
    tower(nc, ap["patches"], ap["consts"], ap["sel"], ap["cols"], ap["mats"], ap["route"], ap["rows_eo"], ap["bias_rows"],
          [ap[f"w{l}"] for l in range(4)], [ap[f"b2_{l}"] for l in range(3)], out)
    r = _run(nc, [arrays], core_ids=[0])
    return np.ascontiguousarray(r.results[0]["out"].T.reshape(B, T, D))
```

```python
from contextlib import ExitStack

import concourse.bass as bass
import numpy as np
from concourse import mybir

F32 = mybir.dt.float32
F32R = mybir.dt.float32r
BF16 = mybir.dt.bfloat16
ALU = mybir.AluOpType
ACT = mybir.ActivationFunctionType
AX = mybir.AxisListType.X

D = 128
B = 8
PATCH = 16
SIDE = 128 // PATCH
NPATCH = SIDE * SIDE
T = NPATCH + 1
N = B * T
HALF = N // 2
HB = B // 2
H = 8
HD = D // H
VW = HD + 1
TT = 104
NT = N // TT
BANK = 512
HP = HB * NPATCH
NFF1 = 512 // D

CONST_BLOCKS = [
    ("ident", D), ("mean", D), ("centre", D), ("blk_mean", D), ("blk_one", D), ("blk_kv", D), ("headmask", H),
    ("rev", 16), ("index", T), ("causal", T), ("pos", NPATCH), ("perm", 7 * D), ("eps", 2),
]
CONST_AT = {}
_at = 0
for _name, _w in CONST_BLOCKS:
    CONST_AT[_name] = (_at, _w)
    _at += _w
CONST_W = _at

BN_STAGES = ["q", "k", "v", "p", "f2"]
COLS = (["ei1a", "ei1b", "ei2a", "ei2b", "eo1", "eo2", "b1", "b2", "sb1", "sb2", "b3", "cls", "g1", "g2", "g3"]
        + [f"bn_{p}_{s}" for p in "bgemv" for s in BN_STAGES + ["f1_0", "f1_1", "f1_2", "f1_3"]]
        + ["l2bq", "l2bk", "l2bv", "l2bo", "l2g", "l2b", "l3bq", "l3bk", "l3bv", "l3bo", "l3dl", "l3g", "l3b"])
COL = {name: i for i, name in enumerate(COLS)}
NBN = len(BN_STAGES) + 4

MATS = (["w1a", "w1b", "w2a", "w2b", "s1a", "s1b", "s2a", "s2b", "w3", "a0qT", "a0dT", "a0q", "a0d",
         "a1q", "a1k", "a1v", "a1p"] + [f"a1f1_{c}" for c in range(NFF1)] + [f"a1f2_{c}" for c in range(NFF1)]
        + ["a2q", "a2k", "a2v", "a2o", "a3q", "a3k", "a3v", "a3o"])
MAT = {name: i for i, name in enumerate(MATS)}
MATS_FIRST = MAT["a1q"]
ROUTE_W = [72, 8, 8, 16]
ROUTE_AT = [0, 72, 80, 88]
ROUTES = sum(ROUTE_W)


class Moe:

    def __init__(self, layer, experts, hidden, unroll, gated):
        self.layer, self.E, self.U, self.gated = layer, experts, unroll, gated
        self.fill = {0: (2, 15, 2, 1), 1: (2, 0, 0, 1), 2: (2, 0, 2, 1), 3: (0, 6, 2, 0)}[layer]
        self.cols = 3 * hidden if gated else 2 * hidden + hidden // D
        self.I = experts // unroll
        self.n0 = self.k0 = self.i0 = 0
        self.C = hidden // D
        self.F = 2 * hidden if gated else hidden
        self.S = 2 * self.C
        self.early = 2 if gated else 4

    def slot(self, u, s):
        return (u * self.S + s) % 4


SPREAD = 2

MOES = [Moe(0, 64, 256, 4, False), Moe(1, 8, 256, 4, False), Moe(2, 8, 512, 4, False), Moe(3, 16, 128, 4, True)]


for _m, _next in zip(MOES, MOES[1:]):
    _next.n0, _next.k0, _next.i0 = _m.n0 + _m.E, _m.k0 + _m.E * _m.S, _m.i0 + _m.I


def tower(nc, patches, consts, cols_d, mats_d, route_d, rows_eo, bias_rows,
          w_moe, b2_moe, gate_rows, out):
    ctx = ExitStack()
    with ctx:
        def sb(name, shape, dt=F32):
            return ctx.enter_context(nc.sbuf_tensor(name, shape, dt))

        def sem(name):
            return ctx.enter_context(nc.semaphore(name))

        cst = sb("cst", [D, CONST_W])

        def const(name, k=None, w=None):
            at, width = CONST_AT[name]
            if k is not None:
                at, width = at + k * w, w
            return cst[:, at:at + width]

        col = sb("col", [D, len(COLS)])
        mats = sb("mats", [D, len(MATS), D])
        route_w = sb("route_w", [D, ROUTES])
        xp = sb("xp", [D, 2, BANK])
        eo_rows = sb("eo_rows", [D, 2, D])
        bias_bc = sb("bias_bc", [D, 32])

        h = sb("h", [D, N])
        xn = sb("xn", [D, N])
        hx = sb("hx", [D, N])
        lnv = sb("lnv", [D, N])
        sq = sb("sq", [D, N])
        rstd = sb("rstd", [D, N])
        t = [sb(f"t{i}", [D, N]) for i in range(10)]
        qm = sb("qm", [D, H, N])
        vtok = sb("vtok", [T, B, H, VW])
        vtok2 = sb("vtok2", [T, 2, H, HD])
        ea = sb("ea", [T, 2, H, T])
        eb = sb("eb", [T, 2, H, T])
        eat = sb("eat", [T, 2, H, T])
        sm = sb("sm", [T, 2, 6, H])
        ytok = sb("ytok", [T, B, D])
        ktok = ytok
        vtok1 = sb("vtok1", [T, B, D])
        kv = sb("kv", [D, B, D])
        h1 = qm[:, 0:NFF1, :]
        sums = sb("sums", [D, 8, B])
        decay = sb("decay", [D, 2, T])
        bnst = sb("bnst", [D, 3, NBN])
        bns = sb("bns", [D, NBN])
        bnb = sb("bnb", [D, NBN])
        small = sb("small", [D, 16])
        nz = sb("nz", [D, 3, 6 + 2 * D])
        g1m = sb("g1m", [D, H])

        NLMAX = NT * 72
        lg = sb("lg", [TT, NLMAX])
        r_oh = [sb(f"r_oh{i}", [TT, NLMAX]) for i in range(4)]
        r_rank = sb("r_rank", [TT, NLMAX], BF16)
        r_top = sb("r_top", [TT, NT * 9], BF16)
        revb = sb("revb", [TT, 16], BF16)
        r_s = sb("r_s", [TT, 8, NT * 9])
        gates = sb("gates", [TT, NT, 64])
        gT = sb("gT", [64, N])
        cb = sb("cb", [D, 4, N])
        ab = sb("ab", [D, 4, HALF])
        tb = sb("tb", [D, 2, HALF])
        gb = sb("gb", [D, 4, HALF])
        vs = sb("vs", [D, 2, N])

        def eb_of(b):
            return eb[:, b % 2] if b % 4 < 2 else vs[0:T, b % 2, :].rearrange("p (h n) -> p h n", h=H)

        aff = sb("aff", [TT, NT * 16])
        rings = [sb(f"w{m.layer}_sb", [D, m.U, m.cols]) for m in (MOES[0], MOES[2])]
        w_sb = [rings[0], rings[0], rings[1], rings[1]]
        xr = sb("xr", [D, 2, N], F32R)
        wr = sb("wr", [D, 2, 2, max(m.F for m in MOES)], F32R)
        ws_sb = sb("ws_sb", [D, 384])
        b2_sb = [sb(f"b2_{m.layer}", [m.E, D]) for m in MOES[:3]]

        wr_flat = wr[:, :, :, :].rearrange("p a b n -> p (a b n)")
        perm_r = wr_flat[:, 0:7 * D]
        vr = wr_flat[:, 7 * D:7 * D + 2 * N].rearrange("p (a n) -> p a n", a=2)
        PAIR = 2 * HD
        vmask = [tile[:, :, :, :].rearrange("p a h n -> p (a h n)")[:, 0:HB * H * PAIR].rearrange("p (b h n) -> p b h n", b=HB, h=H)
                 for tile in (eat, eb)]
        rin = eat[:, 0].rearrange("p h t -> p (h t)")[:, 0:2 * B * H].rearrange("p (k b h) -> p k b h", k=2, b=B)
        rin_full = [tile[:, :, :, :].rearrange("p a h n -> p (a h n)")[:, 0:B * D].rearrange("p (b n) -> p b n", b=B) for tile in (ea, eb)]

        ps = ctx.enter_context(nc.psum_tensor("ps", [D, 8, BANK], F32))

        def pair(k, rows=D):
            return ps[0:rows, 2 * k:2 * k + 2, 0:HALF]

        def two(ap):
            return ap.rearrange("p (a n) -> p a n", a=2)

        def img(ap):
            return ap.rearrange("p (b t) -> p b t", b=B)

        names = """ld_const ld_noise ld_mat0 ld_mat1 ld_patch ld_bias ld_shared
        dve_chain
        noise wn_ready emb_g emb_gate emb_n emb_ng emb_clamped emb_e emb_x emb_proj h_ready
        ln_centred ln_squared ln_var ln_log ln_rstd ln_out ln_post x_split pool_ready gates_stored
        a0_w a0_n a0_qa a0_max a0_inv a0_wsum a0_sq a0_ms a0_log a0_rinv a0_q a0_vF a0_vT a0_vtok a0_scores a0_ea_in a0_eb_in a0_ea a0_eb a0_eT a0_eat a0_v2
        a0_y a0_ytok a0_yT a0_yF a0_out
        bn_std bn_ready a1_qkv a1_v a1_tr a1_ktok a1_vtok a1_kv a1_kvm a1_o a1_orelu a1_p a1_prelu a1_x1
        a1_f1 a1_h1 a1_f2 a1_y
        a2_qkv a2_in a2_prod a2_io a2_rin a2_rin_i a2_rin_o a2_ri a2_rI a2_ksplit a2_vsplit a2_perm a2_prod2 a2_hats a2_sig a2_einp a2_e a2_ks a2_qk a2_A a2_vw a2_vs a2_vse a2_t a2_acc a2_r a2_out
        a3_qkv a3_v a3_lam a3_lnlam a3_dec a3_max a3_exp a3_q a3_den_out a3_inv a3_qk a3_qa a3_zero a3_vm a3_kT a3_ktok a3_kcum a3_qkc a3_den a3_vT a3_scores a3_att a3_y a3_yF a3_out a3_z
        stored""".split()
        S = {n: sem(n) for n in names}
        rt = {n: sem(f"route_{n}") for n in ("logits", "logits_read", "d", "e", "gates", "turned", "rows", "shared_h", "shared_a", "shared_g")}
        RT_E = {0: 1, 2: 2, 3: 2}
        moe_done = sem("moe_done")
        X = {n: sem(f"moe_{n}") for n in ("gates_spread", "gates_copied", "h_ready", "a_ready", "t_ready", "g_ready", "g_used",
                                          "w_split", "w_split_hi")}

        w_loaded = [sem(f"w_loaded{u}") for u in range(4)]
        gates_loaded = [sem(f"gates_loaded{u}") for u in range(4)]

        def gates_there(m, i, u, a):
            if u >= SPREAD:
                return gates_loaded[u], (i + 1 + m.i0) * 16
            if isinstance(i, int) and i == 0:
                return X["gates_copied"], 2 * (SPREAD * m.layer + u) + a + 1
            return gates_loaded[u], (i + m.i0 - m.layer) * 16

        def wait(eng, s, value):
            if isinstance(value, int) and value <= 0:
                return
            eng.wait_ge(s, value)

        block = ctx.enter_context(nc.Block())

        def mat(name):
            return mats[:, MAT[name], :]

        def c_(name):
            return col[:, COL[name]:COL[name] + 1]

        @block.sync
        def _(sp):
            sp.dma_start(col[:, :], cols_d).then_inc(S["ld_noise"], 16)
            sp.dma_start(eo_rows[:, :, :], rows_eo.rearrange("(o a) n -> o a n", o=1).broadcast_to([D, 2, D])).then_inc(S["ld_noise"], 16)
            sp.dma_start(mats[:, 0:MATS_FIRST, :], mats_d[:, 0:MATS_FIRST, :]).then_inc(S["ld_mat0"], 16)
            sp.dma_start(xp[:, :, :], patches).then_inc(S["ld_patch"], 16)
            sp.dma_start(cst[:, :], consts).then_inc(S["ld_const"], 16)
            sp.dma_start(route_w[:, :], route_d).then_inc(S["ld_bias"], 16)
            for m in range(3):
                sp.dma_start(b2_sb[m][:, :], b2_moe[m]).then_inc(S["ld_bias"], 16)
            sp.dma_start(bias_bc[:, :], bias_rows.rearrange("(o n) -> o n", o=1).broadcast_to([D, 32])).then_inc(S["ld_bias"], 16)
            sp.dma_start(mats[:, MATS_FIRST:, :], mats_d[:, MATS_FIRST:, :]).then_inc(S["ld_mat1"], 16)
            for m in MOES:
                L = m.layer

                def load(i, u):
                    e = i * m.U + u + (1 if m.gated else 0)
                    if L > 0 and isinstance(i, int) and i == 0:
                        prev = MOES[L - 1]
                        sp.wait_ge(X["g_used"], prev.k0 + (prev.E - prev.U + u + 1) * prev.S)
                    if not (isinstance(i, int) and i == 0):
                        sp.wait_ge(X["g_used"], ((i - 1) * m.U + u + 1) * m.S + m.k0)
                    src = w_moe[L][e] if isinstance(e, int) else w_moe[L][bass.ds(e, 1)].rearrange("o p n -> p (o n)")
                    sp.dma_start(w_sb[L][:, u, 0:m.cols], src).then_inc(w_loaded[u], 16)

                def load_gates(i, u):
                    sp.dma_start(cb[:, u, :], gate_rows[bass.ds(i * m.U + u + m.n0, 1), :].broadcast_to([D, N])
                                 ).then_inc(gates_loaded[u], 16)

                if m.gated:
                    sp.dma_start(ws_sb[:, :], w_moe[L][0]).then_inc(S["ld_shared"], 16)
                for u in range(m.U):
                    load(0, u)
                sp.wait_ge(rt["rows"], L + 1)
                sp.dma_start(gate_rows[m.n0:m.n0 + m.E, :], gT[0:m.E, :]).then_inc(S["gates_stored"], 16)
                sp.wait_ge(S["gates_stored"], 16 * (L + 1))
                for u in range(SPREAD, m.U):
                    load_gates(0, u)
                if m.I == 2:
                    for u in range(m.U):
                        load(1, u)
                        load_gates(1, u)
                else:
                    with sp.Fori(1, m.I) as i:
                        for u in range(m.U):
                            load(i, u)
                            load_gates(i, u)
            sp.wait_ge(S["h_ready"], 20)
            sp.dma_start(out, h[:, :]).then_inc(S["stored"], 16)
            sp.wait_ge(S["stored"], 16)

        @block.tensor
        def _(pe):
            def mm(o, lhsT, rhs, start=True, stop=True, **kw):
                return nc.tensor.matmul(o, lhsT, rhs, start=start, stop=stop, **kw)

            def full(k, lhsT, src, start=True, stop=True):
                for a in range(2):
                    last = mm(ps[:, 2 * k + a, 0:HALF], lhsT, src[:, a * HALF:(a + 1) * HALF], start, stop)
                return last

            def keep_clock(n):
                for _ in range(n):
                    mm(ps[:, 7, HALF:BANK], const("ident"), cst[:, 0:BANK - HALF])

            def halves(k, lhsT, src, ready):
                for a in range(2):
                    mm(ps[:, 2 * k + a, 0:HALF], lhsT, src[:, a * HALF:(a + 1) * HALF]).then_inc(ready, 1)

            def ln(k, src, ready, value):
                for a in range(2):
                    pe.wait_ge(ready, value - 1 + a)
                    mm(ps[:, a, 0:HALF], const("centre"), src[:, a * HALF:(a + 1) * HALF]).then_inc(S["ln_centred"], 1)
                for a in range(2):
                    pe.wait_ge(S["ln_squared"], 2 * k + a + 1)
                    mm(ps[:, 2 + a, 0:HALF], const("mean"), sq[:, a * HALF:(a + 1) * HALF]).then_inc(S["ln_var"], 1)
                if k > 0:
                    keep_clock(2)

            pe.wait_ge(S["ld_patch"], 16)
            for l in range(2):
                pe.wait_ge(S["wn_ready"], l + 1)
                for a in range(2):
                    for c in range(2):
                        last = mm(ps[:, 2 * l + a, 0:HP], t[6 + l][:, c * D:(c + 1) * D], xp[:, c, a * HP:(a + 1) * HP], c == 0, c == 1)
                    last.then_inc(S["emb_g"], 1)
            for a in range(2):
                pe.wait_ge(S["emb_x"], a + 1)
                mm(ps[:, 4 + a, 0:HP], mat("w3"), t[4][:, a * HP:(a + 1) * HP]).then_inc(S["emb_proj"], 1)

            pe.wait_ge(S["ld_const"], 16)
            ln(0, h, S["h_ready"], 2)
            pe.wait_ge(S["ln_out"], 2)
            pe.wait_ge(S["a0_wsum"], 1)
            halves(2, mat("a0qT"), xn, S["a0_w"])
            for a in range(2):
                pe.wait_ge(S["a0_sq"], a + 1)
                mm(ps[:, 2 + a, 0:HALF], const("blk_mean"), sq[:, a * HALF:(a + 1) * HALF]).then_inc(S["a0_ms"], 1)

            def to_tokens(src, banks, ready):
                for b in range(B):
                    last = nc.tensor.transpose(ps[0:T, banks + b // HB, (b % HB) * D:(b % HB + 1) * D],
                                               src[:, b * T:(b + 1) * T], const("ident"))
                last.then_inc(ready, 1)

            pe.wait_ge(S["a0_vF"], 1)
            to_tokens(t[2], 0, S["a0_vT"])

            def scores_ij(b):
                wait(pe, S["a0_ea_in"], b)
                for hh in range(H):
                    last = mm(ps[0:T, hh // 4, (hh % 4) * T:(hh % 4 + 1) * T],
                              qm[:, hh, b * T:(b + 1) * T], t[1][:, b * T:(b + 1) * T])
                last.then_inc(S["a0_scores"], 1)

            def scores_ji(b, k, ready):
                for a in range(2):
                    last = mm(ps[0:T, 2 * k + a, 0:HALF].rearrange("p (h t) -> p h t", h=4), t[1][:, b * T:(b + 1) * T],
                              qm[:, 4 * a:4 * a + 4, b * T:(b + 1) * T])
                last.then_inc(ready, 1)

            def turn(b):
                pe.wait_ge(S["a0_ea"], b + 1)
                wait(pe, S["a0_eat"], b)
                for hh in range(H):
                    last = nc.tensor.transpose(ps[0:T, 4 + hh // 4, (hh % 4) * T:(hh % 4 + 1) * T],
                                               ea[:, b % 2, hh, :], const("ident")[0:T, 0:T])
                last.then_inc(S["a0_eT"], 1)

            def weigh(b):
                pe.wait_ge(S["a0_eat"], b + 1)
                wait(pe, S["a0_ytok"], b - 1)
                for hh in range(H):
                    mm(ps[0:T, 6 + b % 2, hh * VW:(hh + 1) * VW], eat[:, b % 2, hh, :], vtok[:, b, hh, :])
                pe.wait_ge(S["a0_v2"], b + 1)
                for hh in range(H):
                    last = mm(ps[0:T, 6 + b % 2, H * VW + hh * HD:H * VW + (hh + 1) * HD],
                              eb_of(b)[:, hh, :], vtok2[:, b % 2, hh, :])
                last.then_inc(S["a0_y"], 1)

            pe.wait_ge(S["a0_vtok"], 1)
            for b in range(-2, B):
                if b + 2 < B:
                    if b + 2 in (0, HB):
                        pe.wait_ge(S["a0_q"], (b + 2) // HB + 1)
                        pe.wait_ge(S["a0_qa"], (b + 2) // HB + 1)
                    scores_ij(b + 2)
                if 0 <= b + 1 < B:
                    turn(b + 1)
                if b + 2 < B:
                    wait(pe, S["a0_eb_in"], b + 2)
                    scores_ji(b + 2, 1, S["a0_scores"])
                if b >= 0:
                    weigh(b)

            def to_features(done, ready):
                for b in range(B):
                    pe.wait_ge(done, b + 1)
                    last = nc.tensor.transpose(ps[:, b // HB, (b % HB) * T:(b % HB + 1) * T], ytok[:, b, :],
                                               const("ident")[0:T, 0:T])
                last.then_inc(ready, 1)

            to_features(S["a0_ytok"], S["a0_yT"])
            keep_clock(1)
            pe.wait_ge(S["a0_yF"], 1)
            halves(1, mat("a0q"), t[3], S["a0_out"])

            def route(m, src):
                w, at = ROUTE_W[m.layer], ROUTE_AT[m.layer]
                for k in range(NT):
                    last = mm(ps[0:TT, 0, k * w:(k + 1) * w], src[:, k * TT:(k + 1) * TT], route_w[:, at:at + w])
                last.then_inc(rt["logits"], 1)
                if m.gated:
                    shared_hidden(src)
                keep_clock(m.fill[0])
                pe.wait_ge(S["x_split"], 2 * m.layer + 2)
                pe.wait_ge(rt["logits_read"], m.layer + 1)
                before_gates = 2 if m.layer == 1 else m.early
                for s in range(before_gates):
                    if m.gated and s == 1:
                        pe.wait_ge(rt["shared_a"], 1)
                    first(m, 0, 0, s)
                if m.gated:
                    keep_clock(1)
                    pe.wait_ge(rt["shared_g"], 2)
                keep_clock(m.fill[1])
                pe.wait_ge(rt["gates"], m.layer + 1)
                for k in range(NT):
                    last = nc.tensor.transpose(ps[0:m.E, 4 + k // 4, (k % 4) * TT:(k % 4 + 1) * TT],
                                               gates[:, k, 0:m.E], const("ident")[0:TT, 0:TT])
                last.then_inc(rt["turned"], 1)
                for s in range(before_gates, m.early):
                    first(m, 0, 0, s)
                keep_clock(m.fill[2])
                pe.wait_ge(rt["rows"], m.layer + 1)
                spread(m, 0)
                keep_clock(m.fill[3])
                if m.gated:
                    for a in range(2):
                        mm(ps[:, 6 + a, 0:HALF], ws_sb[:, 2 * D:3 * D], gb[:, 2 + a, :], True, False)

            def three_pass(m, o, w, c, a):
                for n, (wh, xh) in enumerate(((0, 0), (0, 1), (1, 0))):
                    last = mm(o, wr[:, w, wh, c * D:(c + 1) * D], xr[:, xh, a * HALF:(a + 1) * HALF], n == 0, n == 2)
                return last

            def spread(m, u):
                for a in range(2):
                    wait(pe, X["gates_copied"], 2 * (SPREAD * m.layer + u) - 1 + a)
                    mm(ps[:, 4 + a, 0:HALF], const("ident")[0:m.E, u:u + 1].broadcast_to([m.E, D]),
                       gT[0:m.E, a * HALF:(a + 1) * HALF]).then_inc(X["gates_spread"], 1)

            def first(m, i, u, s):
                k = (i * m.U + u) * m.S + s + m.k0
                c, a = s // 2, s % 2
                if s == 0:
                    pe.wait_ge(X["w_split"], i * m.U + u + 1 + m.n0)
                    if isinstance(i, int) and i == 0 and 0 < u < SPREAD:
                        spread(m, u)
                if m.gated:
                    wait(pe, X["a_ready"], k - 1)
                    wait(pe, X["t_ready"], k - m.k0 - 1)
                    for j in range(2):
                        last = three_pass(m, ps[:, 2 * a + j, 0:HALF], u % 2, j, a)
                else:
                    wait(pe, X["a_ready"], k - 3)
                    last = three_pass(m, ps[:, s % 4, 0:HALF], u % 2, c, a)
                last.then_inc(X["h_ready"], 1)

            def experts(m, src):
                L = m.layer
                W = w_sb[L]

                def second(i, u, s, final):
                    k = (i * m.U + u) * m.S + s + m.k0
                    c, a = s // 2, s % 2
                    at = 2 * D if m.gated else (m.C + c) * D
                    opens = isinstance(i, int) and i + u == 0 and s < 2 and not m.gated
                    pe.wait_ge(X["g_ready"], k + 1)
                    mm(ps[:, 6 + a, 0:HALF], W[:, u, at:at + D], gb[:, m.slot(u, s), :], opens, final and m.gated).then_inc(X["g_used"], 1)

                AHEAD = 2

                def body(i, final):
                    for u in range(m.U):
                        for s in range(m.S):
                            n = u * m.S + s + AHEAD
                            if isinstance(i, int) and i == 0 and n < m.early:
                                pass
                            elif n < m.U * m.S:
                                first(m, i, n // m.S, n % m.S)
                            elif not final:
                                first(m, i + 1, 0, n - m.U * m.S)
                            second(i, u, s, final and u == m.U - 1 and s >= m.S - 2)

                body(0, False)
                if m.I > 2:
                    with pe.Fori(1, m.I - 1) as i:
                        body(i, False)
                body(m.I - 1, True)
                if not m.gated:
                    if L == 0:
                        pe.wait_ge(S["ld_bias"], 5 * 16)
                    for a in range(2):
                        mm(ps[:, 6 + a, 0:HALF], b2_sb[L][:, :], gT[0:m.E, a * HALF:(a + 1) * HALF],
                           False, True).then_inc(moe_done, 1)

            def shared_hidden(src):
                pe.wait_ge(S["ld_shared"], 16)
                for a in range(2):
                    for j in range(2):
                        last = mm(ps[:, 2 + 2 * a + j, 0:HALF], ws_sb[:, j * D:(j + 1) * D], src[:, a * HALF:(a + 1) * HALF])
                    last.then_inc(rt["shared_h"], 1)

            ln(1, h, S["h_ready"], 4)
            pe.wait_ge(S["ln_out"], 4)
            pe.wait_ge(S["ld_bias"], 5 * 16)
            route(MOES[0], xn)
            experts(MOES[0], xn)

            ln(2, h, S["h_ready"], 6)
            pe.wait_ge(S["ln_out"], 6)
            pe.wait_ge(S["ld_mat1"], 16)
            def half_mm(bank, lhsT, src, a, start=True, stop=True):
                return mm(ps[:, bank, 0:HALF], lhsT, src[:, a * HALF:(a + 1) * HALF], start, stop)

            for a in range(2):
                for k, name in enumerate(("a1q", "a1k", "a1v")):
                    half_mm(2 * k + a, mat(name), xn, a).then_inc(S["a1_qkv"], 1)
            for a in range(2):
                for k in range(2):
                    pe.wait_ge(S["a1_v"], 3 * a + 2 + k)
                    for c in range(HB):
                        last = nc.tensor.transpose(ps[0:T, 2 * k + a, c * D:(c + 1) * D],
                                                   t[1 + k][:, (a * HB + c) * T:(a * HB + c + 1) * T], const("ident"))
                    last.then_inc(S["a1_tr"], 1)
            for a in range(2):
                pe.wait_ge(S["a1_ktok"], a + 1)
                pe.wait_ge(S["a1_vtok"], a + 1)
                for c in range(HB):
                    last = mm(ps[:, 4 + a, c * D:(c + 1) * D], ktok[:, a * HB + c, :], vtok1[:, a * HB + c, :])
                last.then_inc(S["a1_kv"], 1)
            for a in range(2):
                pe.wait_ge(S["a1_kvm"], a + 1)
                for c in range(HB):
                    last = mm(ps[:, 6 + a, c * T:(c + 1) * T], kv[:, a * HB + c, :], t[0][:, (a * HB + c) * T:(a * HB + c + 1) * T])
                last.then_inc(S["a1_o"], 1)
            for a in range(2):
                pe.wait_ge(S["a1_orelu"], a + 1)
                half_mm(a, mat("a1p"), t[3], a).then_inc(S["a1_p"], 1)
            for c in range(NFF1 + 1):
                for a in range(2):
                    if c < NFF1:
                        if c == 0:
                            pe.wait_ge(S["a1_x1"], a + 1)
                        half_mm(2 + 2 * (c % 2) + a, mat(f"a1f1_{c}"), t[5], a).then_inc(S["a1_f1"], 1)
                for a in range(2):
                    if c > 0:
                        pe.wait_ge(S["a1_h1"], 2 * (c - 1) + a + 1)
                        last = half_mm(6 + a, mat(f"a1f2_{c - 1}"), h1[:, c - 1, :], a, c == 1, c == NFF1)
                        if c == NFF1:
                            last.then_inc(S["a1_f2"], 1)

            ln(3, h, S["h_ready"], 8)
            pe.wait_ge(S["ln_out"], 8)
            route(MOES[1], xn)
            experts(MOES[1], xn)

            ln(4, h, S["h_ready"], 10)
            pe.wait_ge(S["ln_out"], 10)
            for a in range(2):
                for k, name in enumerate(("a2q", "a2k", "a2v")):
                    half_mm(2 * k + a, mat(name), xn, a).then_inc(S["a2_qkv"], 1)
            for a in range(2):
                for j in range(2):
                    pe.wait_ge(S["a2_prod"], 2 * a + j + 1)
                    for c in range(HB):
                        b = a * HB + c
                        last = mm(ps[0:T, 6 + a, (j * HB + c) * H:(j * HB + c + 1) * H], t[3 + j][:, b * T:(b + 1) * T], const("headmask"))
                last.then_inc(S["a2_io"], 1)
            for j in (1, 0):
                for a in range(2):
                    pe.wait_ge(S["a2_rin_o" if j else "a2_rin_i"], a + 1)
                    for c in range(HB):
                        last = mm(ps[:, 2 * j + a, c * T:(c + 1) * T], rin_full[j][:, a * HB + c, :], const("ident")[0:T, 0:T])
                    last.then_inc(S["a2_ri"], 1)
            for j in range(2):
                for a in range(2):
                    pe.wait_ge(S["a2_prod2"], 2 * j + a + 1)
                    half_mm(4 + 2 * j + a, const("blk_one"), t[3 + j], a).then_inc(S["a2_hats"], 1)

            def shifted(k, d, src):
                for a in range(2):
                    for j in range(2):
                        last = mm(ps[:, 2 * k + a, 0:HALF], perm_r[:, (d - 1) * D:d * D], src[:, j, a * HALF:(a + 1) * HALF], j == 0, j == 1)
                return last

            pe.wait_ge(S["a2_qk"], 1)
            halves(1, const("blk_one"), t[3], S["a2_A"])
            pe.wait_ge(S["a2_ksplit"], 2)
            pe.wait_ge(S["a2_perm"], 1)
            shifted(0, 1, xr).then_inc(S["a2_ks"], 1)
            pe.wait_ge(S["a2_sig"], 2)
            shifted(2, 2, xr).then_inc(S["a2_ks"], 1)
            pe.wait_ge(S["a2_einp"], 2)
            keep_clock(5)
            for dlt in range(1, H):
                pe.wait_ge(S["a2_vsplit"], 2)
                wait(pe, S["a2_vse"], dlt - 1)
                shifted(3, dlt, vr).then_inc(S["a2_vs"], 1)
                pe.wait_ge(S["a2_qk"], dlt + 1)
                for a in range(2):
                    pe.wait_ge(S["a2_t"], 2 * (dlt - 1) + a + 1)
                    half_mm(2 + a, const("blk_one"), t[3 + dlt % 2], a).then_inc(S["a2_A"], 1)
                if dlt + 2 < H:
                    shifted(2 * ((dlt + 1) % 2), dlt + 2, xr).then_inc(S["a2_ks"], 1)
            pe.wait_ge(S["a2_t"], 2 * H)
            keep_clock(4)
            pe.wait_ge(S["a2_r"], 1)
            halves(2, mat("a2o"), t[5], S["a2_out"])

            ln(5, h, S["h_ready"], 12)
            ln(6, xn, S["ln_out"], 12)
            pe.wait_ge(S["ln_post"], 1)
            pe.wait_ge(S["h_ready"], 14)
            route(MOES[2], hx)
            experts(MOES[2], hx)

            ln(7, h, S["h_ready"], 16)
            pe.wait_ge(S["ln_out"], 16)
            for k, name in ((1, "a3k"), (0, "a3q"), (2, "a3v")):
                full(k, mat(name), xn).then_inc(S["a3_qkv"], 1)
            pe.wait_ge(S["a3_v"], 1)
            pe.wait_ge(S["a3_exp"], 2)
            pe.wait_ge(S["a3_max"], 2)
            pe.wait_ge(S["a3_q"], 1)
            to_tokens(t[1], 6, S["a3_kT"])
            to_tokens(t[2], 0, S["a3_vT"])

            def scores3(b):
                if b in (0, HB):
                    pe.wait_ge(S["a3_qk"], b // HB + 1)
                    pe.wait_ge(S["a3_qa"], b // HB + 1)
                wait(pe, S["a3_att"], b - 1)
                scores_ji(b, 1 + b % 2, S["a3_scores"])

            pe.wait_ge(S["a3_ktok"], 1)
            for c in range(B):
                last = mm(ps[:, 6 + c // HB, (c % HB) * T:(c % HB + 1) * T], ktok[:, c, :], const("causal")[0:T, :])
            last.then_inc(S["a3_kcum"], 1)
            scores3(0)
            for b in range(B):
                if b + 1 < B:
                    scores3(b + 1)
                if b < 2:
                    pe.wait_ge(S["a3_qkc"], 1)
                    wait(pe, S["a3_den_out"], b)
                    mm(ps[:, 7, 0:HALF], const("blk_one"), t[4][:, b * HALF:(b + 1) * HALF]).then_inc(S["a3_den"], 1)
                if b == HB - 1:
                    pe.wait_ge(S["a3_den_out"], 2)
                if b in (HB - 1, HB):
                    keep_clock(1)
                pe.wait_ge(S["a3_att"], b + 1)
                if b == 0:
                    pe.wait_ge(S["a3_vm"], 1)
                for hh in range(H):
                    rows = slice(hh // 2 * PAIR, hh // 2 * PAIR + PAIR)
                    last = mm(ps[rows, 6 + b // HB, (b % HB) * T:(b % HB + 1) * T], vmask[b // HB][:, b % HB, hh, :],
                              ea[:, b % 2, hh, :], hh % 2 == 0, hh % 2 == 1)
                last.then_inc(S["a3_y"], 1)
            for a in range(2):
                pe.wait_ge(S["a3_yF"], a + 1)
                mm(ps[:, 4 + a, 0:HALF], mat("a3o"), t[3][:, a * HALF:(a + 1) * HALF]).then_inc(S["a3_out"], 1)
            ln(8, t[4], S["a3_z"], 2)

            ln(9, h, S["h_ready"], 18)
            pe.wait_ge(S["ln_out"], 20)
            route(MOES[3], xn)
            experts(MOES[3], xn)


        @block.scalar
        def _(act):
            def fn(o, i, f, **kw):
                return nc.scalar.activation(o, i, f, **kw)

            eps_ln = const("eps")[:, 0:1]
            eps_rms = const("eps")[:, 1:2]

            def half(ap, a):
                return ap[:, a * HALF:(a + 1) * HALF]

            def ln(k):
                for a in range(2):
                    act.wait_ge(S["ln_centred"], 2 * k + a + 1)
                    fn(half(sq, a), ps[:, a, 0:HALF], ACT.Square).then_inc(S["ln_squared"], 1)
                for a in range(2):
                    act.wait_ge(S["ln_var"], 2 * k + a + 1)
                    fn(half(lnv, a), ps[:, 2 + a, 0:HALF], ACT.Ln, bias=eps_ln).then_inc(S["ln_log"], 1)
                for a in range(2):
                    act.wait_ge(S["ln_log"], 2 * k + a + 1)
                    fn(half(rstd, a), half(lnv, a), ACT.Exp, scale=-0.5).then_inc(S["ln_rstd"], 1)

            nc.scalar.preload_act_table_set("sqrt_and_others")
            act.wait_ge(S["ld_noise"], 2 * 16)
            e6, erow = col[:, 0:6], eo_rows[:, :, :].rearrange("p a n -> p (a n)")
            fn(nz[:, 0, 0:6], e6, ACT.Abs)
            fn(nz[:, 0, 6:], erow, ACT.Abs).then_inc(S["noise"], 1)
            fn(nz[:, 2, 0:6], e6, ACT.Sign)
            fn(nz[:, 2, 6:], erow, ACT.Sign)
            act.wait_ge(S["noise"], 1)
            fn(nz[:, 1, :], nz[:, 0, :], ACT.Sqrt).then_inc(S["noise"], 1)
            act.wait_ge(S["ld_const"], 16)
            fn(bnst[:, 0, :], col[:, COL["bn_v_q"]:COL["bn_v_q"] + NBN], ACT.Sqrt, bias=eps_ln).then_inc(S["bn_std"], 1)
            nc.scalar.preload_act_table_set("natural_log_exp_and_others")
            for a in range(2):
                act.wait_ge(S["emb_clamped"], a + 1)
                fn(t[2][:, a * HP:(a + 1) * HP], t[0][:, a * HP:(a + 1) * HP], ACT.Exp).then_inc(S["emb_e"], 1)
                fn(t[1][:, a * HP:(a + 1) * HP], ps[:, a, 0:HP], ACT.Identity, bias=small[:, 0:1]).then_inc(S["emb_gate"], 1)
            fn(small[:, 4:5], c_("l3dl"), ACT.Exp, scale=-1.0).then_inc(S["a3_lam"], 1)

            ln(0)
            act.wait_ge(S["a3_lnlam"], 1)
            fn(small[:, 6:7], small[:, 5:6], ACT.Ln).then_inc(S["a3_lam"], 1)
            for a in range(2):
                act.wait_ge(S["a0_w"], a + 1)
                fn(half(sq, a), ps[:, 4 + a, 0:HALF], ACT.Square).then_inc(S["a0_sq"], 1)
            for a in range(2):
                act.wait_ge(S["a0_ms"], a + 1)
                fn(half(lnv, a), ps[:, 2 + a, 0:HALF], ACT.Ln, bias=eps_rms).then_inc(S["a0_log"], 1)
            for a in range(2):
                act.wait_ge(S["a0_log"], a + 1)
                fn(half(rstd, a), half(lnv, a), ACT.Exp, scale=-0.5).then_inc(S["a0_rinv"], 1)
            act.wait_ge(S["a3_lnlam"], 2)
            fn(decay[:, 0, :], const("index"), ACT.Exp, scale=small[:, 6:7])
            fn(decay[:, 1, :], const("index"), ACT.Exp, scale=small[:, 7:8]).then_inc(S["a3_dec"], 1)
            act.wait_ge(S["a0_n"], 1)
            fn(t[2][:, :], t[0][:, :], ACT.Identity, scale=c_("g3")).then_inc(S["a0_vF"], 1)
            for a in range(2):
                for hh in range(H // 2, H):
                    last = fn(half(qm[:, hh, :], a), half(t[0], a), ACT.Identity, scale=g1m[:, hh:hh + 1])
                last.then_inc(S["a0_qa"], 1)
            for b in range(-1, B):
                if 0 <= b:
                    act.wait_ge(S["a0_eT"], b + 1)
                    wait(act, S["a0_y"], b - 1)
                    fn(eat[:, b % 2].rearrange("p (a h) n -> p a (h n)", a=2), pair(2, T), ACT.Copy).then_inc(S["a0_eat"], 1)
                if b + 1 < B:
                    act.wait_ge(S["a0_ea_in"], b + 2)
                    fn(ea[:, (b + 1) % 2], ea[:, (b + 1) % 2], ACT.Exp).then_inc(S["a0_ea"], 1)
                    act.wait_ge(S["a0_eb_in"], b + 2)
                    fn(eb_of(b + 1), eb_of(b + 1), ACT.Exp).then_inc(S["a0_eb"], 1)
            act.wait_ge(S["a0_yT"], 1)
            fn(two(t[3][:, :]), pair(0), ACT.Copy).then_inc(S["a0_yF"], 1)

            def x_ready(m):
                return {0: (S["ln_out"], 4), 1: (S["ln_out"], 8), 2: (S["ln_post"], 1), 3: (S["ln_out"], 20)}[m.layer]

            def route(m, func):
                R = rt
                act.wait_ge(*x_ready(m))
                fn(xr[:, 0, :], (hx if m.layer == 2 else xn)[:, :], ACT.Copy).then_inc(S["x_split"], 1)
                if m.gated:
                    act.wait_ge(R["logits"], m.layer + 1)
                    fn(aff[:, :], ps[0:TT, 0, 0:NT * m.E], ACT.Sigmoid).then_inc(R["logits_read"], 1)
                    nc.scalar.preload_act_table_set("silu_and_others")
                    for a in range(2):
                        act.wait_ge(R["shared_h"], a + 1)
                        fn(ab[:, 2 + a, :], ps[:, 2 + 2 * a, 0:HALF], ACT.Silu)
                        fn(gb[:, 2 + a, :], ps[:, 3 + 2 * a, 0:HALF], ACT.Copy).then_inc(R["shared_a"], 1)
                elif m.layer != 1:
                    act.wait_ge(R["d"], RT_E[m.layer])
                    n = NT * 9 if m.layer == 0 else NT
                    fn(r_s[:, 4, 0:n], r_s[:, 3, 0:n], ACT.Exp).then_inc(R["e"], 1)
                    if m.layer == 2:
                        nc.scalar.preload_act_table_set("gelu_and_others")
                for k in range(2):
                    activate(m, 0, 0, k, func)
                act.wait_ge(R["turned"], m.layer + 1)
                fn(gT[0:m.E, 0:4 * TT], ps[0:m.E, 4, 0:4 * TT], ACT.Copy)
                fn(gT[0:m.E, 4 * TT:N], ps[0:m.E, 5, 0:N - 4 * TT], ACT.Copy).then_inc(R["rows"], 1)
                for k in range(2, m.early):
                    activate(m, 0, 0, k, func)

            def activate(m, i, u, s, func):
                k = (i * m.U + u) * m.S + s + m.k0
                act.wait_ge(X["h_ready"], k + 1)
                wait(act, X["g_ready"], k - 3)
                if m.gated:
                    fn(ab[:, m.slot(u, s), :], ps[:, 2 * s, 0:HALF], func).then_inc(X["a_ready"], 1)
                else:
                    at = 2 * m.C * D + s // 2
                    bias = w_sb[m.layer][:, u, at:at + 1]
                    fn(ab[:, s % 4, :], ps[:, s % 4, 0:HALF], func, bias=bias).then_inc(X["a_ready"], 1)

            def experts(m, func):
                L = m.layer

                def body(i):
                    for u in range(m.U):
                        if isinstance(i, int) and i == 0 and u < SPREAD:
                            for a in range(2):
                                act.wait_ge(X["gates_spread"], 2 * (SPREAD * L + u) + a + 1)
                                fn(cb[:, u, a * HALF:(a + 1) * HALF], ps[:, 4 + a, 0:HALF], ACT.Copy).then_inc(X["gates_copied"], 1)
                        for s in range(m.early if isinstance(i, int) and i + u == 0 else 0, m.S):
                            activate(m, i, u, s, func)

                body(0)
                if m.I > 2:
                    with act.Fori(1, m.I - 1) as i:
                        body(i)
                body(m.I - 1)

            ln(1)
            route(MOES[0], ACT.Relu)
            experts(MOES[0], ACT.Relu)

            def bn(o, i, k):
                return fn(o, i, ACT.Relu, scale=bns[:, k:k + 1], bias=bnb[:, k:k + 1])

            ln(2)
            act.wait_ge(S["bn_ready"], 1)
            for a in range(2):
                for k in range(3):
                    act.wait_ge(S["a1_qkv"], 3 * a + k + 1)
                    bn(half(t[k], a), ps[:, 2 * k + a, 0:HALF], k).then_inc(S["a1_v"], 1)
            for a in range(2):
                act.wait_ge(S["a1_tr"], 2 * a + 2)
                fn(vtok1[:, a * HB:(a + 1) * HB, :].rearrange("p b n -> p (b n)"), ps[0:T, 2 + a, :], ACT.Copy).then_inc(S["a1_vtok"], 1)
            for a in range(2):
                act.wait_ge(S["a1_o"], a + 1)
                fn(half(t[3], a), ps[:, 6 + a, 0:HALF], ACT.Relu).then_inc(S["a1_orelu"], 1)
            for a in range(2):
                act.wait_ge(S["a1_p"], a + 1)
                bn(half(t[4], a), ps[:, a, 0:HALF], 3).then_inc(S["a1_prelu"], 1)
            for c in range(NFF1):
                for a in range(2):
                    act.wait_ge(S["a1_f1"], 2 * c + a + 1)
                    bn(half(h1[:, c, :], a), ps[:, 2 + 2 * (c % 2) + a, 0:HALF], 5 + c).then_inc(S["a1_h1"], 1)
            for a in range(2):
                act.wait_ge(S["a1_f2"], a + 1)
                bn(half(t[6], a), ps[:, 6 + a, 0:HALF], 4).then_inc(S["a1_y"], 1)

            ln(3)
            route(MOES[1], ACT.Relu)
            experts(MOES[1], ACT.Relu)

            ln(4)
            nc.scalar.preload_act_table_set("sigmoid_and_others")
            for a in range(2):
                for k, name in enumerate(("l2bq", "l2bk", "l2bv")):
                    act.wait_ge(S["a2_qkv"], 3 * a + k + 1)
                    fn(half(t[k], a), ps[:, 2 * k + a, 0:HALF], ACT.Identity if k == 2 else ACT.Sigmoid, bias=c_(name)).then_inc(S["a2_in"], 1)
            for a in range(2):
                act.wait_ge(S["a2_rin"], a + 1)
                fn(rin_full[0][:, a * HB:(a + 1) * HB, :].rearrange("p b (h d) -> p (b h) d", h=H),
                   rin[:, 0, a * HB:(a + 1) * HB, :].rearrange("p b h -> p (b h)").unsqueeze(2).broadcast_to([T, HB * H, HD]),
                   ACT.Copy).then_inc(S["a2_rin_i"], 1)
            for a in range(2):
                act.wait_ge(S["a2_ri"], 3 + a)
                fn(half(t[5], a), ps[:, a, 0:HALF], ACT.Copy).then_inc(S["a2_rI"], 1)
            for a in range(2):
                act.wait_ge(S["a2_hats"], a + 1)
                fn(half(t[9], a), ps[:, 4 + a, 0:HALF], ACT.Sigmoid).then_inc(S["a2_sig"], 1)
            nc.scalar.preload_act_table_set("natural_log_exp_and_others")
            for a in range(2):
                act.wait_ge(S["a2_einp"], a + 1)
                fn(half(t[6], a), half(t[6], a), ACT.Exp).then_inc(S["a2_e"], 1)
            for d in range(1, H):
                act.wait_ge(S["a2_vs"], d)
                wait(act, S["a2_t"], 2 * (d - 1))
                fn(two(vs[:, d % 2, :]), pair(3), ACT.Copy).then_inc(S["a2_vse"], 1)

            ln(5)
            ln(6)
            route(MOES[2], ACT.Gelu)
            experts(MOES[2], ACT.Gelu)
            nc.scalar.preload_act_table_set("natural_log_exp_and_others")

            ln(7)
            for k, name in ((1, "l3bk"), (0, "l3bq")):
                act.wait_ge(S["a3_max"], 2 - k)
                fn(two(t[k][:, :]), pair(k), ACT.Exp, bias=c_(name)).then_inc(S["a3_exp"], 1)
            act.wait_ge(S["a3_qkv"], 3)
            fn(two(t[2][:, :]), pair(2), ACT.Identity, bias=c_("l3bv")).then_inc(S["a3_v"], 1)
            act.wait_ge(S["a3_kT"], 1)
            fn(ktok[:, :, :].rearrange("p (a b) n -> p a (b n)", a=2), ps[0:T, 6:8, :], ACT.Copy).then_inc(S["a3_ktok"], 1)
            for a in range(2):
                act.wait_ge(S["a3_q"], a + 2)
                for hh in range(H // 2, H):
                    last = fn(half(qm[:, hh, :], a), half(t[0], a), ACT.Identity, scale=const("headmask")[:, hh:hh + 1])
                last.then_inc(S["a3_qa"], 1)
                if a == 0:
                    act.wait_ge(S["a3_vT"], 1)
                    act.wait_ge(S["a3_zero"], 1)
                    for c in range(2):
                        for odd in range(2):
                            last = fn(vmask[c].rearrange("p b (g o) n -> p (b g) o n", o=2)[:, :, odd, odd * HD:(odd + 1) * HD],
                                      ps[0:T, c, :].rearrange("p (g o d) -> p g o d", o=2, d=HD)[:, :, odd, :], ACT.Copy)
                    last.then_inc(S["a3_vm"], 1)
            for a in range(2):
                act.wait_ge(S["a3_out"], a + 1)
                fn(half(t[4], a), ps[:, 4 + a, 0:HALF], ACT.Identity, bias=c_("l3bo")).then_inc(S["a3_z"], 1)
            ln(8)
            ln(9)
            nc.scalar.preload_act_table_set("sigmoid_and_others")
            route(MOES[3], ACT.Silu)
            experts(MOES[3], ACT.Silu)

        @block.vector
        def _(dve):
            V = nc.vector
            chain = [0]

            def link(ins):
                chain[0] += 1
                ins.then_inc(S["dve_chain"], 1)
                dve.wait_ge(S["dve_chain"], chain[0])

            def mark(ins):
                chain[0] += 1
                ins.then_inc(S["dve_chain"], 1)
                return chain[0]

            def bc(ap, *shape):
                return ap.broadcast_to(list(shape))

            def half(ap, a):
                return ap[:, a * HALF:(a + 1) * HALF]

            def per_img(cols_):
                return bc(cols_.unsqueeze(2), D, B, T)

            def pair4(k, rows=D):
                return ps[0:rows, 2 * k:2 * k + 2, 0:HALF].rearrange("p a (b t) -> p a b t", b=HB)

            def img4(ap):
                return ap.rearrange("p (a b t) -> p a b t", a=2, b=HB)

            def ln(k, o=None):
                for a in range(2):
                    dve.wait_ge(S["ln_rstd"], 2 * k + a + 1)
                    V.tensor_tensor((xn if o is None else o)[:, a * HALF:(a + 1) * HALF], ps[:, a, 0:HALF],
                                    rstd[:, a * HALF:(a + 1) * HALF], ALU.mult).then_inc(S["ln_out"], 1)

            dve.wait_ge(S["noise"], 2)
            link(V.tensor_tensor(nz[:, 0, :], nz[:, 1, :], nz[:, 2, :], ALU.mult))
            dve.wait_ge(S["ld_mat0"], 16)
            for l in range(2):
                row = nz[:, 0, 6 + l * D:6 + (l + 1) * D]
                tmp = t[8][:, 0:2 * D].rearrange("p (c n) -> p c n", c=2)
                link(V.tensor_tensor(tmp, mats[:, 4 + 2 * l:6 + 2 * l, :], bc(row.unsqueeze(1), D, 2, D), ALU.mult))
                for c in range(2):
                    last = V.scalar_tensor_tensor(t[6 + l][:, c * D:(c + 1) * D], t[8][:, c * D:(c + 1) * D],
                                                  nz[:, 0, 2 * l + c:2 * l + c + 1], mats[:, 2 * l + c, :], ALU.mult, ALU.add)
                last.then_inc(S["wn_ready"], 1)
                dve.wait_ge(S["wn_ready"], l + 1)
            for l in range(2):
                link(V.scalar_tensor_tensor(small[:, l:l + 1], c_(f"sb{l + 1}"), nz[:, 0, 4 + l:5 + l], c_(f"b{l + 1}"),
                                            ALU.mult, ALU.add))
            for a in range(2):
                dve.wait_ge(S["emb_g"], a + 1)
                V.tensor_scalar(t[0][:, a * HP:(a + 1) * HP], ps[:, a, 0:HP], small[:, 0:1], 20.0, ALU.add, ALU.min).then_inc(S["emb_clamped"], 1)
            V.tensor_copy(img(h[:, :])[:, :, 0:1], bc(c_("cls").unsqueeze(2), D, B, 1))
            for a in range(2):
                E_ = slice(a * HP, (a + 1) * HP)
                dve.wait_ge(S["emb_e"], a + 1)
                V.scalar_tensor_tensor(t[3][:, E_], t[2][:, E_], 2.0, t[2][:, E_], ALU.add, ALU.mult).then_inc(S["emb_n"], 1)
                dve.wait_ge(S["emb_n"], a + 1)
                link(V.tensor_scalar(t[5][:, E_], t[3][:, E_], 2.0, None, ALU.add))
                link(V.reciprocal(t[5][:, E_], t[5][:, E_]))
                dve.wait_ge(S["emb_ng"], a + 1)
                link(V.tensor_tensor(t[8][:, E_], t[9][:, E_], t[5][:, E_], ALU.mult))
                dve.wait_ge(S["emb_g"], 3 + a)
                V.scalar_tensor_tensor(t[4][:, E_], ps[:, 2 + a, 0:HP], small[:, 1:2], t[8][:, E_], ALU.add, ALU.mult).then_inc(S["emb_x"], 1)
            dve.wait_ge(S["ld_const"], 16)
            for a in range(2):
                dve.wait_ge(S["emb_proj"], a + 1)
                V.scalar_tensor_tensor(half(h, a).rearrange("p (b t) -> p b t", b=HB)[:, :, 1:T],
                                       ps[:, 4 + a, 0:HP].rearrange("p (b t) -> p b t", b=HB), c_("b3"),
                                       bc(const("pos").unsqueeze(1), D, HB, NPATCH), ALU.add, ALU.add).then_inc(S["h_ready"], 1)

            V.tensor_tensor(mat("a0qT"), mat("a0qT"), mat("a0dT"), ALU.add)
            V.tensor_tensor(mat("a0q"), mat("a0q"), mat("a0d"), ALU.add).then_inc(S["a0_wsum"], 1)
            link(V.tensor_scalar(g1m[:, :], const("headmask"), c_("g1"), 1.0 / HD ** 0.5, ALU.mult, ALU.mult))
            link(V.tensor_copy(revb[:, :], const("rev")[0:TT, :]))
            dve.wait_ge(S["a3_lam"], 1)
            link(V.tensor_scalar(small[:, 4:5], small[:, 4:5], 1.0, None, ALU.add))
            link(V.reciprocal(small[:, 4:5], small[:, 4:5]))
            V.tensor_scalar(small[:, 5:6], small[:, 4:5], 0.01, 0.99, ALU.mult, ALU.add).then_inc(S["a3_lnlam"], 1)
            dve.wait_ge(S["bn_std"], 1)

            def bncols(p):
                return col[:, COL[f"bn_{p}_q"]:COL[f"bn_{p}_q"] + NBN]

            link(V.reciprocal(bnst[:, 1, :], bnst[:, 0, :]))
            link(V.tensor_tensor(bns[:, :], bncols("g"), bnst[:, 1, :], ALU.mult))
            link(V.tensor_tensor(bnst[:, 2, :], bncols("b"), bncols("m"), ALU.subtract))
            link(V.tensor_tensor(bnst[:, 2, :], bnst[:, 2, :], bns[:, :], ALU.mult))
            V.tensor_tensor(bnb[:, :], bnst[:, 2, :], bncols("e"), ALU.add).then_inc(S["bn_ready"], 1)

            ln(0)
            dve.wait_ge(S["a3_lam"], 2)
            V.tensor_scalar(small[:, 7:8], small[:, 6:7], -1.0, None, ALU.mult).then_inc(S["a3_lnlam"], 1)
            for a in range(2):
                dve.wait_ge(S["a0_rinv"], a + 1)
                last = V.tensor_tensor(half(t[0], a), ps[:, 4 + a, 0:HALF], half(rstd, a), ALU.mult)
            last.then_inc(S["a0_n"], 1)
            dve.wait_ge(S["a0_n"], 1)
            for a in range(2):
                V.tensor_scalar(half(t[1], a), half(t[0], a), c_("g2"), None, ALU.mult)
                for hh in range(H // 2):
                    last = V.tensor_scalar(half(qm[:, hh, :], a), half(t[0], a), g1m[:, hh:hh + 1], None, ALU.mult)
                last.then_inc(S["a0_q"], 1)

            def value_rows(ready, done):
                dve.wait_ge(ready, 1)
                for a in range(2):
                    last = V.tensor_copy(vtok[:, a * HB:(a + 1) * HB, :, 0:HD].rearrange("p b h d -> p (b h) d"),
                                         ps[0:T, a, :].rearrange("p (n d) -> p n d", d=HD))
                last.then_inc(done, 1)

            dve.wait_ge(S["pool_ready"], 1)
            value_rows(S["a0_vT"], S["a0_vtok"])
            dve.wait_ge(S["a3_dec"], 1)
            V.tensor_scalar(decay[:, 0, :], decay[:, 0, :], 1.0 / HD ** 0.5, None, ALU.mult)

            def shift(b, pk, j, dst, done, between):
                stat = sm[:, b % 2, j, :].rearrange("p (a h) -> p a h", a=2)
                V.tensor_reduce(stat, pair4(pk, T), AX, ALU.max).then_inc(S["a0_max"], 1)
                between()
                dve.wait_ge(S["a0_max"], 2 * b + j + 1)
                V.tensor_tensor(dst.rearrange("p (a h) n -> p a h n", a=2), pair4(pk, T),
                                bc(stat.unsqueeze(3), T, 2, HB, T), ALU.subtract).then_inc(done, 1)

            def inverse_sums(b):
                if 0 <= b < B:
                    dve.wait_ge(S["a0_eb"], b + 1)
                    link(V.tensor_reduce(sm[:, b % 2, 2, :], eb_of(b), AX, ALU.add))
                    V.reciprocal(sm[:, b % 2, 3, :], sm[:, b % 2, 2, :]).then_inc(S["a0_inv"], 1)

            def y_rows(b, eps, extra, ready, done):
                dve.wait_ge(ready, b + 1)
                rows = ps[0:T, 6 + b % 2, 0:H * VW].rearrange("p (h d) -> p h d", h=H)
                den = rows[:, :, HD:VW]
                r = sm[:, b % 2, 4, :]
                yb = ytok[:, b, :].rearrange("p (h d) -> p h d", h=H)
                if eps:
                    link(V.tensor_scalar(sm[:, b % 2, 5, :].unsqueeze(2), den, eps, None, ALU.add))
                    den = sm[:, b % 2, 5, :].unsqueeze(2)
                link(V.reciprocal(r.unsqueeze(2), den))
                last = V.tensor_tensor(yb, rows[:, :, 0:HD], bc(r.unsqueeze(2), T, H, HD), ALU.mult)
                if extra:
                    link(last)
                    last = V.tensor_tensor(ytok[:, b, :], ytok[:, b, :], ps[0:T, 6 + b % 2, H * VW:H * VW + D], ALU.add)
                last.then_inc(done, 1)

            for b in range(-2, B + 1):
                if b + 2 < B:
                    dve.wait_ge(S["a0_scores"], 2 * (b + 2) + 1)
                    wait(dve, S["a0_eT"], b + 1)
                    shift(b + 2, 0, 0, ea[:, b % 2], S["a0_ea_in"], lambda: None)
                if b >= 1:
                    y_rows(b - 1, 0, True, S["a0_y"], S["a0_ytok"])
                if b + 2 < B:
                    dve.wait_ge(S["a0_scores"], 2 * (b + 2) + 2)
                    wait(dve, S["a0_y"], b - 1)
                    shift(b + 2, 1, 1, eb_of(b + 2), S["a0_eb_in"], lambda: inverse_sums(b + 1))
                else:
                    inverse_sums(b + 1)
            for a in range(2):
                dve.wait_ge(S["a0_out"], a + 1)
                V.tensor_tensor(half(h, a), half(h, a), ps[:, 2 + a, 0:HALF], ALU.add).then_inc(S["h_ready"], 1)

            def split_high(m, i, u):
                n = i * m.U + u
                w, hi = w_sb[m.layer][:, u, 0:m.F], wr[:, u % 2, 0, 0:m.F]
                dve.wait_ge(w_loaded[u], (i + 1 + m.i0) * 16)
                if not (isinstance(n, int) and n < 2):
                    dve.wait_ge(X["h_ready"], (n - 1) * m.S + m.k0)
                V.tensor_copy(hi, w).then_inc(X["w_split_hi"], 1)

            def split_low(m, i, u):
                n = i * m.U + u
                w, hi, lo = w_sb[m.layer][:, u, 0:m.F], wr[:, u % 2, 0, 0:m.F], wr[:, u % 2, 1, 0:m.F]
                dve.wait_ge(X["w_split_hi"], n + 1 + m.n0)
                V.tensor_tensor(lo, w, hi.bitcast(F32), ALU.subtract).then_inc(X["w_split"], 1)

            def route(m):
                R, E = rt, min(m.E, 8) if m.layer == 0 else m.E
                rows = NT * (9 if m.layer == 0 else 1)
                n = rows * E
                flat = lg[:, 0:n]
                logits = ps[0:TT, 0, 0:n]
                for u in range(2 if m.gated else 1):
                    split_high(m, 0, u)
                    split_low(m, 0, u)
                if m.gated:
                    dve.wait_ge(R["logits_read"], m.layer + 1)
                    logits = aff[:, :]
                else:
                    dve.wait_ge(R["logits"], m.layer + 1)
                if m.layer == 0:
                    last = V.tensor_copy(flat, logits)
                else:
                    if m.layer == 1:
                        dve.wait_ge(S["ld_bias"], 5 * 16)
                    at = {1: 0, 2: 8, 3: 16}[m.layer]
                    last = V.tensor_tensor(flat.rearrange("p (r e) -> p r e", e=E), logits.rearrange("p (r e) -> p r e", e=E),
                                           bc(bias_bc[0:TT, at:at + E].unsqueeze(1), TT, rows, E), ALU.add)
                if m.gated:
                    link(last)
                else:
                    last.then_inc(R["logits_read"], 1)
                    dve.wait_ge(R["logits_read"], m.layer + 1)

                def re(ap):
                    return ap[:, 0:n].rearrange("p (r e) -> p r e", e=E)

                def along(stat):
                    return bc(stat.unsqueeze(2), TT, rows, E)

                top = {0: 2, 1: 1, 2: 2, 3: 3}[m.layer]
                rev = bc(revb[:, 0:E].unsqueeze(1), TT, rows, E)
                softmax = m.layer in (0, 2)
                d, e, p1, p2 = (r_s[:, k, 0:rows] for k in (3, 4, 5, 7))
                for j in range(top):
                    last_one = j + 1 == top
                    mx, rk, oh = r_s[:, j, 0:rows], r_top[:, 0:rows], r_oh[j]
                    link(V.tensor_reduce(mx, re(lg), AX, ALU.max))
                    is_top = mark(V.tensor_tensor(re(r_rank), re(lg), along(mx), ALU.is_equal))
                    if softmax and last_one:
                        V.tensor_tensor(d, mx, r_s[:, 0, 0:rows], ALU.subtract).then_inc(R["d"], 1)
                    dve.wait_ge(S["dve_chain"], is_top)
                    ranked = mark(V.tensor_tensor(re(r_rank), re(r_rank), rev, ALU.mult))
                    if m.gated and last_one:
                        mark(V.tensor_tensor(re(r_oh[0]), re(r_oh[0]), re(r_oh[1]), ALU.add))
                    dve.wait_ge(S["dve_chain"], ranked)
                    first_top = mark(V.tensor_reduce(rk, re(r_rank), AX, ALU.max))
                    if softmax and last_one:
                        dve.wait_ge(R["e"], RT_E[m.layer])
                        e_plus = mark(V.tensor_scalar(p1, e, 1.0, None, ALU.add))
                    dve.wait_ge(S["dve_chain"], first_top)
                    found = mark(V.tensor_tensor(re(oh), re(r_rank), along(rk), ALU.is_equal))
                    if softmax and last_one:
                        dve.wait_ge(S["dve_chain"], e_plus)
                        link(V.reciprocal(p1, p1))
                        weight2 = mark(V.tensor_tensor(p2, e, p1, ALU.mult))
                        mark(V.tensor_tensor(re(r_oh[0]), re(r_oh[0]), along(p1), ALU.mult))
                        dve.wait_ge(S["dve_chain"], weight2)
                    dve.wait_ge(S["dve_chain"], found)
                    if not last_one:
                        link(V.scalar_tensor_tensor(flat, oh[:, 0:n], -1e30, flat, ALU.mult, ALU.add))
                if softmax:
                    link(V.tensor_tensor(re(r_oh[1]), re(r_oh[1]), along(p2), ALU.mult))
                    if m.layer == 2:
                        last = V.tensor_tensor(gates[:, :, 0:E], re(r_oh[0]), re(r_oh[1]), ALU.add)
                    else:
                        link(V.tensor_tensor(re(r_oh[3]), re(r_oh[0]), re(r_oh[1]), ALU.add))
                        g4 = r_oh[3][:, 0:n].rearrange("p (k r e) -> p k r e", k=NT, e=8)
                        last = V.tensor_tensor(gates[:, :, :].rearrange("p k (g e) -> p k g e", g=8), g4[:, :, 1:9, :],
                                               bc(g4[:, :, 0, :].unsqueeze(3), TT, NT, 8, 8), ALU.mult)
                elif m.layer == 1:
                    last = V.tensor_copy(gates[:, :, 0:E], re(r_oh[0]))
                else:
                    link(V.tensor_tensor(re(r_oh[0]), re(r_oh[0]), re(r_oh[2]), ALU.add))
                    link(V.tensor_tensor(re(r_oh[0]), re(r_oh[0]), re(aff), ALU.mult))
                    link(V.tensor_reduce(r_s[:, 3, 0:rows], re(r_oh[0]), AX, ALU.add))
                    link(V.tensor_scalar(r_s[:, 3, 0:rows], r_s[:, 3, 0:rows], 1e-9, None, ALU.add))
                    link(V.reciprocal(r_s[:, 4, 0:rows], r_s[:, 3, 0:rows]))
                    last = V.tensor_tensor(gates[:, :, 0:E], re(r_oh[0]), along(r_s[:, 4, 0:rows]), ALU.mult)
                last.then_inc(R["gates"], 1)

            def experts(m):
                L = m.layer

                LEAD = 2 if m.gated else 1

                def body(i, final):
                    for u in range(m.U):
                        n = i * m.U + u
                        for s in range(m.S):
                            k = n * m.S + s + m.k0
                            a = s % 2
                            cb_a = cb[:, u, a * HALF:(a + 1) * HALF]
                            if s == 0 or s == 1 and isinstance(i, int) and i == 0 and u < SPREAD:
                                dve.wait_ge(*gates_there(m, i, u, a))
                            if m.gated:
                                dve.wait_ge(X["h_ready"], k + 1)
                                wait(dve, X["g_ready"], k - 1)
                                V.tensor_tensor(tb[:, s, :], cb_a, ps[:, 2 * s + 1, 0:HALF], ALU.mult).then_inc(X["t_ready"], 1)
                                dve.wait_ge(X["t_ready"], k - m.k0 + 1)
                            dve.wait_ge(X["a_ready"], k + 1)
                            wait(dve, X["g_used"], k - 3)
                            V.tensor_tensor(gb[:, m.slot(u, s), :], ab[:, m.slot(u, s), :], tb[:, s, :] if m.gated else cb_a,
                                            ALU.mult).then_inc(X["g_ready"], 1)
                            if not (final and u + LEAD >= m.U):
                                later = (i, u + LEAD) if u + LEAD < m.U else (i + 1, u + LEAD - m.U)
                                if s == 0:
                                    split_high(m, *later)
                                if s == 1:
                                    split_low(m, *later)

                body(0, False)
                if m.I > 2:
                    with dve.Fori(1, m.I - 1) as i:
                        body(i, False)
                body(m.I - 1, True)
                for a in range(2):
                    if m.gated:
                        dve.wait_ge(X["g_used"], m.k0 + m.E * m.S - 1 + a)
                    else:
                        dve.wait_ge(moe_done, 2 * L + a + 1)
                    V.tensor_tensor(half(h, a), half(h, a), ps[:, 6 + a, 0:HALF], ALU.add).then_inc(S["h_ready"], 1)

            ln(1)
            route(MOES[0])
            experts(MOES[0])

            ln(2)
            for a in range(2):
                dve.wait_ge(S["a1_tr"], 2 * a + 1)
                V.tensor_copy(ktok[:, a * HB:(a + 1) * HB, :].rearrange("p b n -> p (b n)"), ps[0:T, a, :]).then_inc(S["a1_ktok"], 1)
            for a in range(2):
                dve.wait_ge(S["a1_kv"], a + 1)
                V.tensor_tensor(kv[:, a * HB:(a + 1) * HB, :], ps[:, 4 + a, :].rearrange("p (b n) -> p b n", n=D),
                                bc(const("blk_kv").unsqueeze(1), D, HB, D), ALU.mult).then_inc(S["a1_kvm"], 1)
            for a in range(2):
                dve.wait_ge(S["a1_prelu"], a + 1)
                V.tensor_tensor(half(t[5], a), half(xn, a), half(t[4], a), ALU.add).then_inc(S["a1_x1"], 1)
            for a in range(2):
                dve.wait_ge(S["a1_x1"], a + 1)
                link(V.tensor_tensor(half(h, a), half(h, a), half(t[5], a), ALU.add))
            for a in range(2):
                dve.wait_ge(S["a1_y"], a + 1)
                V.tensor_tensor(half(h, a), half(h, a), half(t[6], a), ALU.add).then_inc(S["h_ready"], 1)

            ln(3)
            route(MOES[1])
            experts(MOES[1])

            ln(4)
            q, k_, v = t[0], t[1], t[2]

            def himg(ap, a):
                return half(ap, a).rearrange("p (b t) -> p b t", b=HB)

            def hsum(i, a):
                return sums[:, i, a * HB:(a + 1) * HB]

            def per_himg(i, a):
                return bc(hsum(i, a).unsqueeze(2), D, HB, T)

            for a in range(2):
                dve.wait_ge(S["a2_in"], 3 * a + 1)
                V.tensor_reduce(hsum(0, a), himg(q, a), AX, ALU.add)
                dve.wait_ge(S["a2_in"], 3 * a + 2)
                link(V.tensor_reduce(hsum(1, a), himg(k_, a), AX, ALU.add))
                V.tensor_tensor(himg(t[3], a), himg(q, a), per_himg(1, a), ALU.mult).then_inc(S["a2_prod"], 1)
                V.tensor_tensor(himg(t[4], a), himg(k_, a), per_himg(0, a), ALU.mult).then_inc(S["a2_prod"], 1)
            for a in range(2):
                dve.wait_ge(S["a2_io"], a + 1)
                V.reciprocal(rin[:, :, a * HB:(a + 1) * HB, :].rearrange("p k b h -> p k (b h)"),
                             ps[0:T, 6 + a, 0:2 * HB * H].rearrange("p (k n) -> p k n", k=2)).then_inc(S["a2_rin"], 1)
                dve.wait_ge(S["a2_rin"], a + 1)
                V.tensor_copy(rin_full[1][:, a * HB:(a + 1) * HB, :].rearrange("p b (h d) -> p (b h) d", h=H),
                              bc(rin[:, 1, a * HB:(a + 1) * HB, :].rearrange("p b h -> p (b h)").unsqueeze(2), T, HB * H, HD)
                              ).then_inc(S["a2_rin_o"], 1)
            for a in range(2):
                dve.wait_ge(S["a2_ri"], a + 1)
                link(V.tensor_tensor(half(t[7], a), half(k_, a), ps[:, 2 + a, 0:HALF], ALU.mult))
                link(V.tensor_reduce(hsum(2, a), himg(t[7], a), AX, ALU.add))
                V.tensor_tensor(himg(t[3], a), himg(q, a), per_himg(2, a), ALU.mult).then_inc(S["a2_prod2"], 1)
            for a in range(2):
                dve.wait_ge(S["a2_rI"], a + 1)
                link(V.tensor_tensor(half(t[8], a), half(q, a), half(t[5], a), ALU.mult))
                link(V.tensor_reduce(hsum(3, a), himg(t[8], a), AX, ALU.add))
                V.tensor_tensor(himg(t[4], a), himg(k_, a), per_himg(3, a), ALU.mult).then_inc(S["a2_prod2"], 1)
            for a in range(2):
                dve.wait_ge(S["a2_hats"], 3 + a)
                o_hat = ps[:, 6 + a, 0:HALF].rearrange("p (b t) -> p b t", b=HB)
                link(V.tensor_reduce(hsum(4, a), o_hat, AX, ALU.max))
                V.tensor_tensor(himg(t[6], a), o_hat, per_himg(4, a), ALU.subtract).then_inc(S["a2_einp"], 1)
            V.tensor_tensor(t[3][:, :], q[:, :], k_[:, :], ALU.mult).then_inc(S["a2_qk"], 1)
            for a in range(2):
                dve.wait_ge(S["a2_sig"], a + 1)
                last = V.tensor_tensor(half(t[9], a), half(t[9], a), half(t[5], a), ALU.mult)
            last.then_inc(S["a2_vw"], 1)
            for a in range(2):
                dve.wait_ge(S["a2_e"], a + 1)
                V.tensor_reduce(hsum(5, a), himg(t[6], a), AX, ALU.add)
                link(V.tensor_tensor(half(v, a), half(v, a), half(t[6], a), ALU.mult))
                link(V.reciprocal(hsum(6, a), hsum(5, a)))
                V.tensor_tensor(himg(v, a), himg(v, a), per_himg(6, a), ALU.mult).then_inc(S["a2_vw"], 1)
            dve.wait_ge(S["a2_vw"], 3)
            V.tensor_copy(vr[:, 0, :], v[:, :]).then_inc(S["a2_vsplit"], 1)
            dve.wait_ge(S["a2_vsplit"], 1)
            V.tensor_tensor(vr[:, 1, :], v[:, :], vr[:, 0, :].bitcast(F32), ALU.subtract).then_inc(S["a2_vsplit"], 1)
            for d in range(H):
                if d + 1 < H:
                    dve.wait_ge(S["a2_ks"], d + 1)
                    wait(dve, S["a2_A"], 2 * d)
                    V.tensor_tensor(two(t[3 + (d + 1) % 2][:, :]), two(q[:, :]), pair(2 * (d % 2)), ALU.mult).then_inc(S["a2_qk"], 1)
                if d > 0:
                    dve.wait_ge(S["a2_vse"], d)
                    wait(dve, S["a2_acc"], d - 2)
                for a in range(2):
                    dve.wait_ge(S["a2_A"], 2 * d + a + 1)
                    V.tensor_tensor(half(t[7 + d % 2] if d else t[5], a), half(vs[:, d % 2, :] if d else v, a),
                                    ps[:, 2 + a, 0:HALF], ALU.mult).then_inc(S["a2_t"], 1)
            dve.wait_ge(S["a2_acc"], H - 1)
            V.tensor_tensor(t[5][:, :], t[5][:, :], t[9][:, :], ALU.mult).then_inc(S["a2_r"], 1)
            for a in range(2):
                dve.wait_ge(S["a2_out"], a + 1)
                V.scalar_tensor_tensor(half(h, a), ps[:, 4 + a, 0:HALF], c_("l2bo"), half(h, a),
                                       ALU.add, ALU.add).then_inc(S["h_ready"], 1)

            ln(5)
            dve.wait_ge(S["ln_out"], 12)
            V.tensor_tensor(h[:, :], h[:, :], xn[:, :], ALU.add).then_inc(S["h_ready"], 2)
            ln(6, hx)
            dve.wait_ge(S["ln_out"], 14)
            V.tensor_scalar(hx[:, :], hx[:, :], c_("l2g"), c_("l2b"), ALU.mult, ALU.add).then_inc(S["ln_post"], 1)
            route(MOES[2])
            experts(MOES[2])

            ln(7)
            for k, name in ((1, "l3bk"), (0, "l3bq")):
                dve.wait_ge(S["a3_qkv"], {1: 1, 0: 2}[k])
                V.tensor_scalar(two(t[3 + k][:, :]), pair(k), c_(name), 0.0, ALU.add, ALU.max).then_inc(S["a3_max"], 1)
            dve.wait_ge(S["a3_max"], 2)
            dve.wait_ge(S["a3_exp"], 1)
            link(V.scalar_tensor_tensor(t[1][:, :], t[1][:, :], 1.0, t[4][:, :], ALU.min, ALU.add))
            V.tensor_tensor(img(t[1][:, :]), img(t[1][:, :]), bc(decay[:, 1, :].unsqueeze(1), D, B, T), ALU.mult).then_inc(S["a3_q"], 1)
            dve.wait_ge(S["a3_exp"], 2)
            link(V.scalar_tensor_tensor(t[0][:, :], t[0][:, :], 1.0, t[3][:, :], ALU.min, ALU.add))
            for a in range(2):
                V.tensor_tensor(half(t[0], a).rearrange("p (b t) -> p b t", b=HB), half(t[0], a).rearrange("p (b t) -> p b t", b=HB),
                                bc(decay[:, 0, :].unsqueeze(1), D, HB, T), ALU.mult).then_inc(S["a3_q"], 1)
            for a in range(2):
                dve.wait_ge(S["a3_q"], a + 2)
                for hh in range(H // 2):
                    last = V.tensor_scalar(half(qm[:, hh, :], a), half(t[0], a), const("headmask")[:, hh:hh + 1], None, ALU.mult)
                last.then_inc(S["a3_qk"], 1)

            dve.wait_ge(S["a3_kcum"], 1)
            V.tensor_tensor(two(t[4][:, :]), two(t[0][:, :]), pair(3), ALU.mult).then_inc(S["a3_qkc"], 1)

            for b in range(B):
                dve.wait_ge(S["a3_scores"], b + 1)
                wait(dve, S["a3_y"], b - 1)
                V.tensor_tensor(ea[:, b % 2].rearrange("p (a h) n -> p (a h) n", a=2).rearrange("p (a h) n -> p a h n", a=2),
                                pair4(1 + b % 2, T), bc(const("causal")[0:T, :].unsqueeze(1).unsqueeze(1), T, 2, HB, T),
                                ALU.mult).then_inc(S["a3_att"], 1)
                if b < 2:
                    dve.wait_ge(S["a3_den"], b + 1)
                    V.tensor_scalar(half(t[5], b), ps[:, 7, 0:HALF], 1e-6, None, ALU.add).then_inc(S["a3_den_out"], 1)
                elif b < 4:
                    dve.wait_ge(S["a3_den_out"], 2)
                    V.reciprocal(half(t[5], b - 2), half(t[5], b - 2)).then_inc(S["a3_inv"], 1)
            for a in range(2):
                dve.wait_ge(S["a3_inv"], 2)
                dve.wait_ge(S["a3_y"], B)
                V.tensor_tensor(half(t[3], a), half(t[5], a), ps[:, 6 + a, 0:HALF], ALU.mult).then_inc(S["a3_yF"], 1)
            ln(8, t[5])
            dve.wait_ge(S["ln_out"], 18)
            link(V.tensor_scalar(t[5][:, :], t[5][:, :], c_("l3g"), c_("l3b"), ALU.mult, ALU.add))
            V.tensor_tensor(h[:, :], h[:, :], t[5][:, :], ALU.add).then_inc(S["h_ready"], 2)
            ln(9)
            route(MOES[3])
            experts(MOES[3])

        @block.gpsimd
        def _(pool):
            nc.gpsimd.memset(vtok[:, :, :, :], 1.0).then_inc(S["pool_ready"], 1)
            for a in range(2):
                pool.wait_ge(S["emb_n"], a + 1)
                pool.wait_ge(S["emb_gate"], a + 1)
                E_ = slice(a * HP, (a + 1) * HP)
                nc.gpsimd.tensor_tensor(t[9][:, E_], t[3][:, E_], t[1][:, E_], ALU.mult).then_inc(S["emb_ng"], 1)
            pool.wait_ge(S["a0_vtok"], 1)
            for b in range(B):
                pool.wait_ge(S["a0_inv"], b + 1)
                wait(pool, S["a0_y"], b - 1)
                nc.gpsimd.tensor_tensor(vtok2[:, b % 2], vtok[:, b, :, 0:HD],
                                        sm[:, b % 2, 3, :].unsqueeze(2).broadcast_to([T, H, HD]), ALU.mult).then_inc(S["a0_v2"], 1)

            def split_x(m):
                pool.wait_ge(S["x_split"], 2 * m.layer + 1)
                nc.gpsimd.tensor_tensor(xr[:, 1, :], (hx if m.layer == 2 else xn)[:, :], xr[:, 0, :].bitcast(F32),
                                        ALU.subtract).then_inc(S["x_split"], 1)

            split_x(MOES[0])
            split_x(MOES[1])
            pool.wait_ge(S["ld_const"], 16)
            pool.wait_ge(moe_done, 4)
            nc.gpsimd.tensor_copy(perm_r, const("perm")).then_inc(S["a2_perm"], 1)
            pool.wait_ge(S["a2_in"], 5)
            nc.gpsimd.tensor_copy(xr[:, 0, :], t[1][:, :]).then_inc(S["a2_ksplit"], 1)
            pool.wait_ge(S["a2_ksplit"], 1)
            nc.gpsimd.tensor_tensor(xr[:, 1, :], t[1][:, :], xr[:, 0, :].bitcast(F32), ALU.subtract).then_inc(S["a2_ksplit"], 1)
            for d in range(1, H):
                pool.wait_ge(S["a2_t"], 2 * (d + 1))
                wait(pool, S["a2_acc"], d - 1)
                nc.gpsimd.tensor_tensor(t[5][:, :], t[5][:, :], t[7 + d % 2][:, :], ALU.add).then_inc(S["a2_acc"], 1)
            split_x(MOES[2])
            pool.wait_ge(S["a2_t"], 2 * H)
            pool.wait_ge(moe_done, 6)
            for values in vmask:
                last = nc.gpsimd.memset(values, 0.0)
            last.then_inc(S["a3_zero"], 1)
            split_x(MOES[3])
            for a in range(2):
                pool.wait_ge(rt["shared_a"], a + 1)
                nc.gpsimd.tensor_tensor(gb[:, 2 + a, :], gb[:, 2 + a, :], ab[:, 2 + a, :], ALU.mult).then_inc(rt["shared_g"], 1)


def constants():
    blk = np.kron(np.eye(H), np.ones((HD, HD)))
    c = np.zeros((D, CONST_W), np.float32)

    def put(name, a):
        at, w = CONST_AT[name]
        c[:a.shape[0], at:at + a.shape[1]] = a

    put("ident", np.eye(D))
    put("mean", np.full((D, D), 1.0 / D))
    put("centre", np.eye(D) - 1.0 / D)
    put("blk_mean", blk / HD)
    put("blk_one", blk)
    put("blk_kv", blk * 0.125)
    put("headmask", np.kron(np.eye(H), np.ones((HD, 1))))
    put("rev", np.tile(16.0 - np.arange(16), (D, 1)))
    put("index", np.tile(np.arange(T, dtype=np.float64), (D, 1)))
    put("causal", np.triu(np.ones((T, T))))
    div = np.exp(np.arange(0, D, 2, dtype=np.float32) * np.float32(-np.log(10000.0) / D)).astype(np.float32)
    ang = np.arange(NPATCH, dtype=np.float32)[:, None] * div
    put("pos", np.stack([np.sin(ang), np.cos(ang)], -1).reshape(NPATCH, D).T)
    put("perm", np.concatenate([np.kron(np.roll(np.eye(H), d, axis=0), np.eye(HD)) for d in range(1, H)], axis=1))
    put("eps", np.tile([1e-5, 1.1920929e-07], (D, 1)))
    return c


def kernel(**inputs):
    import concourse.bacc as _bacc
    from concourse.bass_utils import run_bass_kernel_spmd as _run

    x = {k: np.asarray(v) for k, v in inputs.items()}
    patches = x["x"].reshape(B, SIDE, PATCH, SIDE, PATCH).transpose(2, 4, 0, 1, 3).reshape(2, D, B * NPATCH).transpose(1, 0, 2)
    consts = constants()

    def heads(a):
        return a.reshape((H, 3, HD) + a.shape[1:]).swapaxes(0, 1).reshape((3, D) + a.shape[1:])

    def tile_heads(a):
        return np.tile(a, H)

    bq2, wq2 = heads(x["L2_attn_b_qkv"]), heads(x["L2_attn_W_qkv"])
    col = {"cls": x["cls_tok"].reshape(D), "b3": x["L0_tok_W3_b"]}
    for l in (1, 2):
        e = x[f"L0_tok_eps_in{l}"]
        col[f"ei{l}a"], col[f"ei{l}b"] = e[:D], e[D:]
        col[f"eo{l}"], col[f"b{l}"], col[f"sb{l}"] = x[f"L0_tok_eps_out{l}"], x[f"L0_tok_W{l}_b"], x[f"L0_tok_W{l}_sb"]
    for g in (1, 2, 3):
        col[f"g{g}"] = tile_heads(x[f"L0_attn_g{g}"])
    for p, key in zip("bgemv", ("b", "g", "be", "m", "v")):
        for s in BN_STAGES:
            col[f"bn_{p}_{s}"] = x[f"L1_attn_{s}_{key}"]
        for c in range(NFF1):
            col[f"bn_{p}_f1_{c}"] = x[f"L1_attn_f1_{key}"][c * D:(c + 1) * D]
    b3 = x["L3_attn_b_qkv"]
    for j, n in enumerate("qkv"):
        col[f"l2b{n}"], col[f"l3b{n}"] = bq2[j], b3[j * D:(j + 1) * D]
    col.update(l2bo=x["L2_attn_b_out"], l2g=x["L2_ffn_ln_g"], l2b=x["L2_ffn_ln_b"], l3bo=x["L3_attn_b_out"],
               l3dl=np.repeat(x["L3_attn_decay_logits"], HD), l3g=x["L3_attn_ln_g"], l3b=x["L3_attn_ln_b"])
    mat = {"w3": x["L0_tok_W3_w"].T, "a0qT": x["L0_attn_qkv_w"].T, "a0dT": x["L0_attn_delta_w"].T,
           "a0q": x["L0_attn_qkv_w"], "a0d": x["L0_attn_delta_w"], "a2o": x["L2_attn_W_out"].T, "a3o": x["L3_attn_W_out"]}
    for l in (1, 2):
        for n, key in (("w", "w"), ("s", "sw")):
            a = x[f"L0_tok_W{l}_{key}"].T
            mat[f"{n}{l}a"], mat[f"{n}{l}b"] = a[:D], a[D:]
    for s in "qkvp":
        mat[f"a1{s}"] = x[f"L1_attn_{s}_w"].T
    for c in range(NFF1):
        mat[f"a1f1_{c}"] = x["L1_attn_f1_w"][c * D:(c + 1) * D].T
        mat[f"a1f2_{c}"] = x["L1_attn_f2_w"][:, c * D:(c + 1) * D].T
    for j, n in enumerate("qkv"):
        mat[f"a2{n}"], mat[f"a3{n}"] = wq2[j].T, x["L3_attn_W_qkv"][:, j * D:(j + 1) * D]
    g2 = x["L0_ffn_g2"].transpose(1, 0, 2).reshape(D, 64)
    route = np.concatenate([x["L0_ffn_g1"], g2, x["L1_ffn_Wg"], x["L2_ffn_w_r"].T, x["L3_ffn_gate_w"].T], axis=1)

    def pack(l, e, f):
        w1, w2, b1 = (x[f"L{l}_ffn_{n}"] for n in ("W1", "W2", "b1"))
        return np.concatenate([w1.reshape(e, D, f), w2.reshape(e, f // D, D, D).transpose(0, 2, 1, 3).reshape(e, D, f),
                               b1.reshape(e, f // D, D).transpose(0, 2, 1)], axis=2)

    gu = np.concatenate([x["L3_ffn_shared_gate_up"][None], x["L3_ffn_expert_gate_up"]], axis=0).transpose(0, 2, 1)
    dn = np.concatenate([x["L3_ffn_shared_down"][None], x["L3_ffn_expert_down"]], axis=0).transpose(0, 2, 1)
    w = [pack(0, 64, 256), pack(1, 8, 256), pack(2, 8, 512), np.concatenate([gu, dn], axis=2)]
    b2 = [x[f"L{l}_ffn_b2"].reshape(-1, D) for l in range(3)]
    data = {
        "patches": patches, "consts": consts,
        "cols": np.stack([col[n] for n in COLS], axis=1), "mats": np.stack([mat[n] for n in MATS], axis=1),
        "route": route, "rows_eo": np.stack([x["L0_tok_eps_out1"], x["L0_tok_eps_out2"]]),
        "bias_rows": np.concatenate([x["L1_ffn_bg"], x["L2_ffn_b_r"], x["L3_ffn_expert_bias"]]),
        **{f"w{l}": w[l] for l in range(4)}, **{f"b2_{l}": b2[l] for l in range(3)},
    }
    nc = _bacc.Bacc("TRN2", target_bir_lowering=False, num_devices=1)
    arrays, ap = {}, {}
    for name, a in data.items():
        a = np.ascontiguousarray(a)
        arrays[f"in_{name}"] = a
        ap[name] = nc.dram_tensor(f"in_{name}", a.shape, mybir.dt.from_np(a.dtype), kind="ExternalInput").ap()
    gate_rows = nc.dram_tensor("gate_rows", (sum(m.E for m in MOES), N), F32, kind="Internal").ap()
    out = nc.dram_tensor("out", (D, N), F32, kind="ExternalOutput").ap()
    tower(nc, ap["patches"], ap["consts"], ap["cols"], ap["mats"], ap["route"], ap["rows_eo"], ap["bias_rows"],
          [ap[f"w{l}"] for l in range(4)], [ap[f"b2_{l}"] for l in range(3)], gate_rows, out)
    r = _run(nc, [arrays], core_ids=[0])
    return np.ascontiguousarray(r.results[0]["out"].T.reshape(B, T, D))
```
